# Optimizing a Trainium2 kernel written in Bass

```python
import numpy as np
import jax
import jax.numpy as jnp

def _softmax(x, axis=-1):
    return jax.nn.softmax(x, axis=axis)

def _gelu(x):
    return jax.nn.gelu(x, approximate=True)

def _silu(x):
    return jax.nn.silu(x)

def _sigmoid(x):
    return jax.nn.sigmoid(x)

def _layernorm(x, axis=-1, eps=1e-05):
    m = jnp.mean(x, axis=axis, keepdims=True)
    v = jnp.var(x, axis=axis, keepdims=True)
    return (x - m) / jnp.sqrt(v + eps)

def _scatter_add(tgt, idx, src, axis=0):
    return tgt.at[idx].add(src)

def _segment_sum(src, seg, n):
    return jax.ops.segment_sum(src, seg, n)
kernel_name = 'mk_seq_preln_d1_jaxref_r8_3e8ce2'

def setup_inputs(seed: int=0):
    np.random.seed(seed)
    _w = jnp.asarray

    def _L0_attn_setup():
        import jax, jax.numpy as jnp
        import numpy as np
        D_MODEL = 128
        D_STATE = 64
        D_CONV = 4
        EXPAND = 2
        HEADDIM = 64
        NGROUPS = 1
        D_INNER = EXPAND * D_MODEL
        NHEADS = D_INNER // HEADDIM
        CONV_DIM = D_INNER + 2 * NGROUPS * D_STATE
        D_IN_PROJ = 2 * D_INNER + 2 * NGROUPS * D_STATE + NHEADS
        BATCH, SEQLEN = (2, 512)
        CHUNK = 64
        LN_EPS = 1e-05
        RMS_EPS = 1e-05

        def _segsum(a):
            q = a.shape[-1]
            cs = jnp.cumsum(a, axis=-1)
            seg = cs[..., :, None] - cs[..., None, :]
            mask = jnp.tril(jnp.ones((q, q), dtype=bool))
            return jnp.where(mask, seg, -jnp.inf)

        def _ssd(xdt, Adt, Bm, Cm):
            b, l, h, p = xdt.shape
            c = l // CHUNK
            X = xdt.reshape(b, c, CHUNK, h, p)
            A = Adt.reshape(b, c, CHUNK, h).transpose(0, 3, 1, 2)
            Bq = Bm.reshape(b, c, CHUNK, -1)
            Cq = Cm.reshape(b, c, CHUNK, -1)
            A_cum = jnp.cumsum(A, -1)
            Lmat = jnp.exp(_segsum(A))
            Y_diag = jnp.einsum('bcln,bcsn,bhcls,bcshp->bclhp', Cq, Bq, Lmat, X)
            decay_states = jnp.exp(A_cum[..., -1:] - A_cum)
            states = jnp.einsum('bcln,bhcl,bclhp->bchpn', Bq, decay_states, X)
            chunk_decay = jnp.exp(A_cum[..., -1])

            def step(hprev, inp):
                s, dec = inp
                return (dec[..., None, None] * hprev + s, hprev)
            h0 = jnp.zeros((b, h, p, states.shape[-1]), xdt.dtype)
            _, prev = jax.lax.scan(step, h0, (jnp.moveaxis(states, 1, 0), jnp.moveaxis(chunk_decay, 2, 0)))
            prev = jnp.moveaxis(prev, 0, 1)
            Y_off = jnp.einsum('bcln,bchpn,bhcl->bclhp', Cq, prev, jnp.exp(A_cum))
            return (Y_diag + Y_off).reshape(b, l, h, p)
        key = jax.random.key(seed)
        ks = jax.random.split(key, 8)
        dt = jnp.exp(jax.random.uniform(ks[3], (NHEADS,)) * (np.log(0.1) - np.log(0.001)) + np.log(0.001))
        dt_bias = dt + jnp.log(-jnp.expm1(-dt))
        return {'x': jax.random.normal(ks[0], (BATCH, SEQLEN, D_MODEL), jnp.float32), 'ln_w': jnp.ones((D_MODEL,), jnp.float32), 'ln_b': jnp.zeros((D_MODEL,), jnp.float32), 'in_proj_w': 0.02 * jax.random.normal(ks[1], (D_IN_PROJ, D_MODEL), jnp.float32), 'conv_w': 0.2 * jax.random.normal(ks[2], (CONV_DIM, 1, D_CONV), jnp.float32), 'conv_b': jnp.zeros((CONV_DIM,), jnp.float32), 'dt_bias': dt_bias, 'A_log': jnp.log(1.0 + 15.0 * jax.random.uniform(ks[4], (NHEADS,), jnp.float32)), 'D_skip': jnp.ones((NHEADS,), jnp.float32), 'norm_w': jnp.ones((D_INNER,), jnp.float32), 'out_proj_w': 0.02 * jax.random.normal(ks[5], (D_MODEL, D_INNER), jnp.float32)}
    _L0_attn_in = _L0_attn_setup()

    def _L0_ffn_setup():
        import jax, jax.numpy as jnp
        import numpy as np
        E = 8
        C = 160
        D = 128
        H = 512
        B, S = (4, 256)
        key = jax.random.key(seed)
        ks = jax.random.split(key, 12)
        sc = 0.02
        return {'input': jax.random.normal(ks[0], (B, S, D), jnp.float32), 'router_w': jax.random.normal(ks[1], (D, E), jnp.float32) * sc, 'router_b': jnp.zeros((E,), jnp.float32), 'w1': jax.random.normal(ks[2], (E, D, H), jnp.float32) * sc, 'b1': jnp.zeros((E, H), jnp.float32), 'w2': jax.random.normal(ks[3], (E, H, D), jnp.float32) * sc, 'b2': jnp.zeros((E, D), jnp.float32), 'ow1': jax.random.normal(ks[4], (D, H), jnp.float32) * sc, 'ob1': jnp.zeros((H,), jnp.float32), 'ow2': jax.random.normal(ks[5], (H, D), jnp.float32) * sc, 'ob2': jnp.zeros((D,), jnp.float32)}
    _L0_ffn_in = _L0_ffn_setup()
    _d = {'L0_attn_x': _L0_attn_in['x'], 'L0_attn_ln_w': _L0_attn_in['ln_w'], 'L0_attn_ln_b': _L0_attn_in['ln_b'], 'L0_attn_in_proj_w': _L0_attn_in['in_proj_w'], 'L0_attn_conv_w': _L0_attn_in['conv_w'], 'L0_attn_conv_b': _L0_attn_in['conv_b'], 'L0_attn_dt_bias': _L0_attn_in['dt_bias'], 'L0_attn_A_log': _L0_attn_in['A_log'], 'L0_attn_D_skip': _L0_attn_in['D_skip'], 'L0_attn_norm_w': _L0_attn_in['norm_w'], 'L0_attn_out_proj_w': _L0_attn_in['out_proj_w'], 'L0_ffn_router_w': _L0_ffn_in['router_w'], 'L0_ffn_router_b': _L0_ffn_in['router_b'], 'L0_ffn_w1': _L0_ffn_in['w1'], 'L0_ffn_b1': _L0_ffn_in['b1'], 'L0_ffn_w2': _L0_ffn_in['w2'], 'L0_ffn_b2': _L0_ffn_in['b2'], 'L0_ffn_ow1': _L0_ffn_in['ow1'], 'L0_ffn_ob1': _L0_ffn_in['ob1'], 'L0_ffn_ow2': _L0_ffn_in['ow2'], 'L0_ffn_ob2': _L0_ffn_in['ob2']}
    _x0 = _d['L0_attn_x']
    _d['L0_attn_x'] = jax.random.normal(jax.random.fold_in(jax.random.key(seed), 1), (1, 2048, 128), dtype=_x0.dtype)
    del _x0
    return _d

def reference(L0_attn_x, L0_attn_ln_w, L0_attn_ln_b, L0_attn_in_proj_w, L0_attn_conv_w, L0_attn_conv_b, L0_attn_dt_bias, L0_attn_A_log, L0_attn_D_skip, L0_attn_norm_w, L0_attn_out_proj_w, L0_ffn_router_w, L0_ffn_router_b, L0_ffn_w1, L0_ffn_b1, L0_ffn_w2, L0_ffn_b2, L0_ffn_ow1, L0_ffn_ob1, L0_ffn_ow2, L0_ffn_ob2):

    def _L0_attn_ref(x, ln_w, ln_b, in_proj_w, conv_w, conv_b, dt_bias, A_log, D_skip, norm_w, out_proj_w):
        import jax, jax.numpy as jnp
        import numpy as np
        D_MODEL = 128
        D_STATE = 64
        D_CONV = 4
        EXPAND = 2
        HEADDIM = 64
        NGROUPS = 1
        D_INNER = EXPAND * D_MODEL
        NHEADS = D_INNER // HEADDIM
        CONV_DIM = D_INNER + 2 * NGROUPS * D_STATE
        D_IN_PROJ = 2 * D_INNER + 2 * NGROUPS * D_STATE + NHEADS
        BATCH, SEQLEN = (2, 512)
        CHUNK = 64
        LN_EPS = 1e-05
        RMS_EPS = 1e-05

        def _segsum(a):
            q = a.shape[-1]
            cs = jnp.cumsum(a, axis=-1)
            seg = cs[..., :, None] - cs[..., None, :]
            mask = jnp.tril(jnp.ones((q, q), dtype=bool))
            return jnp.where(mask, seg, -jnp.inf)

        def _ssd(xdt, Adt, Bm, Cm):
            b, l, h, p = xdt.shape
            c = l // CHUNK
            X = xdt.reshape(b, c, CHUNK, h, p)
            A = Adt.reshape(b, c, CHUNK, h).transpose(0, 3, 1, 2)
            Bq = Bm.reshape(b, c, CHUNK, -1)
            Cq = Cm.reshape(b, c, CHUNK, -1)
            A_cum = jnp.cumsum(A, -1)
            Lmat = jnp.exp(_segsum(A))
            Y_diag = jnp.einsum('bcln,bcsn,bhcls,bcshp->bclhp', Cq, Bq, Lmat, X)
            decay_states = jnp.exp(A_cum[..., -1:] - A_cum)
            states = jnp.einsum('bcln,bhcl,bclhp->bchpn', Bq, decay_states, X)
            chunk_decay = jnp.exp(A_cum[..., -1])

            def step(hprev, inp):
                s, dec = inp
                return (dec[..., None, None] * hprev + s, hprev)
            h0 = jnp.zeros((b, h, p, states.shape[-1]), xdt.dtype)
            _, prev = jax.lax.scan(step, h0, (jnp.moveaxis(states, 1, 0), jnp.moveaxis(chunk_decay, 2, 0)))
            prev = jnp.moveaxis(prev, 0, 1)
            Y_off = jnp.einsum('bcln,bchpn,bhcl->bclhp', Cq, prev, jnp.exp(A_cum))
            return (Y_diag + Y_off).reshape(b, l, h, p)
        b, l, _ = x.shape
        mu = jnp.mean(x, -1, keepdims=True)
        var = jnp.mean(jnp.square(x - mu), -1, keepdims=True)
        xn = (x - mu) * jax.lax.rsqrt(var + LN_EPS) * ln_w + ln_b
        zxbcdt = xn @ in_proj_w.T
        z = zxbcdt[..., :D_INNER]
        xBC = zxbcdt[..., D_INNER:D_INNER + CONV_DIM]
        dt = zxbcdt[..., D_INNER + CONV_DIM:]
        xBC_t = jnp.transpose(xBC, (0, 2, 1))
        xBC_c = jax.lax.conv_general_dilated(xBC_t, conv_w, (1,), [(D_CONV - 1, 0)], dimension_numbers=('NCH', 'OIH', 'NCH'), feature_group_count=CONV_DIM)
        xBC = jax.nn.silu(jnp.transpose(xBC_c, (0, 2, 1)) + conv_b)
        xs = xBC[..., :D_INNER].reshape(b, l, NHEADS, HEADDIM)
        Bm = xBC[..., D_INNER:D_INNER + D_STATE]
        Cm = xBC[..., D_INNER + D_STATE:]
        dt = jax.nn.softplus(dt + dt_bias)
        A = -jnp.exp(A_log)
        y = _ssd(xs * dt[..., None], dt * A, Bm, Cm)
        y = y + D_skip[None, None, :, None] * xs
        y = y.reshape(b, l, D_INNER)
        yg = y * jax.nn.silu(z)
        yg = yg * jax.lax.rsqrt(jnp.mean(jnp.square(yg), -1, keepdims=True) + RMS_EPS) * norm_w
        return x + yg @ out_proj_w.T

    def _L0_ffn_ref(input, router_w, router_b, w1, b1, w2, b2, ow1, ob1, ow2, ob2):
        import jax, jax.numpy as jnp
        import numpy as np
        E = 8
        C = 160
        D = 128
        H = 512
        B, S = (4, 256)
        Bq, Sq, Dq = input.shape
        N = Bq * Sq
        xf = input.reshape(N, Dq)
        probs = jax.nn.softmax(xf @ router_w + router_b, axis=-1)
        eid = jnp.argmax(probs, axis=-1)
        onehot = jax.nn.one_hot(eid, E, dtype=xf.dtype)
        rank = (jnp.cumsum(onehot, axis=0)[jnp.arange(N), eid] - 1.0).astype(jnp.int32)
        valid = rank < C
        pos = jnp.where(valid, rank, 0)
        vmask = valid.astype(xf.dtype)[:, None]
        buf = jnp.zeros((E, C, Dq), xf.dtype).at[eid, pos].add(xf * vmask)
        h = jax.nn.relu(jnp.einsum('ecd,edh->ech', buf, w1) + b1[:, None, :])
        y = jnp.einsum('ech,ehd->ecd', h, w2) + b2[:, None, :]
        y_tok = y[eid, pos] * vmask
        yov = jax.nn.relu(xf @ ow1 + ob1) @ ow2 + ob2
        out = y_tok + yov * (1.0 - vmask)
        return out.reshape(Bq, Sq, Dq)
    x = L0_attn_x
    x = x + _L0_attn_ref(_layernorm(x, axis=-1), L0_attn_ln_w, L0_attn_ln_b, L0_attn_in_proj_w, L0_attn_conv_w, L0_attn_conv_b, L0_attn_dt_bias, L0_attn_A_log, L0_attn_D_skip, L0_attn_norm_w, L0_attn_out_proj_w)
    x = x + _L0_ffn_ref(_layernorm(x, axis=-1), L0_ffn_router_w, L0_ffn_router_b, L0_ffn_w1, L0_ffn_b1, L0_ffn_w2, L0_ffn_b2, L0_ffn_ow1, L0_ffn_ob1, L0_ffn_ow2, L0_ffn_ob2)
    return x

_drawn_inputs = setup_inputs


def setup_inputs(seed=0):
    import zlib

    import numpy as np

    out = dict(_drawn_inputs(seed))
    spreads = {'L0_attn_ln_w': (1.0, 0.2),
     'L0_attn_ln_b': (0.0, 0.355),
     'L0_attn_conv_b': (0.0, 0.1),
     'L0_attn_D_skip': (1.0, 0.6),
     'L0_attn_norm_w': (1.0, 0.2),
     'L0_ffn_router_b': (0.0, 0.1),
     'L0_ffn_b1': (0.0, 0.676),
     'L0_ffn_b2': (0.0, 0.1),
     'L0_ffn_ob1': (0.0, 0.8),
     'L0_ffn_ob2': (0.0, 0.1)}
    factors = {'L0_attn_dt_bias': 8.0, 'L0_attn_A_log': 8.0, 'L0_ffn_ow1': 2.99}
    for name, (base, spread) in spreads.items():
        noise = np.random.default_rng([zlib.crc32(name.encode()), seed]).standard_normal(out[name].shape)
        drawn = base * np.exp(spread * noise) if base else spread * noise
        out[name] = jnp.asarray(drawn.astype(out[name].dtype))
    for name, factor in factors.items():
        out[name] = (out[name] * factor).astype(out[name].dtype)
    return out
```

```python
from contextlib import ExitStack

import concourse.bass as bass
from concourse import mybir

P = 128
T = 2048
D = 128
NT = T // P
DI = 256
H = 4
HD = DI // H
N = 64
NXBC = DI + 2 * N
NB = NXBC // P
TAPS = 4
GT = 4
G = NT // GT
GW = GT * P
E = 8
CAP = 160
F = 512
FB = F // P
PAIRS = NT // 2
EI = 4
SLOTS = E * CAP
SI = EI * CAP
STI = SI // P
ROW = D + 1
EPS = 1e-5
FAR = 1 << 20

C_LNW, C_LNB, C_CONVW, C_CONVB = 0, 1, 2, 2 + NB * TAPS
C_NORMW = C_CONVB + NB
C_OB1 = C_NORMW + 2
C_B1 = C_OB1 + FB
C_B2 = C_B1 + E * FB
C_DTB = C_B2 + E
C_ALOG = C_DTB + H
C_DSKIP = C_ALOG + H
C_RB = C_DSKIP + H
C_OB2 = C_RB + E
SHEET = C_OB2 + D

F32 = mybir.dt.float32
BF16 = mybir.dt.bfloat16
I32 = mybir.dt.int32
ALU = mybir.AluOpType
ACT = mybir.ActivationFunctionType
AX = mybir.AxisListType


def build(nc, x, sheet, in_w, out_w, router_w, ow1, ow2, w1, w2, out):
    with ExitStack() as ctx:
        def sb(name, shape, dt=F32):
            return ctx.enter_context(nc.sbuf_tensor(name, shape, dt))

        def sem(name):
            return ctx.enter_context(nc.semaphore(name))

        bc_dram = nc.dram_tensor("bc_dram", [P, T], F32, kind="Internal").ap()
        slots_dram = nc.dram_tensor("slots_dram", [SLOTS, ROW], F32, kind="Internal").ap()

        par = sb("par", [P, SHEET])
        win = sb("win", [P, 2 * DI + 2 * N + H])
        wout = sb("wout", [P, 2, D])
        wrt = sb("wrt", [P, E])
        wo1 = sb("wo1", [P, F])
        wo2 = sb("wo2", [P, FB, D])
        w1s = sb("w1s", [P, EI, F])
        w2s = sb("w2s", [P, EI, FB, D])

        ident = sb("ident", [P, P])
        upto = sb("upto", [P, P])
        after = sb("after", [P, P])
        ones = sb("ones", [P, P])
        upto_h = sb("upto_h", [P, P], BF16)
        ones_h = sb("ones_h", [P, P], BF16)
        mhalf = sb("mhalf", [P, 8])
        eps = sb("eps", [P, 8])
        eps_sum = sb("eps_sum", [P, 1])
        none = sb("none", [P, STI], I32)
        passed = sb("passed", [P, 1 + 2 * (E // EI)])
        pair_step = sb("pair_step", [P, 2], I32)
        slot_base = sb("slot_base", [P, 2 * E])
        prefer = sb("prefer", [P, 2 * E])
        dskip = sb("dskip", [P, DI])

        x_all = sb("x_all", [P, NT, D])
        raw = sb("raw", [P, NB, TAPS - 1 + T])
        sz_all = sb("sz_all", [P, NT, DI])
        xs_all = sb("xs_all", [P, NT, DI + N])
        dt_all = sb("dt_all", [P, NT * H])
        a_all = sb("a_all", [P, NT * H])
        ex_all = sb("ex_all", [P, 3, NT * H])
        w_all = sb("w_all", [P, NT * H])

        st1 = sb("st1", [P, GT, 6])
        mv1 = sb("mv1", [P, GT, 2])
        sm1 = sb("sm1", [P, 9, GT])
        xn = sb("xn", [P, GT, D])
        xnT = sb("xnT", [P, GW])
        acc = sb("acc", [P, NB, GW])
        cv = sb("cv", [P, NB, GW])
        sp = sb("sp", [P, 20, NT * H])
        nA = sb("nA", [P, 2, H])

        bcT = sb("bcT", [N, 2, 2, P])
        btok = sb("btok", [P, 2, N])
        at = sb("at", [P, 2, H * P])
        xdt = sb("xdt", [P, 2, DI])
        xw = sb("xw", [P, 2, DI])
        dxs = sb("dxs", [P, 2, DI])
        decay = sb("decay", [P, 2, H * P])
        cb = sb("cb", [P, P])
        m_t = sb("m_t", [P, 2, H * P])
        state = sb("state", [N, DI])
        sdec = sb("sdec", [N, DI])
        y_off = sb("y_off", [P, DI])
        y_sum = sb("y_sum", [P, DI])
        y_skip = sb("y_skip", [P, DI])
        yg = sb("yg", [P, 2, DI])
        junk = sb("junk", [P, DI])
        ssq = sb("ssq", [P, 2])
        msq = sb("msq", [P, 2])
        rms = sb("rms", [P, 2])
        ygT = sb("ygT", [P, 2, DI])

        st2 = sb("st2", [P, 2, 6])
        mv2 = sb("mv2", [P, 2, 2])
        ve2 = sb("ve2", [P, 2])
        rs2 = sb("rs2", [P, 2])
        rowC = sb("rowC", [P, 2, ROW])
        xfT = sb("xfT", [P, 2 * P])
        lg = sb("lg", [P, 2 * E])
        lmax = sb("lmax", [P, 2])
        iseq = sb("iseq", [P, 2 * E])
        pref = sb("pref", [P, 2 * E])
        pmax = sb("pmax", [P, 2])
        oh = sb("oh", [P, 2 * E], BF16)
        count = sb("count", [P, E])
        rk = sb("rk", [P, 2 * E])
        over = sb("over", [P, 2 * E])
        place = sb("place", [P, 2 * E])
        place2 = sb("place2", [P, 2 * E])
        chosen = sb("chosen", [P, 2 * E])
        slotf = sb("slotf", [P, 2])
        sloti = sb("sloti", [P, 2], I32)
        noslot = sb("noslot", [P, 2])
        hT = sb("hT", [P, FB, 2 * P])
        ovb = sb("ovb", [P, 2, D])
        outrow = sb("outrow", [P, 2, D])

        fill = sb("fill", [P, SLOTS // P, ROW])
        rows = sb("rows", [P, STI, ROW])
        tok5 = sb("tok5", [P, STI], I32)
        bufT = sb("bufT", [P, SI])
        hE = sb("hE", [P, 2, FB, CAP])
        yT = sb("yT", [P, SI])
        yrow = sb("yrow", [P, STI, D])

        bank = [ctx.enter_context(nc.psum_tensor(f"bank{i}", [P, 512], F32)) for i in range(8)]

        par_in, win_in, wout_in, ffn_in = sem("par_in"), sem("win_in"), sem("wout_in"), sem("ffn_in")
        x_in = [sem(f"x_in{g}") for g in range(G)]
        w_in = [sem(f"w_in{e}") for e in range(EI)]
        const0, consts, filled = sem("const0"), sem("consts"), sem("filled")
        zeroed, consts_v = sem("zeroed"), sem("consts_v")
        st1_ready, mv1_ready, sm1_step, xn_ready, xx_ready = (
            sem("st1_ready"), sem("mv1_ready"), sem("sm1_step"), sem("xn_ready"), sem("xx_ready"))
        xn_turned, xnT_ready, xbc_done, raw_ready = sem("xn_turned"), sem("xnT_ready"), sem("xbc_done"), sem("raw_ready")
        dt_done, dt_read, z_done, z_read = sem("dt_done"), sem("dt_read"), sem("z_done"), sem("z_read")
        tap_done, cv_ready, bc_stored, cv_turned, xs_ready = (
            sem("tap_done"), sem("cv_ready"), sem("bc_stored"), sem("cv_turned"), sem("xs_ready"))
        sp_step, sp_exp, A_exp, a_ready, sums_done, sums_exp, w_ready = (
            sem("sp_step"), sem("sp_exp"), sem("A_exp"), sem("a_ready"), sem("sums_done"), sem("sums_exp"), sem("w_ready"))
        bc_in = [sem("bc_in0"), sem("bc_in1")]
        at_ready, xdt_ready, xw_ready, dxs_ready, sdec_ready = (
            sem("at_ready"), sem("xdt_ready"), sem("xw_ready"), sem("dxs_ready"), sem("sdec_ready"))
        cbst_done, seg_done, off_done, decay_ready, cb_ready, state_ready, m_ready = (
            sem("cbst_done"), sem("seg_done"), sem("off_done"), sem("decay_ready"), sem("cb_ready"),
            sem("state_ready"), sem("m_ready"))
        diag_done, y_step, yg_ready, ssq_ready, msq_ready, rms_ready = (
            sem("diag_done"), sem("y_step"), sem("yg_ready"), sem("ssq_ready"), sem("msq_ready"), sem("rms_ready"))
        yg_turned, ygT_ready, proj_done, x1_ready = sem("yg_turned"), sem("ygT_ready"), sem("proj_done"), sem("x1_ready")
        st2_ready, mv2_ready, ve2_ready, rs2_ready, xf_ready, xf_turned, xfT_ready = (
            sem("st2_ready"), sem("mv2_ready"), sem("ve2_ready"), sem("rs2_ready"), sem("xf_ready"),
            sem("xf_turned"), sem("xfT_ready"))
        logits_done, route_step, oh_ready, rank_done, rank_step, slot_ready = (
            sem("logits_done"), sem("route_step"), sem("oh_ready"), sem("rank_done"), sem("rank_step"), sem("slot_ready"))
        hid_done, hid_ready, ov_done, ov_read, outrow_ready = (
            sem("hid_done"), sem("hid_ready"), sem("ov_done"), sem("ov_read"), sem("outrow_ready"))
        pm_ready, noslot_ready, passes = sem("pm_ready"), sem("noslot_ready"), sem("passes")
        tok_ready, scattered, stored = sem("tok_ready"), sem("scattered"), sem("stored")
        rows_in, rows_turned, bufT_ready, tok5_ready = sem("rows_in"), sem("rows_turned"), sem("bufT_ready"), sem("tok5_ready")
        eh_done, eh_act, eh_dve, ey_done, ey_ready, ey_turned, yrow_ready, added = (
            sem("eh_done"), sem("eh_act"), sem("eh_dve"), sem("ey_done"), sem("ey_ready"), sem("ey_turned"),
            sem("yrow_ready"), sem("added"))

        def col(i, n=1):
            return par[:, i:i + n]

        def heads(ap, n):
            return ap.unsqueeze(2).to_broadcast([ap.shape[0], H, n])

        def by_head(ap, n):
            return ap.rearrange("p (h n) -> p h n", h=H)

        def begun(count):
            return not isinstance(count, int) or count > 0

        block = ctx.enter_context(nc.Block())

        @block.sync
        def _(sp_q):
            x_t = x.rearrange("(t p) d -> p t d", p=P)
            out_t = out.rearrange("(t p) d -> p t d", p=P)
            rows_t = slots_dram.rearrange("(t p) r -> p t r", p=P)
            sp_q.dma_start(x_all[:, 0:GT, :], x_t[:, 0:GT, :]).then_inc(x_in[0], 16)
            sp_q.dma_start(par[:, :], sheet).then_inc(par_in, 16)
            sp_q.dma_start(win[:, :], in_w).then_inc(win_in, 16)
            for g in range(1, G):
                sp_q.dma_start(x_all[:, g * GT:(g + 1) * GT, :], x_t[:, g * GT:(g + 1) * GT, :]).then_inc(x_in[g], 16)
            sp_q.dma_start(wout[:, :, :], out_w).then_inc(wout_in, 16)
            sp_q.dma_start(wrt[:, :], router_w).then_inc(ffn_in, 16)
            sp_q.dma_start(wo1[:, :], ow1).then_inc(ffn_in, 16)
            sp_q.dma_start(wo2[:, :, :], ow2).then_inc(ffn_in, 16)
            for e in range(EI):
                sp_q.dma_start(w1s[:, e, :], w1[:, e, :]).then_inc(w_in[e], 16)
                sp_q.dma_start(w2s[:, e, :, :], w2[:, e, :, :]).then_inc(w_in[e], 16)
            sp_q.wait_ge(zeroed, 2)
            sp_q.dma_start(rows_t, fill[:, :, :]).then_inc(filled, 16)

            with sp_q.Fori(0, G) as g:
                sp_q.wait_ge(cv_ready, g * NB + NB)
                sp_q.dma_start(bc_dram[:, bass.ts(g, GW)], cv[:, 2, :]).then_inc(bc_stored, 16)

            sp_q.wait_ge(bc_stored, 16 * G)
            sp_q.wait_ge(xs_ready, NT)

            def load_chunk(c, k, i):
                sp_q.dma_start(bcT[:, k, :, :], bc_dram[:, bass.ts(c, P)].rearrange("(b n) t -> n b t", b=2)).then_inc(bc_in[k], 16)
                sp_q.dma_start(btok[:, k, :], xs_all[:, bass.ds(c, 1), DI:DI + N].rearrange("p a n -> p (a n)")).then_inc(bc_in[k], 16)

            for k in range(2):
                load_chunk(k, k, 0)

            def store_pair(q):
                sp_q.wait_ge(outrow_ready, q + 1)
                sp_q.dma_start(out_t[:, bass.ds(2 * q, 2), :], outrow[:, :, :]).then_inc(stored, 16)

            def pair(i):
                for k in range(2):
                    sp_q.wait_ge(off_done, 2 * i + k - 1)
                    load_chunk(2 * i + k, k, i)
                store_pair(i - 1)

            pair(1)
            with sp_q.Fori(2, PAIRS) as i:
                pair(i)
            store_pair(PAIRS - 1)

            sp_q.wait_ge(scattered, 32 * PAIRS)
            sp_q.wait_ge(filled, 16)
            sp_q.dma_start(rows[:, :, :], rows_t[:, 0:STI, :]).then_inc(rows_in, 16)
            sp_q.wait_ge(rows_turned, STI)
            sp_q.wait_ge(tok5_ready, 1)
            sp_q.dma_start(rows[:, :, :], rows_t[:, STI:2 * STI, :]).then_inc(rows_in, 16)
            for e in range(EI):
                sp_q.wait_ge(ey_done, e + 1)
                sp_q.dma_start(w1s[:, e, :], w1[:, EI + e, :]).then_inc(w_in[e], 16)
                sp_q.dma_start(w2s[:, e, :, :], w2[:, EI + e, :, :]).then_inc(w_in[e], 16)
            sp_q.wait_ge(stored, 16 * PAIRS)
            sp_q.wait_ge(added, 16 * SLOTS // P)

        @block.gpsimd
        def _(pool):
            pool.memset(fill[:, :, :], 0.0).then_inc(const0, 1)
            pool.memset(ones[:, :], 1.0).then_inc(const0, 1)
            pool.memset(ones_h[:, :], 1.0).then_inc(consts, 1)
            pool.memset(mhalf[:, :], -0.5).then_inc(consts, 1)
            pool.memset(eps[:, :], EPS).then_inc(consts, 1)
            pool.memset(none[:, :], 0).then_inc(consts, 1)
            pool.memset(eps_sum[:, :], EPS * DI).then_inc(consts, 1)
            pool.memset(pair_step[:, :], 2 * P).then_inc(consts, 1)
            pool.memset(ident[:, :], 0.0).then_inc(const0, 1)
            pool.wait_ge(const0, 3)
            pool.wait_ge(consts, 1)
            pool.affine_select(out=ident[:, :], in_=ident[:, :], compare_op=ALU.not_equal, fill=1.0, base=0,
                               pattern=[[-1, P]], channel_multiplier=1).then_inc(consts, 1)
            pool.affine_select(out=upto[:, :], in_=ones[:, :], compare_op=ALU.is_ge, fill=0.0, base=0,
                               pattern=[[1, P]], channel_multiplier=-1).then_inc(consts, 1)
            pool.affine_select(out=after[:, :], in_=ones[:, :], compare_op=ALU.is_gt, fill=0.0, base=0,
                               pattern=[[-1, P]], channel_multiplier=1).then_inc(consts, 1)
            pool.affine_select(out=upto_h[:, :], in_=ones_h[:, :], compare_op=ALU.is_ge, fill=0.0, base=0,
                               pattern=[[1, P]], channel_multiplier=-1).then_inc(consts, 1)
            pool.memset(fill[:, :, D:ROW].bitcast(I32), FAR).then_inc(zeroed, 1)
            pool.memset(raw[:, :, 0:TAPS - 1], 0.0).then_inc(zeroed, 1)
            pool.memset(state[:, :], 0.0).then_inc(consts, 1)
            pool.memset(count[:, :], 0.0).then_inc(consts, 1)
            pool.iota(slot_base[:, :], pattern=[[0, 2], [CAP, E]], base=-1, channel_multiplier=0,
                      allow_small_or_imprecise_dtypes=True).then_inc(consts, 1)
            pool.iota(prefer[:, :], pattern=[[0, 2], [-1, E]], base=E, channel_multiplier=0,
                      allow_small_or_imprecise_dtypes=True).then_inc(consts, 1)
            pool.iota(rowC[:, :, D:ROW].bitcast(I32), pattern=[[P, 2], [1, 1]], base=-2 * P,
                      channel_multiplier=1).then_inc(tok_ready, 1)
            pool.wait_ge(par_in, 16)
            pool.tensor_copy(by_head(dskip[:, :], HD), heads(col(C_DSKIP, H), HD)).then_inc(consts, 1)

            def ln1_factors(g):
                mu, var = mv1[:, :, 0], mv1[:, :, 1]
                ve, r1, q1, q2, q3, r2, rr, s1, nm = (sm1[:, n, :] for n in range(9))
                half = mhalf[:, 0:GT]
                pool.wait_ge(consts, 15)
                pool.wait_ge(mv1_ready, g * GT + GT)
                if begun(g * GT):
                    pool.wait_ge(xx_ready, g * GT)
                pool.tensor_tensor(ve, var, eps[:, 0:GT], ALU.add).then_inc(sm1_step, 1)
                pool.wait_ge(sm1_step, 9 * g + 1)
                pool.tensor_tensor(r1, ve, half, ALU.pow).then_inc(sm1_step, 1)
                pool.wait_ge(sm1_step, 9 * g + 2)
                pool.tensor_tensor(q1, var, r1, ALU.mult).then_inc(sm1_step, 1)
                pool.wait_ge(sm1_step, 9 * g + 3)
                pool.tensor_tensor(q2, q1, r1, ALU.mult).then_inc(sm1_step, 1)
                pool.wait_ge(sm1_step, 9 * g + 4)
                pool.tensor_tensor(q3, q2, eps[:, 0:GT], ALU.add).then_inc(sm1_step, 1)
                pool.wait_ge(sm1_step, 9 * g + 5)
                pool.tensor_tensor(r2, q3, half, ALU.pow).then_inc(sm1_step, 1)
                pool.wait_ge(sm1_step, 9 * g + 6)
                pool.tensor_tensor(rr, r1, r2, ALU.mult).then_inc(sm1_step, 1)
                pool.tensor_tensor(s1, r1, ones[:, 0:GT], ALU.add).then_inc(sm1_step, 1)
                pool.tensor_tensor(nm, mu, r1, ALU.mult).then_inc(sm1_step, 1)

            ln1_factors(0)
            with pool.Fori(1, G) as g:
                ln1_factors(g)

            pool.wait_ge(w_ready, 1)

            def inputs(c, k, skip=False):
                a_c = a_all[:, bass.ds(c * H, H)]
                xs_c = by_head(xs_all[:, bass.ds(c, 1), 0:DI].rearrange("p a n -> p (a n)"), HD)
                if not skip:
                    pool.wait_ge(yg_ready, c - 1)
                pool.tensor_tensor(by_head(at[:, k, :], P), heads(a_c, P),
                                   upto[:, :].unsqueeze(1).to_broadcast([P, H, P]), ALU.mult).then_inc(at_ready, 1)
                pool.tensor_tensor(by_head(xw[:, k, :], HD), xs_c, heads(w_all[:, bass.ds(c * H, H)], HD), ALU.mult).then_inc(xw_ready, 1)
                pool.tensor_tensor(by_head(xdt[:, k, :], HD), xs_c, heads(dt_all[:, bass.ds(c * H, H)], HD), ALU.mult).then_inc(xdt_ready, 1)
                pool.tensor_tensor(dxs[:, k, :], xs_all[:, bass.ds(c, 1), 0:DI].rearrange("p a n -> p (a n)"), dskip[:, :], ALU.mult).then_inc(dxs_ready, 1)

            def decay_state(c):
                if begun(c):
                    pool.wait_ge(state_ready, c)
                pool.tensor_tensor(by_head(sdec[:, :], HD), by_head(state[:, :], HD),
                                   heads(ex_all[0:N, 2, bass.ds(c * H, H)], HD), ALU.mult).then_inc(sdec_ready, 1)

            def rms_factor(c, k, skip=False):
                pool.wait_ge(ssq_ready, c + 1)
                pool.tensor_tensor(msq[:, k:k + 1], ssq[:, k:k + 1], eps_sum[:, :], ALU.add).then_inc(msq_ready, 1)
                pool.wait_ge(msq_ready, c + 1)
                if not skip:
                    pool.wait_ge(x1_ready, c - 1)
                pool.tensor_tensor(rms[:, k:k + 1], msq[:, k:k + 1], mhalf[:, 0:1], ALU.pow).then_inc(rms_ready, 1)

            def ln2_factor(q):
                pool.wait_ge(mv2_ready, 2 * q + 2)
                pool.tensor_tensor(ve2[:, :], mv2[:, :, 1], eps[:, 0:2], ALU.add).then_inc(ve2_ready, 1)
                pool.wait_ge(ve2_ready, q + 1)
                pool.tensor_tensor(rs2[:, :], ve2[:, :], mhalf[:, 0:2], ALU.pow).then_inc(rs2_ready, 1)

            def pass_waits(n=0):
                pool.tensor_tensor(passed[:, n:n + 1], eps_sum[:, :], eps_sum[:, :], ALU.add).then_inc(passes, 1)

            def scatter(q):
                if begun(32 * q):
                    pool.wait_ge(scattered, 32 * q)
                pool.wait_ge(tok_ready, q + 1)
                tok = rowC[:, :, D:ROW].bitcast(I32)
                pool.tensor_tensor(tok, tok, pair_step[:, :].unsqueeze(2), ALU.add).then_inc(tok_ready, 1)
                pool.wait_ge(tok_ready, q + 2)
                pool.wait_ge(xf_ready, 2 * q + 2)
                pool.wait_ge(slot_ready, q + 1)
                pool.wait_ge(filled, 16)
                pass_waits()
                for j in range(2):
                    pool.indirect_dma_start(slots_dram, bass.IndirectOffsetOnAxis(ap=sloti[:, j:j + 1], axis=0),
                                            rowC[:, j, :], None, bounds_check=SLOTS - 1, oob_is_err=False).then_inc(scattered, 16)

            inputs(0, 0, skip=True)
            decay_state(0)
            inputs(1, 1, skip=True)
            rms_factor(0, 0, skip=True)
            decay_state(1)
            inputs(2, 0)
            rms_factor(1, 1, skip=True)

            def pair(i, last=False):
                decay_state(2 * i)
                ln2_factor(i - 1)
                inputs(2 * i + 1, 1)
                rms_factor(2 * i, 0)
                decay_state(2 * i + 1)
                if not last:
                    inputs(2 * i + 2, 0)
                scatter(i - 1)
                rms_factor(2 * i + 1, 1)

            pair(1)
            with pool.Fori(2, PAIRS - 1) as i:
                pair(i)
            pair(PAIRS - 1, last=True)
            ln2_factor(PAIRS - 1)
            scatter(PAIRS - 1)

            for it in range(E // EI):
                pool.wait_ge(rows_in, it * 16 + 16)
                if begun(it * 16 * STI):
                    pool.wait_ge(added, it * 16 * STI)
                pool.tensor_tensor(tok5[:, :], rows[:, :, D].bitcast(I32), none[:, :], ALU.add).then_inc(tok5_ready, 1)
                pool.wait_ge(tok5_ready, it + 1)
                pool.wait_ge(stored, 16 * PAIRS)
                for t in range(STI):
                    if t in (0, 4):
                        pool.wait_ge(yrow_ready, it * 2 + (1 if t < 4 else 2))
                        pass_waits(1 + it * 2 + (t == 4))
                    pool.indirect_dma_start(out, bass.IndirectOffsetOnAxis(ap=tok5[:, t:t + 1], axis=0),
                                            yrow[:, t, :], None, bounds_check=T - 1, oob_is_err=False,
                                            compute_op=ALU.add).then_inc(added, 16)

        @block.scalar
        def _(act):
            act.wait_ge(par_in, 16)
            act.activation(nA[:, 0, :], col(C_ALOG, H), ACT.Exp).then_inc(A_exp, 1)

            def turn_xn(g):
                act.wait_ge(xn_turned, g + 1)
                act.activation(xnT[:, :], bank[0][:, :], ACT.Identity, bias=col(C_LNB), scale=col(C_LNW)).then_inc(xnT_ready, 1)

            def take_raw(g):
                for m in range(NB):
                    act.wait_ge(xbc_done, g * NB + m + 1)
                    act.activation(raw[:, m, bass.ds(g * GW + TAPS - 1, GW)], bank[1 + m][:, :], ACT.Copy).then_inc(raw_ready, 1)

            def gate(g):
                for p in range(2):
                    act.wait_ge(z_done, g * 2 + p + 1)
                    act.activation(sz_all[:, bass.ds(g * GT + 2 * p, 2), :].rearrange("p a n -> p (a n)"), bank[4 + p][:, :],
                                   ACT.Silu).then_inc(z_read, 1)

            def silu_conv(g, skip=False):
                for m in range(NB):
                    act.wait_ge(tap_done, g * NB * TAPS + NB * (TAPS - 1) + m + 1)
                    if not skip and m == 0:
                        act.wait_ge(cv_turned, g * GT)
                        act.wait_ge(bc_stored, 16 * g)
                    act.activation(cv[:, m, :], acc[:, m, :], ACT.Silu, bias=col(C_CONVB + m)).then_inc(cv_ready, 1)

            def take_xs(g):
                for j in range(GT):
                    act.wait_ge(cv_turned, g * GT + j + 1)
                    act.activation(xs_all[:, bass.ds(g * GT + j, 1), :].rearrange("p a n -> p (a n)"),
                                   bank[6 + j % 2][:, 0:DI + N], ACT.Copy).then_inc(xs_ready, 1)

            turn_xn(0)
            take_raw(0)
            gate(0)
            turn_xn(1)
            take_raw(1)
            gate(1)
            silu_conv(0, skip=True)
            take_xs(0)
            with act.Fori(2, G) as g:
                turn_xn(g)
                take_raw(g)
                gate(g)
                silu_conv(g - 1)
                take_xs(g - 1)
            silu_conv(G - 1)
            take_xs(G - 1)

            act.wait_ge(sp_step, 2)
            act.activation(sp[:, 2, :], sp[:, 1, :], ACT.Exp).then_inc(sp_exp, 1)
            act.wait_ge(sums_done, 1)
            act.activation(ex_all[:, :, :].rearrange("p a n -> p (a n)"), bank[1][:, 0:3 * NT * H], ACT.Exp).then_inc(sums_exp, 1)

            def chunk_decay(c, k, skip=False):
                act.wait_ge(seg_done, c + 1)
                if not skip:
                    act.wait_ge(m_ready, c - 1)
                act.activation(decay[:, k, :], bank[0][:, :], ACT.Exp).then_inc(decay_ready, 1)

            def sum_squares(c, k, skip=False):
                act.wait_ge(yg_ready, c + 1)
                if not skip:
                    act.wait_ge(msq_ready, c - 1)
                act.activation(junk[:, :], yg[:, k, :], ACT.Square, accum_out=ssq[:, k:k + 1]).then_inc(ssq_ready, 1)

            def take_ygT(c, k):
                act.wait_ge(yg_turned, c + 1)
                act.activation(ygT[:, k, :], bank[3][:, 0:DI], ACT.Copy).then_inc(ygT_ready, 1)

            def take_xfT(q):
                act.wait_ge(xf_turned, q + 1)
                act.activation(xfT[:, :], bank[3][:, DI:2 * DI], ACT.Copy).then_inc(xfT_ready, 1)

            def hidden(q, b, skip=False):
                act.wait_ge(hid_done, q * FB + b + 1)
                if not skip:
                    if begun(q):
                        act.wait_ge(ov_done, q)
                act.activation(hT[:, b, :], bank[6 + b % 2][:, 0:2 * P], ACT.Relu, bias=col(C_OB1 + b)).then_inc(hid_ready, 1)

            chunk_decay(0, 0, skip=True)
            sum_squares(0, 0, skip=True)
            take_ygT(0, 0)
            chunk_decay(1, 1, skip=True)
            sum_squares(1, 1, skip=True)
            take_ygT(1, 1)
            def pair(i):
                chunk_decay(2 * i, 0)
                take_xfT(i - 1)
                hidden(i - 1, 0)
                sum_squares(2 * i, 0)
                take_ygT(2 * i, 0)
                hidden(i - 1, 1)
                chunk_decay(2 * i + 1, 1)
                hidden(i - 1, 2)
                hidden(i - 1, 3)
                sum_squares(2 * i + 1, 1)
                take_ygT(2 * i + 1, 1)

            pair(1)
            with act.Fori(2, PAIRS) as i:
                pair(i)
            take_xfT(PAIRS - 1)
            for b in range(FB):
                hidden(PAIRS - 1, b)

            for it in range(E // EI):
                act.wait_ge(rows_turned, it * STI + 4)
                act.activation(bufT[:, 0:4 * P], bank[0][:, :], ACT.Copy).then_inc(bufT_ready, 1)
                act.wait_ge(rows_turned, it * STI + 5)
                act.activation(bufT[:, 4 * P:SI], bank[1][:, 0:P], ACT.Copy).then_inc(bufT_ready, 1)
                for e in range(EI):
                    act.wait_ge(eh_done, (it * EI + e) * 2 + 1)
                    if begun(it * EI if e < 2 else it * EI + e - 1):
                        act.wait_ge(ey_done, it * EI if e < 2 else it * EI + e - 1)
                    for b in range(2):
                        act.activation(hE[:, e % 2, b, :], bank[(6, 0)[e % 2]][:, b * CAP:(b + 1) * CAP], ACT.Relu,
                                       bias=col(C_B1 + (it * EI + e) * FB + b)).then_inc(eh_act, 1)
                act.wait_ge(ey_turned, it * STI + 4)
                if begun(it * 16 * STI):
                    act.wait_ge(added, it * 16 * STI)
                act.activation(yrow[:, 0:4, :].rearrange("p a n -> p (a n)"), bank[2][:, :], ACT.Copy).then_inc(yrow_ready, 1)
                act.wait_ge(ey_turned, it * STI + 5)
                act.activation(yrow[:, 4, :], bank[3][:, 0:P], ACT.Copy).then_inc(yrow_ready, 1)

        @block.tensor
        def _(pe):
            pe.wait_ge(consts, 15)
            pe.wait_ge(win_in, 16)

            def turn_xn(g, skip=False):
                pe.wait_ge(xn_ready, g + 1)
                if not skip:
                    pe.wait_ge(dt_read, g)
                for j in range(GT):
                    last = pe.transpose(bank[0][:, j * P:(j + 1) * P], xn[:, j, :], ident[:, :])
                last.then_inc(xn_turned, 1)

            def in_proj(g, skip=False):
                pe.wait_ge(xnT_ready, g + 1)
                for m in range(NB):
                    if not skip:
                        pe.wait_ge(raw_ready, (g - 1) * NB + m + 1)
                    pe.matmul(bank[1 + m][:, :], win[:, DI + m * P:DI + (m + 1) * P], xnT[:, :], start=True, stop=True).then_inc(xbc_done, 1)
                for j in range(GT):
                    last = pe.matmul(bank[0][:, j * H:(j + 1) * H], xnT[:, j * P:(j + 1) * P], win[:, DI + NXBC:DI + NXBC + H],
                                     start=True, stop=True)
                last.then_inc(dt_done, 1)
                for p in range(2):
                    if not skip:
                        pe.wait_ge(z_read, (g - 1) * 2 + p + 1)
                    for j in range(2):
                        last = pe.matmul(bank[4 + p][:, j * DI:(j + 1) * DI], xnT[:, (2 * p + j) * P:(2 * p + j + 1) * P], win[:, 0:DI],
                                         start=True, stop=True)
                    last.then_inc(z_done, 1)

            def turn_cv(g, skip=False):
                pe.wait_ge(cv_ready, g * NB + NB)
                for j in range(GT):
                    if not (skip and j < 2):
                        pe.wait_ge(xs_ready, g * GT + j - 1)
                    to = bank[6 + j % 2]
                    for m in range(2):
                        pe.transpose(to[:, m * P:(m + 1) * P], cv[:, m, j * P:(j + 1) * P], ident[:, :])
                    pe.transpose(to[:, DI:DI + N], cv[0:N, 2, j * P:(j + 1) * P], ident[0:N, 0:N]).then_inc(cv_turned, 1)

            turn_xn(0, skip=True)
            in_proj(0, skip=True)
            turn_xn(1)
            in_proj(1)
            turn_cv(0, skip=True)
            with pe.Fori(2, G) as g:
                turn_xn(g)
                in_proj(g)
                turn_cv(g - 1)
            turn_cv(G - 1)

            pe.wait_ge(a_ready, 1)
            pe.wait_ge(raw_ready, G * NB)
            w = NT * H
            pe.matmul(bank[1][:, 0:w], upto[:, :], a_all[:, :], start=True, stop=True)
            pe.matmul(bank[1][:, w:2 * w], after[:, :], a_all[:, :], start=True, stop=True)
            pe.matmul(bank[1][:, 2 * w:3 * w], ones[:, :], a_all[:, :], start=True, stop=True).then_inc(sums_done, 1)
            pe.wait_ge(sums_exp, 1)
            pe.wait_ge(wout_in, 16)
            pe.wait_ge(consts_v, 2)
            pe.wait_ge(ffn_in, 48)

            def front(c, k, i, skip=False):
                b_t, c_t = bcT[:, k, 0, :], bcT[:, k, 1, :]
                pe.wait_ge(bc_in[k], 32 * i + 32)
                pe.wait_ge(xw_ready, c + 1)
                if begun(c):
                    pe.wait_ge(state_ready, c)
                pe.matmul(bank[1][:, 0:P], b_t, c_t, start=True, stop=True)
                pe.matmul(bank[1][0:N, P:P + DI], btok[:, k, :], xw[:, k, :], start=True, stop=True).then_inc(cbst_done, 1)
                pe.wait_ge(at_ready, c + 1)
                if not skip:
                    pe.wait_ge(decay_ready, c)
                pe.matmul(bank[0][:, :], after[:, :], at[:, k, :], start=True, stop=True).then_inc(seg_done, 1)
                if not skip:
                    pe.wait_ge(yg_ready, c)
                pe.matmul(bank[2][:, 0:DI], c_t, state[:, :], start=True, stop=True).then_inc(off_done, 1)

            def diag(c, k):
                pe.wait_ge(m_ready, c + 1)
                pe.wait_ge(xdt_ready, c + 1)
                for h in range(H):
                    last = pe.matmul(bank[2][:, DI + h * HD:DI + (h + 1) * HD], m_t[:, k, h * P:(h + 1) * P],
                                     xdt[:, k, h * HD:(h + 1) * HD], start=True, stop=True)
                last.then_inc(diag_done, 1)

            def turn_yg(c, k, q=None):
                pe.wait_ge(yg_ready, c + 1)
                if q is not None:
                    pe.wait_ge(xfT_ready, q + 1)
                for m in range(2):
                    last = pe.transpose(bank[3][:, m * P:(m + 1) * P], yg[:, k, m * P:(m + 1) * P], ident[:, :])
                last.then_inc(yg_turned, 1)

            def project(c, k, reader=None, count=0):
                pe.wait_ge(ygT_ready, c + 1)
                if reader is not None:
                    pe.wait_ge(reader, count)
                for m in range(2):
                    last = pe.matmul(bank[4][:, 0:D], ygT[:, k, m * P:(m + 1) * P], wout[:, m, :], start=(m == 0), stop=(m == 1))
                last.then_inc(proj_done, 1)

            def turn_xf(q):
                pe.wait_ge(xf_ready, 2 * q + 2)
                pe.wait_ge(ygT_ready, 2 * q + 2)
                for j in range(2):
                    last = pe.transpose(bank[3][:, DI + j * P:DI + (j + 1) * P], rowC[:, j, 0:D], ident[:, :])
                last.then_inc(xf_turned, 1)

            def router(q):
                pe.wait_ge(xfT_ready, q + 1)
                pe.wait_ge(x1_ready, 2 * q + 2)
                for j in range(2):
                    last = pe.matmul(bank[4][:, P + j * E:P + (j + 1) * E], xfT[:, j * P:(j + 1) * P], wrt[:, :], start=True, stop=True)
                last.then_inc(logits_done, 1)

            def hidden(q, b, skip=False):
                if not skip:
                    pe.wait_ge(hid_ready, q * FB + b - 1)
                pe.matmul(bank[6 + b % 2][:, 0:2 * P], wo1[:, b * P:(b + 1) * P], xfT[:, :], start=True, stop=True).then_inc(hid_done, 1)

            def rank(q, reader, count):
                first, second, total = (bank[4][:, 160 + n * E:160 + (n + 1) * E] for n in range(3))
                pe.wait_ge(oh_ready, q + 1)
                pe.wait_ge(reader, count)
                pe.matmul(first, upto_h[:, :], oh[:, 0:E], start=True, stop=True)
                pe.matmul(second, upto_h[:, :], oh[:, E:2 * E], start=True, stop=False)
                pe.matmul(second, ones_h[:, :], oh[:, 0:E], start=False, stop=True)
                pe.matmul(total, ones_h[:, :], oh[:, 0:E], start=True, stop=False)
                pe.matmul(total, ones_h[:, :], oh[:, E:2 * E], start=False, stop=True).then_inc(rank_done, 1)

            def overflow(q, j, skip=False):
                if j == 0:
                    pe.wait_ge(hid_ready, q * FB + FB)
                    if not skip:
                        if begun(q):
                            pe.wait_ge(ov_read, q)
                for b in range(FB):
                    last = pe.matmul(bank[5][:, j * D:(j + 1) * D], hT[:, b, j * P:(j + 1) * P], wo2[:, b, :],
                                     start=(b == 0), stop=(b == FB - 1))
                if j == 1:
                    last.then_inc(ov_done, 1)

            front(0, 0, 0, skip=True)
            diag(0, 0)
            turn_yg(0, 0)
            project(0, 0)
            front(1, 1, 0)
            diag(1, 1)
            turn_yg(1, 1)
            project(1, 1, reader=x1_ready, count=1)
            def pair(i):
                q = i - 1
                front(2 * i, 0, i)
                turn_xf(q)
                diag(2 * i, 0)
                router(q)
                hidden(q, 0, skip=True)
                turn_yg(2 * i, 0, q)
                hidden(q, 1, skip=True)
                project(2 * i, 0, reader=route_step, count=q * 4 + 1)
                front(2 * i + 1, 1, i)
                hidden(q, 2)
                diag(2 * i + 1, 1)
                hidden(q, 3)
                rank(q, x1_ready, 2 * i + 1)
                overflow(q, 0)
                turn_yg(2 * i + 1, 1, q)
                overflow(q, 1)
                project(2 * i + 1, 1, reader=rank_step, count=q * 7 + 2)

            pair(1)
            with pe.Fori(2, PAIRS) as i:
                pair(i)
            q = PAIRS - 1
            turn_xf(q)
            router(q)
            hidden(q, 0, skip=True)
            hidden(q, 1, skip=True)
            hidden(q, 2)
            hidden(q, 3)
            rank(q, route_step, q * 4 + 1)
            overflow(q, 0)
            overflow(q, 1)

            def expert_hidden(it, e):
                n = it * EI + e
                if e == 0:
                    pe.wait_ge(bufT_ready, it * 2 + 2)
                    pe.wait_ge(hid_ready, PAIRS * FB)
                pe.wait_ge(w_in[e], it * 32 + 32)
                read = it * EI * 2 if e < 2 else (n - 1) * 2
                if begun(read):
                    pe.wait_ge(eh_act, read)
                if begun(read):
                    pe.wait_ge(eh_dve, read)
                for half in range(2):
                    for b in range(2):
                        last = pe.matmul(bank[(6, 0)[e % 2] + half][:, b * CAP:(b + 1) * CAP], w1s[:, e, (2 * half + b) * P:(2 * half + b + 1) * P],
                                         bufT[:, e * CAP:(e + 1) * CAP], start=True, stop=True)
                    last.then_inc(eh_done, 1)

            def expert_out(it, e):
                n = it * EI + e
                pe.wait_ge(eh_act, n * 2 + 2)
                pe.wait_ge(eh_dve, n * 2 + 2)
                if e < 2:
                    pe.wait_ge(outrow_ready, PAIRS)
                    if begun(it * EI):
                        pe.wait_ge(ey_ready, it * EI)
                else:
                    pe.wait_ge(ey_ready, n - 1)
                for b in range(FB):
                    last = pe.matmul(bank[4 + e % 2][:, 0:CAP], w2s[:, e, b, :], hE[:, e % 2, b, :], start=(b == 0), stop=(b == FB - 1))
                last.then_inc(ey_done, 1)

            pe.wait_ge(state_ready, NT)
            for it in range(E // EI):
                pe.wait_ge(rows_in, it * 16 + 16)
                for t in range(STI):
                    to = bank[0][:, t * P:(t + 1) * P] if t < 4 else bank[1][:, 0:P]
                    pe.transpose(to, rows[:, t, 0:D], ident[:, :]).then_inc(rows_turned, 1)
                expert_hidden(it, 0)
                for e in range(EI):
                    if e + 1 < EI:
                        expert_hidden(it, e + 1)
                    expert_out(it, e)
                pe.wait_ge(ey_ready, it * EI + EI)
                if begun(it * 2):
                    pe.wait_ge(yrow_ready, it * 2)
                for t in range(STI):
                    to = bank[2][:, t * P:(t + 1) * P] if t < 4 else bank[3][:, 0:P]
                    pe.transpose(to, yT[:, t * P:(t + 1) * P], ident[:, :]).then_inc(ey_turned, 1)

        @block.vector
        def _(dve):
            def stats(g, first=False):
                for j in range(GT):
                    dve.bn_stats(st1[:, j, :], x_all[:, bass.ds(g * GT + j, 1), :].rearrange("p a d -> p (a d)")).then_inc(st1_ready, 1)
                dve.wait_ge(st1_ready, g * GT + GT)
                if not first:
                    add_ln(g - 1)
                for j in range(GT):
                    dve.bn_aggr(mv1[:, j, :], st1[:, j, :]).then_inc(mv1_ready, 1)

            def add_ln(g):
                dve.wait_ge(sm1_step, 9 * g + 9)
                for j in range(GT):
                    xt = x_all[:, bass.ds(g * GT + j, 1), :].rearrange("p a d -> p (a d)")
                    dve.tensor_scalar(xt, xt, sm1[:, 7, j:j + 1], sm1[:, 8, j:j + 1], ALU.mult, ALU.subtract).then_inc(xx_ready, 1)

            def normalise(g, first=False):
                dve.wait_ge(sm1_step, 9 * g + 7)
                if not first:
                    dve.wait_ge(xn_turned, g)
                for j in range(GT):
                    last = dve.tensor_scalar(xn[:, j, :], x_all[:, bass.ds(g * GT + j, 1), :].rearrange("p a d -> p (a d)"), mv1[:, j, 0:1],
                                             sm1[:, 6, j:j + 1], ALU.subtract, ALU.mult)
                last.then_inc(xn_ready, 1)

            def take_dt(g):
                dve.wait_ge(dt_done, g + 1)
                dve.tensor_tensor(dt_all[:, bass.ts(g, GT * H)].rearrange("p (j h) -> p j h", h=H),
                                  bank[0][:, 0:GT * H].rearrange("p (j h) -> p j h", h=H),
                                  col(C_DTB, H).unsqueeze(1).to_broadcast([P, GT, H]), ALU.add).then_inc(dt_read, 1)

            def conv(g, first=False):
                for k in range(TAPS):
                    for m in range(NB):
                        n = g * NB * TAPS + k * NB + m
                        src = raw[:, m, bass.ds(g * GW + k, GW)]
                        tap = col(C_CONVW + m * TAPS + k)
                        if k == 0:
                            dve.wait_ge(raw_ready, g * NB + m + 1)
                            if not first:
                                dve.wait_ge(cv_ready, (g - 1) * NB + m + 1)
                            dve.tensor_scalar(acc[:, m, :], src, tap, None, ALU.mult).then_inc(tap_done, 1)
                        else:
                            dve.wait_ge(tap_done, n - NB + 1)
                            dve.scalar_tensor_tensor(out=acc[:, m, :], in0=src, scalar=tap, in1=acc[:, m, :],
                                                     op0=ALU.mult, op1=ALU.add).then_inc(tap_done, 1)

            dve.wait_ge(par_in, 16)
            dve.wait_ge(zeroed, 2)
            dve.wait_ge(x_in[0], 16)
            stats(0, first=True)
            normalise(0, first=True)
            take_dt(0)
            for g in range(1, G):
                dve.wait_ge(x_in[g], 16)
            stats(1)
            normalise(1)
            conv(0, first=True)
            take_dt(1)
            with dve.Fori(2, G) as g:
                stats(g)
                normalise(g)
                conv(g - 1)
                take_dt(g)
            conv(G - 1)
            add_ln(G - 1)
            dve.wait_ge(wout_in, 16)
            for m in range(2):
                dve.tensor_scalar(wout[:, m, :], wout[:, m, :], col(C_NORMW + m), float(DI) ** 0.5, ALU.mult, ALU.mult).then_inc(consts_v, 1)

            step = 0

            def after_step(ins):
                nonlocal step
                step += 1
                ins.then_inc(sp_step, 1)

            def row(n):
                return sp[:, n, :]

            dve.wait_ge(dt_read, G)
            after_step(dve.tensor_scalar(row(0), dt_all[:, :], -1.0, None, ALU.mult))
            dve.wait_ge(sp_step, step)
            after_step(dve.tensor_tensor(row(1), row(0), dt_all[:, :], ALU.min))
            dve.wait_ge(A_exp, 1)
            after_step(dve.tensor_scalar(nA[:, 1, :], nA[:, 0, :], -1.0, None, ALU.mult))
            dve.wait_ge(sp_exp, 1)
            after_step(dve.tensor_scalar(row(3), row(2), 2.0, None, ALU.add))
            dve.wait_ge(sp_step, step)
            after_step(dve.reciprocal(row(4), row(3)))
            dve.wait_ge(sp_step, step)
            after_step(dve.tensor_tensor(row(5), row(2), row(4), ALU.mult))
            dve.wait_ge(sp_step, step)
            after_step(dve.tensor_tensor(row(6), row(5), row(5), ALU.mult))
            dve.wait_ge(sp_step, step)
            after_step(dve.tensor_scalar(row(7), row(6), 1.0 / 15.0, None, ALU.mult))
            for n, odd in enumerate((13, 11, 9, 7, 5, 3)):
                dve.wait_ge(sp_step, step)
                after_step(dve.scalar_tensor_tensor(out=row(8 + n), in0=row(7 + n), scalar=1.0 / odd, in1=row(6), op0=ALU.add, op1=ALU.mult))
            dve.wait_ge(sp_step, step)
            after_step(dve.scalar_tensor_tensor(out=row(14), in0=row(13), scalar=1.0, in1=row(5), op0=ALU.add, op1=ALU.mult))
            after_step(dve.tensor_scalar(row(15), dt_all[:, :], 0.0, None, ALU.max))
            dve.wait_ge(sp_step, step)
            after_step(dve.scalar_tensor_tensor(out=dt_all[:, :], in0=row(14), scalar=2.0, in1=row(15), op0=ALU.mult, op1=ALU.add))
            dve.wait_ge(sp_step, step)
            dve.tensor_tensor(a_all[:, :].rearrange("p (t h) -> p t h", h=H), dt_all[:, :].rearrange("p (t h) -> p t h", h=H),
                              nA[:, 1, :].unsqueeze(1).to_broadcast([P, NT, H]), ALU.mult).then_inc(a_ready, 1)
            dve.wait_ge(sums_exp, 1)
            dve.tensor_tensor(w_all[:, :], ex_all[:, 1, :], dt_all[:, :], ALU.mult).then_inc(w_ready, 1)

            def scores(c):
                dve.wait_ge(cbst_done, c + 1)
                dve.tensor_tensor(cb[:, :], bank[1][:, 0:P], upto[:, :], ALU.mult).then_inc(cb_ready, 1)

            def carry_state(c, q=None):
                if q is not None:
                    dve.wait_ge(st2_ready, 2 * q + 2)
                    if begun(q):
                        dve.wait_ge(rs2_ready, q)
                dve.wait_ge(sdec_ready, c + 1)
                dve.wait_ge(off_done, c + 1)
                dve.tensor_tensor(state[:, :], bank[1][0:N, P:P + DI], sdec[:, :], ALU.add).then_inc(state_ready, 1)

            def mix(c, k, skip=False):
                dve.wait_ge(decay_ready, c + 1)
                dve.wait_ge(cb_ready, c + 1)
                if not skip:
                    dve.wait_ge(diag_done, c - 1)
                dve.tensor_tensor(by_head(m_t[:, k, :], P), by_head(decay[:, k, :], P),
                                  cb[:, :].unsqueeze(1).to_broadcast([P, H, P]), ALU.mult).then_inc(m_ready, 1)

            def gated(c, k, skip=False):
                dve.wait_ge(diag_done, c + 1)
                dve.tensor_tensor(by_head(y_off[:, :], HD), by_head(bank[2][:, 0:DI], HD),
                                  heads(ex_all[:, 0, bass.ds(c * H, H)], HD), ALU.mult).then_inc(y_step, 1)
                dve.wait_ge(y_step, 3 * c + 1)
                dve.tensor_tensor(y_sum[:, :], bank[2][:, DI:2 * DI], y_off[:, :], ALU.add).then_inc(y_step, 1)
                dve.wait_ge(y_step, 3 * c + 2)
                dve.wait_ge(dxs_ready, c + 1)
                dve.tensor_tensor(y_skip[:, :], y_sum[:, :], dxs[:, k, :], ALU.add).then_inc(y_step, 1)
                dve.wait_ge(y_step, 3 * c + 3)
                if not skip:
                    dve.wait_ge(yg_turned, c - 1)
                    dve.wait_ge(ssq_ready, c - 1)
                dve.tensor_tensor(yg[:, k, :], y_skip[:, :], sz_all[:, bass.ds(c, 1), :].rearrange("p a n -> p (a n)"), ALU.mult).then_inc(yg_ready, 1)

            def residual(c, k):
                dve.wait_ge(proj_done, c + 1)
                dve.wait_ge(rms_ready, c + 1)
                xt = x_all[:, bass.ds(c, 1), :].rearrange("p a d -> p (a d)")
                dve.scalar_tensor_tensor(out=xt, in0=bank[4][:, 0:D], scalar=rms[:, k:k + 1], in1=xt, op0=ALU.mult, op1=ALU.add).then_inc(x1_ready, 1)

            def ln2_stats(q):
                dve.wait_ge(x1_ready, 2 * q + 2)
                for j in range(2):
                    dve.bn_stats(st2[:, j, :], x_all[:, bass.ds(2 * q + j, 1), :].rearrange("p a d -> p (a d)")).then_inc(st2_ready, 1)

            def ln2_aggregate(q):
                for j in range(2):
                    dve.bn_aggr(mv2[:, j, :], st2[:, j, :]).then_inc(mv2_ready, 1)

            def ln2(q):
                dve.wait_ge(rs2_ready, q + 1)
                if begun(32 * q):
                    dve.wait_ge(scattered, 32 * q)
                for j in range(2):
                    xt = x_all[:, bass.ds(2 * q + j, 1), :].rearrange("p a d -> p (a d)")
                    dve.tensor_scalar(rowC[:, j, 0:D], xt, mv2[:, j, 0:1], rs2[:, j:j + 1], ALU.subtract, ALU.mult).then_inc(xf_ready, 1)

            def pairwise(ap):
                return ap.rearrange("p (j e) -> p j e", e=E)

            def choose(q):
                dve.wait_ge(logits_done, q + 1)
                dve.tensor_tensor(pairwise(lg[:, :]), pairwise(bank[4][:, P:P + 2 * E]),
                                  col(C_RB, E).unsqueeze(1).to_broadcast([P, 2, E]), ALU.add).then_inc(route_step, 1)
                dve.wait_ge(route_step, 4 * q + 1)
                dve.tensor_reduce(lmax[:, :], pairwise(lg[:, :]), AX.X, ALU.max).then_inc(route_step, 1)
                dve.wait_ge(route_step, 4 * q + 2)
                dve.tensor_tensor(pairwise(iseq[:, :]), pairwise(lg[:, :]), lmax[:, :].unsqueeze(2).to_broadcast([P, 2, E]), ALU.is_equal).then_inc(route_step, 1)
                dve.wait_ge(route_step, 4 * q + 3)
                dve.tensor_tensor(pref[:, :], iseq[:, :], prefer[:, :], ALU.mult).then_inc(route_step, 1)
                dve.wait_ge(route_step, 4 * q + 4)
                dve.tensor_reduce(pmax[:, :], pairwise(pref[:, :]), AX.X, ALU.max).then_inc(pm_ready, 1)
                dve.wait_ge(pm_ready, q + 1)
                dve.tensor_tensor(pairwise(oh[:, :]), pairwise(pref[:, :]), pmax[:, :].unsqueeze(2).to_broadcast([P, 2, E]), ALU.is_equal).then_inc(oh_ready, 1)

            def slots(q):
                dve.wait_ge(rank_done, q + 1)
                if begun(7 * q):
                    dve.wait_ge(rank_step, 7 * q)
                dve.tensor_tensor(pairwise(rk[:, :]), pairwise(bank[4][:, 160:160 + 2 * E]),
                                  count[:, :].unsqueeze(1).to_broadcast([P, 2, E]), ALU.add).then_inc(rank_step, 1)
                dve.wait_ge(rank_step, 7 * q + 1)
                dve.tensor_tensor(count[:, :], bank[4][:, 160 + 2 * E:160 + 3 * E], count[:, :], ALU.add).then_inc(rank_step, 1)
                dve.tensor_scalar(over[:, :], rk[:, :], CAP + 0.5, float(FAR), ALU.is_gt, ALU.mult).then_inc(rank_step, 1)
                dve.tensor_tensor(place[:, :], rk[:, :], slot_base[:, :], ALU.add).then_inc(rank_step, 1)
                dve.wait_ge(rank_step, 7 * q + 4)
                dve.tensor_tensor(place2[:, :], place[:, :], over[:, :], ALU.add).then_inc(rank_step, 1)
                dve.wait_ge(rank_step, 7 * q + 5)
                dve.tensor_tensor(chosen[:, :], place2[:, :], oh[:, :], ALU.mult).then_inc(rank_step, 1)
                dve.wait_ge(rank_step, 7 * q + 6)
                dve.tensor_reduce(slotf[:, :], pairwise(chosen[:, :]), AX.X, ALU.add).then_inc(rank_step, 1)
                dve.wait_ge(rank_step, 7 * q + 7)
                dve.tensor_copy(sloti[:, :], slotf[:, :]).then_inc(slot_ready, 1)
                dve.tensor_scalar(noslot[:, :], slotf[:, :], float(FAR // 2), None, ALU.is_ge).then_inc(noslot_ready, 1)

            def finish(q):
                dve.wait_ge(ov_done, q + 1)
                dve.tensor_tensor(ovb[:, :, :], bank[5][:, 0:2 * D].rearrange("p (j d) -> p j d", j=2),
                                  col(C_OB2, D).unsqueeze(1).to_broadcast([P, 2, D]), ALU.add).then_inc(ov_read, 1)
                dve.wait_ge(ov_read, q + 1)
                dve.wait_ge(noslot_ready, q + 1)
                if begun(16 * q):
                    dve.wait_ge(stored, 16 * q)
                for j in range(2):
                    xt = x_all[:, bass.ds(2 * q + j, 1), :].rearrange("p a d -> p (a d)")
                    last = dve.scalar_tensor_tensor(out=outrow[:, j, :], in0=ovb[:, j, :], scalar=noslot[:, j:j + 1], in1=xt,
                                                    op0=ALU.mult, op1=ALU.add)
                last.then_inc(outrow_ready, 1)

            dve.wait_ge(consts, 15)
            dve.wait_ge(xx_ready, NT)
            for c in range(2):
                scores(c)
                carry_state(c)
                mix(c, c, skip=True)
                gated(c, c, skip=True)
                residual(c, c)
            def pair(i):
                q = i - 1
                scores(2 * i)
                ln2_stats(q)
                carry_state(2 * i, q)
                ln2_aggregate(q)
                mix(2 * i, 0)
                ln2(q)
                gated(2 * i, 0)
                choose(q)
                residual(2 * i, 0)
                scores(2 * i + 1)
                carry_state(2 * i + 1)
                mix(2 * i + 1, 1)
                gated(2 * i + 1, 1)
                slots(q)
                finish(q)
                residual(2 * i + 1, 1)

            pair(1)
            with dve.Fori(2, PAIRS) as i:
                pair(i)
            q = PAIRS - 1
            ln2_stats(q)
            dve.wait_ge(st2_ready, 2 * q + 2)
            dve.wait_ge(rs2_ready, q)
            ln2_aggregate(q)
            ln2(q)
            choose(q)
            slots(q)
            finish(q)

            for it in range(E // EI):
                for e in range(EI):
                    n = it * EI + e
                    dve.wait_ge(eh_done, n * 2 + 2)
                    if begun(it * EI if e < 2 else n - 1):
                        dve.wait_ge(ey_done, it * EI if e < 2 else n - 1)
                    for b in range(2):
                        dve.tensor_scalar(hE[:, e % 2, 2 + b, :], bank[(7, 1)[e % 2]][:, b * CAP:(b + 1) * CAP],
                                          col(C_B1 + n * FB + 2 + b), 0.0, ALU.add, ALU.max).then_inc(eh_dve, 1)
                    if e >= 1:
                        if begun(it * STI):
                            dve.wait_ge(ey_turned, it * STI)
                        dve.wait_ge(ey_done, n)
                        dve.tensor_scalar(yT[:, (e - 1) * CAP:e * CAP], bank[4 + (e - 1) % 2][:, 0:CAP],
                                          col(C_B2 + n - 1), None, ALU.add).then_inc(ey_ready, 1)
                n = it * EI + EI - 1
                dve.wait_ge(ey_done, n + 1)
                dve.tensor_scalar(yT[:, (EI - 1) * CAP:], bank[4 + (EI - 1) % 2][:, 0:CAP],
                                  col(C_B2 + n), None, ALU.add).then_inc(ey_ready, 1)


def kernel(**inputs):
    import numpy as np
    import concourse.bacc as bacc
    from concourse.bass_utils import run_bass_kernel_spmd as run

    v = {k: np.asarray(a) for k, a in inputs.items()}

    def at(name):
        return v["L0_" + name]

    def rows(a):
        return np.broadcast_to(a.reshape(1, -1), (P, a.size))

    sheet = np.concatenate([
        at("attn_ln_w")[:, None], at("attn_ln_b")[:, None],
        at("attn_conv_w").reshape(NB, P, TAPS).transpose(1, 0, 2).reshape(P, NB * TAPS),
        at("attn_conv_b").reshape(NB, P).T, at("attn_norm_w").reshape(2, P).T,
        at("ffn_ob1").reshape(FB, P).T, at("ffn_b1").reshape(E * FB, P).T, at("ffn_b2").T,
        rows(at("attn_dt_bias")), rows(at("attn_A_log")), rows(at("attn_D_skip")), rows(at("ffn_router_b")),
        rows(at("ffn_ob2"))], axis=1)
    arrays = {
        "x": at("attn_x").reshape(T, D), "sheet": sheet, "in_w": at("attn_in_proj_w").T,
        "out_w": at("attn_out_proj_w").T.reshape(2, P, D).transpose(1, 0, 2), "router_w": at("ffn_router_w"),
        "ow1": at("ffn_ow1"), "ow2": at("ffn_ow2").reshape(FB, P, D).transpose(1, 0, 2),
        "w1": at("ffn_w1").transpose(1, 0, 2), "w2": at("ffn_w2").reshape(E, FB, P, D).transpose(2, 0, 1, 3),
    }
    arrays = {k: np.ascontiguousarray(a) for k, a in arrays.items()}
    nc = bacc.Bacc("TRN2", target_bir_lowering=False, num_devices=1)
    args = {k: nc.dram_tensor("in_" + k, a.shape, F32, kind="ExternalInput").ap() for k, a in arrays.items()}
    out = nc.dram_tensor("out_rows", [T, D], F32, kind="ExternalOutput").ap()
    build(nc, out=out, **args)
    r = run(nc, [{"in_" + k: a for k, a in arrays.items()}], core_ids=[0])
    return np.asarray(r.results[0]["out_rows"]).reshape(at("attn_x").shape)
```

```python
from contextlib import ExitStack

import concourse.bass as bass
from concourse import mybir

P = 128
T = 2048
D = 128
NT = T // P
DI = 256
H = 4
HD = DI // H
N = 64
NXBC = DI + 2 * N
NB = NXBC // P
TAPS = 4
GT = 4
G = NT // GT
GW = GT * P
E = 8
CAP = 160
F = 512
FB = F // P
PAIRS = NT // 2
SLOTS = E * CAP
ST = SLOTS // P
SC = NB * (TAPS - 1)
ROW = D + 1
EPS = 1e-5
FAR = 1 << 20

C_LNW, C_LNB, C_CONVW, C_CONVB = 0, 1, 2, 2 + NB * TAPS
C_NORMW = C_CONVB + NB
C_OB1 = C_NORMW + 2
C_B1 = C_OB1 + FB
C_B2 = C_B1 + E * FB
C_DTB = C_B2 + E
C_ALOG = C_DTB + H
C_DSKIP = C_ALOG + H
C_RB = C_DSKIP + H
C_OB2 = C_RB + E
SHEET = C_OB2 + D

F32 = mybir.dt.float32
BF16 = mybir.dt.bfloat16
I32 = mybir.dt.int32
ALU = mybir.AluOpType
ACT = mybir.ActivationFunctionType
AX = mybir.AxisListType


def build(nc, x, sheet, in_w, out_w, router_w, ow1, ow2, w1, w2, out):
    with ExitStack() as ctx:
        def sb(name, shape, dt=F32):
            return ctx.enter_context(nc.sbuf_tensor(name, shape, dt))

        def sem(name):
            return ctx.enter_context(nc.semaphore(name))

        bc_dram = nc.dram_tensor("bc_dram", [P, T], F32, kind="Internal").ap()
        cs_dram = nc.dram_tensor("cs_dram", [NT * H, P], F32, kind="Internal").ap()
        slots_dram = nc.dram_tensor("slots_dram", [SLOTS, ROW], F32, kind="Internal").ap()

        par = sb("par", [P, SHEET])
        win = sb("win", [P, 2 * DI + 2 * N + H])
        wout = sb("wout", [P, 2, D])
        wrt = sb("wrt", [P, E])
        wo1 = sb("wo1", [P, F])
        wo2 = sb("wo2", [P, FB, D])
        w1s = sb("w1s", [P, E, F])
        w2s = sb("w2s", [P, E, FB, D])

        ident = sb("ident", [P, P])
        upto = sb("upto", [P, P])
        after = sb("after", [P, P])
        ones = sb("ones", [P, P])
        upto_h = sb("upto_h", [P, P], BF16)
        ones_h = sb("ones_h", [P, P], BF16)
        mhalf = sb("mhalf", [P, 8])
        eps = sb("eps", [P, 8])
        eps_sum = sb("eps_sum", [P, 1])
        none = sb("none", [P, ST], I32)
        passed = sb("passed", [P, 1])
        pair_step = sb("pair_step", [P, 2], I32)
        first_slot = sb("first_slot", [P, 2 * E])
        prefer = sb("prefer", [P, 2 * E])
        dskip = sb("dskip", [P, DI])

        x_all = sb("x_all", [P, NT, D])
        raw = sb("raw", [P, NB, TAPS - 1 + T])
        sz_all = sb("sz_all", [P, NT, DI])
        xs_all = sb("xs_all", [P, NT, DI + N])
        dt_all = sb("dt_all", [P, NT * H])
        a_all = sb("a_all", [P, NT * H])
        ex_all = sb("ex_all", [P, 3, NT * H])
        w_all = sb("w_all", [P, NT * H])

        st1 = sb("st1", [P, NT, 6])
        mv1 = sb("mv1", [P, NT, 2])
        v1 = sb("v1", [P, 2, NT])
        r1 = sb("r1", [P, 2, NT])
        s1 = sb("s1", [P, NT])
        nm1 = sb("nm1", [P, NT])
        xs1 = sb("xs1", [P, GT, D])
        tap0 = sb("tap0", [P, NB, GW])
        xn = sb("xn", [P, GT, D])
        xnT = sb("xnT", [P, GW])
        acc = sb("acc", [P, NB, GW])
        cv = sb("cv", [P, NB, GW])
        sp = sb("sp", [P, 20, NT * H])
        nA = sb("nA", [P, 2, H])
        cs_all = sb("cs_all", [P, NT * H])
        ncs_all = sb("ncs_all", [P, NT * H])
        csT = sb("csT", [NT * H, P])

        bcT = sb("bcT", [N, 2, 2, P])
        btok = sb("btok", [P, 2, N])
        csb = sb("csb", [P, 2, H * P])
        xdt = sb("xdt", [P, 2, DI])
        xw = sb("xw", [P, 2, DI])
        dxs = sb("dxs", [P, 2, DI])
        decay = sb("decay", [P, 2, H * P])
        cb = sb("cb", [P, 2, P])
        m_t = sb("m_t", [P, 2, H * P])
        state = sb("state", [N, DI])
        sdec = sb("sdec", [N, DI])
        y_off = sb("y_off", [P, DI])
        y_sum = sb("y_sum", [P, DI])
        y_skip = sb("y_skip", [P, 2, DI])
        yg = sb("yg", [P, 2, DI])
        junk = sb("junk", [P, DI])
        ssq = sb("ssq", [P, 2])
        msq = sb("msq", [P, 2])
        rms = sb("rms", [P, 2])
        ygT = sb("ygT", [P, 2, DI])

        st2 = sb("st2", [P, 2, 6])
        mv2 = sb("mv2", [P, 2, 2])
        ve2 = sb("ve2", [P, 2])
        rs2 = sb("rs2", [P, 2])
        rowC = sb("rowC", [P, 2, D])
        rowS = sb("rowS", [P, 2, ROW])
        xfT = sb("xfT", [P, 2 * P])
        lmax = sb("lmax", [P, 2])
        pref = sb("pref", [P, 2 * E])
        pmax = sb("pmax", [P, 2])
        oh = sb("oh", [P, 2 * E], BF16)
        limit = sb("limit", [P, 2])
        before = sb("before", [P, 2 * E], BF16)
        both = sb("both", [P, E], BF16)
        chosen = sb("chosen", [P, 2 * E])
        slotf = sb("slotf", [P, 2])
        sloti = sb("sloti", [P, 2], I32)
        noslot = sb("noslot", [P, 2])
        hT = sb("hT", [P, FB, 2 * P])
        ovb = sb("ovb", [P, 2, D])
        outrow = sb("outrow", [P, 2, D])

        fill = sb("fill", [P, ST, ROW])
        tok = sb("tok", [P, ST], I32)
        hE = sb("hE", [P, 2, FB, CAP])
        bufT = raw[:, 0, 0:SLOTS]
        yT = raw[:, 1, 0:SLOTS]
        yrow = raw[:, 2, 0:SLOTS].rearrange("p (t d) -> p t d", d=D)
        rows = tap0[:, :, :].rearrange("p m t -> p (m t)")[:, 0:ST * ROW].rearrange("p (t r) -> p t r", r=ROW)

        bank = [ctx.enter_context(nc.psum_tensor(f"bank{i}", [P, 512], F32)) for i in range(8)]

        par_in, win_in, wout_in, ffn_in = sem("par_in"), sem("win_in"), sem("wout_in"), sem("ffn_in")
        x_in = [sem(f"x_in{g}") for g in range(G)]
        w_in = [sem(f"w_in{e}") for e in range(E)]
        const0, consts, filled = sem("const0"), sem("consts"), sem("filled")
        zeroed, consts_v = sem("zeroed"), sem("consts_v")
        st1_ready, mv1_ready, v1_ready, r1_ready, s1_ready, xn_ready, xs1_ready, xx_ready, tap0_ready = (
            sem("st1_ready"), sem("mv1_ready"), sem("v1_ready"), sem("r1_ready"), sem("s1_ready"), sem("xn_ready"),
            sem("xs1_ready"), sem("xx_ready"), sem("tap0_ready"))
        xn_turned, xnT_ready, xbc_done, raw_ready = sem("xn_turned"), sem("xnT_ready"), sem("xbc_done"), sem("raw_ready")
        dt_done, dt_read, z_done, z_read = sem("dt_done"), sem("dt_read"), sem("z_done"), sem("z_read")
        tap_done, cv_ready, bc_stored, cv_turned, xs_ready = (
            sem("tap_done"), sem("cv_ready"), sem("bc_stored"), sem("cv_turned"), sem("xs_ready"))
        sp_step, sp_exp, A_exp, a_ready, sums_done, cs_ready, sums_exp, w_ready = (
            sem("sp_step"), sem("sp_exp"), sem("A_exp"), sem("a_ready"), sem("sums_done"), sem("cs_ready"),
            sem("sums_exp"), sem("w_ready"))
        cs_turned, csT_ready, cs_stored = sem("cs_turned"), sem("csT_ready"), sem("cs_stored")
        bc_in = [sem("bc_in0"), sem("bc_in1")]
        csb_in = [sem("csb_in0"), sem("csb_in1")]
        xdt_ready, xw_ready, dxs_ready, sdec_ready = (
            sem("xdt_ready"), sem("xw_ready"), sem("dxs_ready"), sem("sdec_ready"))
        cbst_done, off_done, decay_ready, cb_ready, state_ready, m_ready = (
            sem("cbst_done"), sem("off_done"), sem("decay_ready"), sem("cb_ready"),
            sem("state_ready"), sem("m_ready"))
        diag_done, y_step, yg_ready, ssq_ready, msq_ready, rms_ready = (
            sem("diag_done"), sem("y_step"), sem("yg_ready"), sem("ssq_ready"), sem("msq_ready"), sem("rms_ready"))
        yg_turned, ygT_ready, proj_done, x1_ready = sem("yg_turned"), sem("ygT_ready"), sem("proj_done"), sem("x1_ready")
        st2_ready, mv2_ready, ve2_ready, rs2_ready, xf_ready, xf_turned, xfT_ready = (
            sem("st2_ready"), sem("mv2_ready"), sem("ve2_ready"), sem("rs2_ready"), sem("xf_ready"),
            sem("xf_turned"), sem("xfT_ready"))
        logits_done, route_step, oh_ready, rank_done, rank_step, slot_ready = (
            sem("logits_done"), sem("route_step"), sem("oh_ready"), sem("rank_done"), sem("rank_step"), sem("slot_ready"))
        hid_done, hid_ready, ov_done, ov_read, outrow_ready = (
            sem("hid_done"), sem("hid_ready"), sem("ov_done"), sem("ov_read"), sem("outrow_ready"))
        pm_ready, noslot_ready, passes = sem("pm_ready"), sem("noslot_ready"), sem("passes")
        rowS_ready, limit_ready, before_step = sem("rowS_ready"), sem("limit_ready"), sem("before_step")
        tok_ready, scattered, stored = sem("tok_ready"), sem("scattered"), sem("stored")
        rows_in = [sem("rows_in0"), sem("rows_in1")]
        rows_turned, bufT_ready, toks_ready = sem("rows_turned"), sem("bufT_ready"), sem("toks_ready")
        eh_done, eh_act, eh_dve, ey_done, ey_ready, ey_turned, yrow_ready, added = (
            sem("eh_done"), sem("eh_act"), sem("eh_dve"), sem("ey_done"), sem("ey_ready"), sem("ey_turned"),
            sem("yrow_ready"), sem("added"))

        def col(i, n=1):
            return par[:, i:i + n]

        def heads(ap, n):
            return ap.unsqueeze(2).to_broadcast([ap.shape[0], H, n])

        def by_head(ap, n):
            return ap.rearrange("p (h n) -> p h n", h=H)

        def begun(count):
            return not isinstance(count, int) or count > 0

        block = ctx.enter_context(nc.Block())

        @block.sync
        def _(sp_q):
            x_t = x.rearrange("(t p) d -> p t d", p=P)
            out_t = out.rearrange("(t p) d -> p t d", p=P)
            rows_t = slots_dram.rearrange("(t p) r -> p t r", p=P)
            sp_q.dma_start(x_all[:, 0:GT, :], x_t[:, 0:GT, :]).then_inc(x_in[0], 16)
            sp_q.dma_start(par[:, :], sheet).then_inc(par_in, 16)
            sp_q.dma_start(win[:, :], in_w).then_inc(win_in, 16)
            for g in range(1, G):
                sp_q.dma_start(x_all[:, g * GT:(g + 1) * GT, :], x_t[:, g * GT:(g + 1) * GT, :]).then_inc(x_in[g], 16)
            sp_q.dma_start(wout[:, :, :], out_w).then_inc(wout_in, 16)
            sp_q.dma_start(wrt[:, :], router_w).then_inc(ffn_in, 16)
            sp_q.dma_start(wo1[:, :], ow1).then_inc(ffn_in, 16)
            sp_q.dma_start(wo2[:, :, :], ow2).then_inc(ffn_in, 16)
            sp_q.wait_ge(zeroed, 2)
            sp_q.dma_start(rows_t, fill[:, :, :]).then_inc(filled, 16)

            with sp_q.Fori(0, G - 1) as g:
                sp_q.wait_ge(cv_ready, g * NB + NB)
                sp_q.dma_start(bc_dram[:, bass.ts(g, GW)], cv[:, 2, :]).then_inc(bc_stored, 16)
            sp_q.wait_ge(csT_ready, 1)
            sp_q.dma_start(cs_dram, csT[:, :]).then_inc(cs_stored, 16)
            sp_q.wait_ge(cs_stored, 16)

            def load_sums(c, k):
                sp_q.dma_start(csb[:, k, :], cs_dram[bass.ds(c * H, H), :].rearrange("h l -> (h l)").partition_broadcast(P))\
                    .then_inc(csb_in[k], 16)

            for k in range(2):
                load_sums(k, k)
            sp_q.wait_ge(cv_ready, G * NB)
            sp_q.dma_start(bc_dram[:, (G - 1) * GW:G * GW], cv[:, 2, :]).then_inc(bc_stored, 16)
            sp_q.wait_ge(bc_stored, 16 * G)

            def load_chunk(c, k):
                sp_q.dma_start(bcT[:, k, :, :], bc_dram[:, bass.ts(c, P)].rearrange("(b n) t -> n b t", b=2)).then_inc(bc_in[k], 16)
                sp_q.dma_start(btok[:, k, :], xs_all[:, bass.ds(c, 1), DI:DI + N].rearrange("p a n -> p (a n)")).then_inc(bc_in[k], 16)

            sp_q.wait_ge(xs_ready, NT)
            for k in range(2):
                load_chunk(k, k)
            for e in range(E):
                sp_q.dma_start(w1s[:, e, :], w1[:, e, :]).then_inc(w_in[e], 16)
                sp_q.dma_start(w2s[:, e, :, :], w2[:, e, :, :]).then_inc(w_in[e], 16)

            def ahead(c, k, chunk=True, sums=True):
                if chunk:
                    sp_q.wait_ge(off_done, c + 1)
                    load_chunk(c + 2, k)
                if sums:
                    sp_q.wait_ge(decay_ready, c + 2)
                    load_sums(c + 3, 1 - k)

            def store_pair(q):
                sp_q.wait_ge(outrow_ready, q + 1)
                sp_q.dma_start(out_t[:, bass.ds(2 * q, 2), :], outrow[:, :, :]).then_inc(stored, 16)

            sp_q.wait_ge(decay_ready, 1)
            load_sums(2, 0)

            def pair(i):
                late = isinstance(i, int) and i >= PAIRS - 2
                last = isinstance(i, int) and i >= PAIRS - 1
                for k in range(2):
                    ahead(2 * i + k, k, chunk=not last, sums=not (last or late and k == 1))
                    if k == 0 and begun(i - 2):
                        store_pair(i - 3)

            for i in range(3):
                pair(i)
            with sp_q.Fori(3, PAIRS - 2) as i:
                pair(i)
            for i in range(PAIRS - 2, PAIRS):
                pair(i)
            store_pair(PAIRS - 3)
            store_pair(PAIRS - 2)

            sp_q.wait_ge(scattered, 32 * PAIRS)
            sp_q.wait_ge(filled, 16)
            for half in range(2):
                part = slice(half * ST // 2, (half + 1) * ST // 2)
                sp_q.dma_start(rows[:, part, :], rows_t[:, part, :]).then_inc(rows_in[half], 16)
            store_pair(PAIRS - 1)
            sp_q.wait_ge(stored, 16 * PAIRS)
            sp_q.wait_ge(added, 16 * ST)

        @block.gpsimd
        def _(pool):
            pool.memset(ones[:, :], 1.0).then_inc(const0, 1)
            pool.memset(ident[:, :], 0.0).then_inc(const0, 1)
            pool.memset(ones_h[:, :], 1.0).then_inc(consts, 1)
            pool.memset(mhalf[:, :], -0.5).then_inc(consts, 1)
            pool.wait_ge(const0, 2)
            pool.wait_ge(consts, 2)
            pool.affine_select(out=ident[:, :], in_=ident[:, :], compare_op=ALU.not_equal, fill=1.0, base=0,
                               pattern=[[-1, P]], channel_multiplier=1).then_inc(consts, 1)
            pool.memset(raw[:, :, 0:TAPS - 1], 0.0).then_inc(zeroed, 1)

            def ln1_factors(g):
                t = slice(g * GT, (g + 1) * GT)
                pool.wait_ge(v1_ready, 2 * g + 2)
                pool.tensor_tensor(r1[:, :, t], v1[:, :, t], mhalf[:, :].rearrange("p (a b) -> p a b", a=2), ALU.pow).then_inc(r1_ready, 1)

            def ln1_sums(g):
                t = slice(g * GT, (g + 1) * GT)
                pool.wait_ge(r1_ready, g + 1)
                pool.tensor_tensor(s1[:, t], r1[:, 0, t], ones[:, 0:GT], ALU.add).then_inc(s1_ready, 1)
                pool.tensor_tensor(nm1[:, t], r1[:, 0, t], mv1[:, t, 0], ALU.mult).then_inc(s1_ready, 1)

            ln1_factors(0)
            pool.affine_select(out=upto[:, :], in_=ones[:, :], compare_op=ALU.is_ge, fill=0.0, base=0,
                               pattern=[[1, P]], channel_multiplier=-1).then_inc(consts, 1)
            pool.affine_select(out=after[:, :], in_=ones[:, :], compare_op=ALU.is_gt, fill=0.0, base=0,
                               pattern=[[-1, P]], channel_multiplier=1).then_inc(consts, 1)
            pool.affine_select(out=upto_h[:, :], in_=ones_h[:, :], compare_op=ALU.is_ge, fill=0.0, base=0,
                               pattern=[[1, P]], channel_multiplier=-1).then_inc(consts, 1)
            ln1_factors(1)
            pool.memset(fill[:, :, :], 0.0).then_inc(const0, 1)
            pool.memset(state[:, :], 0.0).then_inc(consts, 1)
            pool.memset(eps[:, :], EPS).then_inc(consts, 1)
            pool.memset(none[:, :], 0).then_inc(consts, 1)
            pool.memset(eps_sum[:, :], EPS * DI).then_inc(consts, 1)
            pool.memset(pair_step[:, :], 2 * P).then_inc(consts, 1)
            pool.iota(first_slot[:, :], pattern=[[0, 2], [CAP, E]], base=0, channel_multiplier=0,
                      allow_small_or_imprecise_dtypes=True).then_inc(consts, 1)
            pool.iota(prefer[:, :], pattern=[[0, 2], [-1, E]], base=E, channel_multiplier=0,
                      allow_small_or_imprecise_dtypes=True).then_inc(consts, 1)
            pool.iota(rowS[:, :, D:ROW].bitcast(I32), pattern=[[P, 2], [1, 1]], base=-2 * P,
                      channel_multiplier=1).then_inc(tok_ready, 1)
            pool.wait_ge(const0, 3)
            pool.memset(fill[:, :, D:ROW].bitcast(I32), FAR).then_inc(zeroed, 1)
            for g in range(2, G):
                ln1_factors(g)
            for g in range(G):
                ln1_sums(g)

            def first_tap(g, first=False):
                for m in range(NB):
                    pool.wait_ge(raw_ready, g * NB + m + 1)
                    if not first:
                        pool.wait_ge(tap_done, (g - 1) * SC + m * (TAPS - 1) + 1)
                    pool.tensor_tensor(tap0[:, m, :], raw[:, m, bass.ds(g * GW, GW)], col(C_CONVW + m * TAPS).to_broadcast([P, GW]),
                                       ALU.mult).then_inc(tap0_ready, 1)

            def add_ln(g):
                xg = x_all[:, bass.ds(g * GT, GT), :]
                pool.wait_ge(xn_ready, g + 1)
                if begun(g):
                    pool.wait_ge(xx_ready, g)
                pool.tensor_tensor(xs1[:, :, :], xg, s1[:, bass.ds(g * GT, GT)].unsqueeze(2).to_broadcast([P, GT, D]), ALU.mult).then_inc(xs1_ready, 1)
                pool.wait_ge(xs1_ready, g + 1)
                pool.tensor_tensor(xg, xs1[:, :, :], nm1[:, bass.ds(g * GT, GT)].unsqueeze(2).to_broadcast([P, GT, D]), ALU.subtract).then_inc(xx_ready, 1)

            pool.wait_ge(par_in, 16)
            pool.wait_ge(s1_ready, 2 * G)
            first_tap(0, first=True)
            add_ln(0)
            with pool.Fori(1, G) as g:
                first_tap(g)
                add_ln(g)
            pool.tensor_copy(by_head(dskip[:, :], HD), heads(col(C_DSKIP, H), HD)).then_inc(consts, 1)

            pool.wait_ge(w_ready, 1)
            pool.wait_ge(xs_ready, NT)
            pool.wait_ge(consts, 14)

            def xs_of(c):
                return xs_all[:, bass.ds(c, 1), 0:DI].rearrange("p a n -> p (a n)")

            def weighted(c, k):
                if begun(c - 1):
                    pool.wait_ge(cbst_done, c - 1)
                pool.tensor_tensor(by_head(xw[:, k, :], HD), by_head(xs_of(c), HD), heads(w_all[:, bass.ds(c * H, H)], HD), ALU.mult).then_inc(xw_ready, 1)

            def inputs(c, k):
                if begun(c - 1):
                    pool.wait_ge(yg_ready, c - 1)
                pool.tensor_tensor(by_head(xdt[:, k, :], HD), by_head(xs_of(c), HD), heads(dt_all[:, bass.ds(c * H, H)], HD), ALU.mult).then_inc(xdt_ready, 1)
                pool.tensor_tensor(dxs[:, k, :], xs_of(c), dskip[:, :], ALU.mult).then_inc(dxs_ready, 1)

            def decay_state(c):
                if begun(c):
                    pool.wait_ge(state_ready, c)
                pool.tensor_tensor(by_head(sdec[:, :], HD), by_head(state[:, :], HD),
                                   heads(ex_all[0:N, 2, bass.ds(c * H, H)], HD), ALU.mult).then_inc(sdec_ready, 1)

            def rms_factor(c, k):
                pool.wait_ge(ssq_ready, c + 1)
                pool.tensor_tensor(msq[:, k:k + 1], ssq[:, k:k + 1], eps_sum[:, :], ALU.add).then_inc(msq_ready, 1)
                pool.wait_ge(msq_ready, c + 1)
                if begun(c - 1):
                    pool.wait_ge(x1_ready, c - 1)
                pool.tensor_tensor(rms[:, k:k + 1], msq[:, k:k + 1], mhalf[:, 0:1], ALU.pow).then_inc(rms_ready, 1)

            def ln2_factor(q):
                pool.wait_ge(mv2_ready, 2 * q + 2)
                pool.tensor_tensor(ve2[:, :], mv2[:, :, 1], eps[:, 0:2], ALU.add).then_inc(ve2_ready, 1)
                pool.wait_ge(ve2_ready, q + 1)
                pool.tensor_tensor(rs2[:, :], ve2[:, :], mhalf[:, 0:2], ALU.pow).then_inc(rs2_ready, 1)

            def pass_waits():
                pool.tensor_tensor(passed[:, :], eps_sum[:, :], eps_sum[:, :], ALU.add).then_inc(passes, 1)

            def scatter(q):
                pool.wait_ge(rowS_ready, q + 1)
                pool.wait_ge(tok_ready, q + 1)
                tok_c = rowS[:, :, D:ROW].bitcast(I32)
                pool.tensor_tensor(tok_c, tok_c, pair_step[:, :].unsqueeze(2), ALU.add).then_inc(tok_ready, 1)
                pool.wait_ge(tok_ready, q + 2)
                pool.wait_ge(slot_ready, q + 1)
                pool.wait_ge(filled, 16)
                pass_waits()
                for j in range(2):
                    pool.indirect_dma_start(slots_dram, bass.IndirectOffsetOnAxis(ap=sloti[:, j:j + 1], axis=0),
                                            rowS[:, j, :], None, bounds_check=SLOTS - 1, oob_is_err=False).then_inc(scattered, 16)

            weighted(0, 0)
            weighted(1, 1)
            inputs(0, 0)
            decay_state(0)
            decay_state(1)

            def pair(i):
                last = isinstance(i, int) and i >= PAIRS - 1
                if begun(i - 2):
                    scatter(i - 3)
                for k in range(2):
                    c = 2 * i + k
                    if begun(c):
                        rms_factor(c - 1, 1 - k)
                    if not last:
                        weighted(c + 2, k)
                    if not (last and k == 1):
                        inputs(c + 1, 1 - k)
                    if not last:
                        decay_state(c + 2)
                    if k == 1 and begun(i):
                        ln2_factor(i - 1)

            for i in range(3):
                pair(i)
            with pool.Fori(3, PAIRS - 1) as i:
                pair(i)
            pair(PAIRS - 1)
            rms_factor(NT - 1, 1)
            scatter(PAIRS - 3)
            ln2_factor(PAIRS - 1)
            scatter(PAIRS - 2)
            scatter(PAIRS - 1)

            for half in range(2):
                pool.wait_ge(rows_in[half], 16)
            pool.tensor_tensor(tok[:, :], rows[:, :, D].bitcast(I32), none[:, :], ALU.add).then_inc(toks_ready, 1)
            pool.wait_ge(toks_ready, 1)
            pool.wait_ge(stored, 16 * PAIRS)
            for t in range(ST):
                pool.wait_ge(yrow_ready, t + 1)
                pool.indirect_dma_start(out, bass.IndirectOffsetOnAxis(ap=tok[:, t:t + 1], axis=0),
                                        yrow[:, t, :], None, bounds_check=T - 1, oob_is_err=False,
                                        compute_op=ALU.add).then_inc(added, 16)

        @block.scalar
        def _(act):
            act.wait_ge(par_in, 16)
            act.activation(nA[:, 0, :], col(C_ALOG, H), ACT.Exp).then_inc(A_exp, 1)

            def turn_xn(g):
                act.wait_ge(xn_turned, g + 1)
                act.activation(xnT[:, :], bank[0][:, :], ACT.Identity, bias=col(C_LNB), scale=col(C_LNW)).then_inc(xnT_ready, 1)

            def take_raw(g):
                for m in range(NB):
                    act.wait_ge(xbc_done, g * NB + m + 1)
                    act.activation(raw[:, m, bass.ds(g * GW + TAPS - 1, GW)], bank[1 + m][:, :], ACT.Copy).then_inc(raw_ready, 1)

            def gate(g):
                for p in range(2):
                    act.wait_ge(z_done, g * 2 + p + 1)
                    act.activation(sz_all[:, bass.ds(g * GT + 2 * p, 2), :].rearrange("p a n -> p (a n)"), bank[4 + p][:, :],
                                   ACT.Silu).then_inc(z_read, 1)

            def silu_conv(g):
                for m in range(NB):
                    if m == 0 and begun(g):
                        act.wait_ge(cv_turned, g * GT)
                        act.wait_ge(bc_stored, 16 * g)
                    act.wait_ge(tap_done, g * SC + (m + 1) * (TAPS - 1))
                    act.activation(cv[:, m, :], acc[:, m, :], ACT.Silu, bias=col(C_CONVB + m)).then_inc(cv_ready, 1)

            def take_xs(g):
                for j in range(GT):
                    act.wait_ge(cv_turned, g * GT + j + 1)
                    act.activation(xs_all[:, bass.ds(g * GT + j, 1), :].rearrange("p a n -> p (a n)"),
                                   bank[6 + j % 2][:, 0:DI + N], ACT.Copy).then_inc(xs_ready, 1)

            def group(g):
                turn_xn(g)
                if begun(g - 1):
                    take_xs(g - 2)
                take_raw(g)
                gate(g)
                if begun(g):
                    silu_conv(g - 1)

            group(0)
            group(1)
            with act.Fori(2, G) as g:
                group(g)
            take_xs(G - 2)

            act.wait_ge(sp_step, 2)
            act.activation(sp[:, 2, :], sp[:, 1, :], ACT.Exp).then_inc(sp_exp, 1)
            act.wait_ge(sums_done, 1)
            act.activation(cs_all[:, :], bank[1][:, 0:NT * H], ACT.Copy).then_inc(cs_ready, 1)
            act.activation(ncs_all[:, :], bank[1][:, 0:NT * H], ACT.Copy, scale=-1.0).then_inc(cs_ready, 1)
            act.activation(ex_all[:, :, :].rearrange("p a n -> p (a n)"), bank[1][:, 0:3 * NT * H], ACT.Exp).then_inc(sums_exp, 1)
            act.wait_ge(cs_turned, 1)
            act.activation(csT[:, :], bank[2][0:NT * H, 0:P], ACT.Copy).then_inc(csT_ready, 1)
            silu_conv(G - 1)
            take_xs(G - 1)

            def chunk_decay(c, k, i):
                act.wait_ge(csb_in[k], 16 * i + 16)
                if begun(c - 1):
                    act.wait_ge(m_ready, c - 1)
                for h in range(H):
                    last = act.activation(decay[:, k, h * P:(h + 1) * P], csb[:, k, h * P:(h + 1) * P], ACT.Exp,
                                          bias=ncs_all[:, bass.ds(c * H + h, 1)])
                last.then_inc(decay_ready, 1)

            def sum_squares(c, k):
                act.wait_ge(yg_ready, c + 1)
                if begun(c - 1):
                    act.wait_ge(msq_ready, c - 1)
                if begun(c):
                    act.wait_ge(ssq_ready, c)
                act.activation(junk[:, :], yg[:, k, :], ACT.Square, accum_out=ssq[:, k:k + 1]).then_inc(ssq_ready, 1)

            def take_ygT(c, k, q=None):
                act.wait_ge(yg_turned, c + 1)
                if q is not None:
                    act.wait_ge(xf_turned, q + 1)
                act.activation(ygT[:, k, :], bank[3][:, 0:DI], ACT.Copy).then_inc(ygT_ready, 1)

            def take_xfT(q):
                act.wait_ge(xf_turned, q + 1)
                if begun(q):
                    act.wait_ge(hid_done, q * FB)
                act.activation(xfT[:, :], bank[3][:, DI:2 * DI], ACT.Copy).then_inc(xfT_ready, 1)

            def keep_rows(q):
                act.wait_ge(xf_ready, 2 * q + 2)
                if begun(q):
                    act.wait_ge(scattered, 32 * q)
                act.activation(rowS[:, :, 0:D], rowC[:, :, :], ACT.Copy).then_inc(rowS_ready, 1)

            def hidden(q, b):
                act.wait_ge(hid_done, q * FB + b + 1)
                if begun(q):
                    act.wait_ge(ov_done, q)
                act.activation(hT[:, b, :], bank[6 + b % 2][:, 0:2 * P], ACT.Relu, bias=col(C_OB1 + b)).then_inc(hid_ready, 1)

            chunk_decay(0, 0, 0)
            chunk_decay(1, 1, 0)

            def pair(i):
                last = isinstance(i, int) and i >= PAIRS - 1
                if begun(i):
                    sum_squares(2 * i - 1, 1)
                if begun(i):
                    take_ygT(2 * i - 1, 1, i - 2 if begun(i - 1) else None)
                if begun(i - 1):
                    take_xfT(i - 2)
                    hidden(i - 2, 0)
                    hidden(i - 2, 1)
                if not last:
                    chunk_decay(2 * i + 2, 0, i + 1)
                sum_squares(2 * i, 0)
                take_ygT(2 * i, 0)
                if begun(i - 1):
                    hidden(i - 2, 2)
                    hidden(i - 2, 3)
                    keep_rows(i - 2)
                if not last:
                    chunk_decay(2 * i + 3, 1, i + 1)

            for i in range(3):
                pair(i)
            with act.Fori(3, PAIRS - 1) as i:
                pair(i)
            pair(PAIRS - 1)
            sum_squares(NT - 1, 1)
            take_ygT(NT - 1, 1, PAIRS - 2)
            take_xfT(PAIRS - 2)
            for b in range(FB):
                hidden(PAIRS - 2, b)
                if b == 1:
                    keep_rows(PAIRS - 2)
            take_xfT(PAIRS - 1)
            for b in range(FB):
                hidden(PAIRS - 1, b)
                if b == 1:
                    keep_rows(PAIRS - 1)

            for t in (3, 7, 9):
                act.wait_ge(rows_turned, t + 1)
                w = (t % 4 + 1) * P
                act.activation(bufT[:, (t + 1) * P - w:(t + 1) * P], bank[(0, 1, 2)[t // 4]][:, 0:w], ACT.Copy).then_inc(bufT_ready, 1)

            def expert_hidden(e):
                act.wait_ge(eh_done, e * 2 + 1)
                if begun(e - 1):
                    act.wait_ge(ey_done, e - 1)
                for b in range(2):
                    act.activation(hE[:, e % 2, b, :], bank[(6, 0)[e % 2]][:, b * CAP:(b + 1) * CAP], ACT.Relu,
                                   bias=col(C_B1 + e * FB + b)).then_inc(eh_act, 1)

            def take_rows(t):
                act.wait_ge(ey_turned, t + 1)
                act.activation(yrow[:, t, :], bank[2 + t % 2][:, 0:P], ACT.Copy).then_inc(yrow_ready, 1)

            expert_hidden(0)
            done = 0
            for e in range(E):
                if e + 1 < E:
                    expert_hidden(e + 1)
                while (done + 1) * P <= (e + 1) * CAP:
                    take_rows(done)
                    done += 1

        @block.tensor
        def _(pe):
            pe.wait_ge(consts, 3)
            pe.wait_ge(win_in, 16)

            def turn_xn(g):
                pe.wait_ge(xn_ready, g + 1)
                if begun(g):
                    pe.wait_ge(dt_read, g)
                for j in range(GT):
                    last = pe.transpose(bank[0][:, j * P:(j + 1) * P], xn[:, j, :], ident[:, :])
                last.then_inc(xn_turned, 1)

            def in_proj(g):
                pe.wait_ge(xnT_ready, g + 1)
                for m in range(NB):
                    if begun(g):
                        pe.wait_ge(raw_ready, (g - 1) * NB + m + 1)
                    pe.matmul(bank[1 + m][:, :], win[:, DI + m * P:DI + (m + 1) * P], xnT[:, :], start=True, stop=True).then_inc(xbc_done, 1)
                for j in range(GT):
                    last = pe.matmul(bank[0][:, j * H:(j + 1) * H], xnT[:, j * P:(j + 1) * P], win[:, DI + NXBC:DI + NXBC + H],
                                     start=True, stop=True)
                last.then_inc(dt_done, 1)
                for p in range(2):
                    if begun(g):
                        pe.wait_ge(z_read, (g - 1) * 2 + p + 1)
                    for j in range(2):
                        last = pe.matmul(bank[4 + p][:, j * DI:(j + 1) * DI], xnT[:, (2 * p + j) * P:(2 * p + j + 1) * P], win[:, 0:DI],
                                         start=True, stop=True)
                    last.then_inc(z_done, 1)

            def turn_cv(g):
                pe.wait_ge(cv_ready, g * NB + NB)
                for j in range(GT):
                    if j >= 2:
                        pe.wait_ge(xs_ready, g * GT + j - 1)
                    to = bank[6 + j % 2]
                    for m in range(2):
                        pe.transpose(to[:, m * P:(m + 1) * P], cv[:, m, j * P:(j + 1) * P], ident[:, :])
                    pe.transpose(to[:, DI:DI + N], cv[0:N, 2, j * P:(j + 1) * P], ident[0:N, 0:N]).then_inc(cv_turned, 1)

            def group(g):
                turn_xn(g)
                if begun(g - 1):
                    turn_cv(g - 2)
                in_proj(g)

            group(0)
            group(1)
            with pe.Fori(2, G) as g:
                group(g)
            turn_cv(G - 2)

            w = NT * H
            pe.wait_ge(a_ready, 1)
            pe.wait_ge(raw_ready, G * NB)
            pe.wait_ge(consts, 13)
            pe.matmul(bank[1][:, 0:w], upto[:, :], a_all[:, :], start=True, stop=True)
            pe.matmul(bank[1][:, w:2 * w], after[:, :], a_all[:, :], start=True, stop=True)
            pe.matmul(bank[1][:, 2 * w:3 * w], ones[:, :], a_all[:, :], start=True, stop=True).then_inc(sums_done, 1)
            pe.wait_ge(cs_ready, 1)
            pe.transpose(bank[2][0:w, 0:P], cs_all[:, :], ident[:, :]).then_inc(cs_turned, 1)
            turn_cv(G - 1)
            pe.wait_ge(sums_exp, 1)
            pe.wait_ge(csT_ready, 1)
            pe.wait_ge(wout_in, 16)
            pe.wait_ge(consts_v, 3)
            pe.wait_ge(ffn_in, 48)

            y_bank = (bank[0], bank[2])

            def front(c, k, i):
                b_t, c_t = bcT[:, k, 0, :], bcT[:, k, 1, :]
                pe.wait_ge(bc_in[k], 32 * i + 32)
                pe.wait_ge(xw_ready, c + 1)
                if begun(c):
                    pe.wait_ge(state_ready, c)
                pe.matmul(bank[1][:, 0:P], b_t, c_t, start=True, stop=True)
                pe.matmul(bank[1][0:N, P:P + DI], btok[:, k, :], xw[:, k, :], start=True, stop=True).then_inc(cbst_done, 1)
                if begun(c - 1):
                    pe.wait_ge(yg_ready, c - 1)
                pe.matmul(y_bank[k][:, 0:DI], c_t, state[:, :], start=True, stop=True).then_inc(off_done, 1)

            def diag(c, k):
                pe.wait_ge(m_ready, c + 1)
                pe.wait_ge(xdt_ready, c + 1)
                for h in range(H):
                    last = pe.matmul(y_bank[k][:, DI + h * HD:DI + (h + 1) * HD], m_t[:, k, h * P:(h + 1) * P],
                                     xdt[:, k, h * HD:(h + 1) * HD], start=True, stop=True)
                last.then_inc(diag_done, 1)

            def turn_yg(c, k):
                pe.wait_ge(yg_ready, c + 1)
                if begun(c):
                    pe.wait_ge(ygT_ready, c)
                for m in range(2):
                    last = pe.transpose(bank[3][:, m * P:(m + 1) * P], yg[:, k, m * P:(m + 1) * P], ident[:, :])
                last.then_inc(yg_turned, 1)

            def project(c, k):
                pe.wait_ge(ygT_ready, c + 1)
                if begun(c):
                    pe.wait_ge(x1_ready, c)
                for m in range(2):
                    last = pe.matmul(bank[4][:, 0:D], ygT[:, k, m * P:(m + 1) * P], wout[:, m, :], start=(m == 0), stop=(m == 1))
                last.then_inc(proj_done, 1)

            def turn_xf(q):
                pe.wait_ge(xf_ready, 2 * q + 2)
                for j in range(2):
                    last = pe.transpose(bank[3][:, DI + j * P:DI + (j + 1) * P], rowC[:, j, :], ident[:, :])
                last.then_inc(xf_turned, 1)

            def router(q):
                pe.wait_ge(xfT_ready, q + 1)
                if begun(q):
                    pe.wait_ge(ov_read, q)
                pe.matmul(bank[5][:, DI:DI + 2 * E], ones[0:1, :], par[0:1, C_RB:C_RB + E].unsqueeze(1).to_broadcast([1, 2, E]), start=True, stop=False)
                for j in range(2):
                    last = pe.matmul(bank[5][:, DI + j * E:DI + (j + 1) * E], xfT[:, j * P:(j + 1) * P], wrt[:, :], start=False, stop=(j == 1))
                last.then_inc(logits_done, 1)

            def hidden(q, b):
                if b >= 2:
                    pe.wait_ge(hid_ready, q * FB + b - 1)
                if b == 0 and begun(q):
                    pe.wait_ge(rank_step, 2 * q - 1)
                pe.matmul(bank[6 + b % 2][:, 0:2 * P], wo1[:, b * P:(b + 1) * P], xfT[:, :], start=True, stop=True).then_inc(hid_done, 1)

            def rank(q):
                place = bank[6][:, 2 * P:2 * P + 2 * E]
                pe.wait_ge(oh_ready, q + 1)
                if begun(q):
                    pe.wait_ge(before_step, 2 * q)
                pe.wait_ge(hid_ready, q * FB + 3)
                pe.matmul(place, upto_h[:, :], oh[:, :], start=True, stop=False)
                pe.matmul(place[:, E:2 * E], ones_h[:, :], oh[:, 0:E], start=False, stop=False)
                pe.matmul(place, ones_h[:, :], before[:, :], start=False, stop=True).then_inc(rank_done, 1)

            def overflow(q):
                pe.wait_ge(hid_ready, q * FB + FB)
                for j in range(2):
                    for b in range(FB):
                        last = pe.matmul(bank[5][:, j * D:(j + 1) * D], hT[:, b, j * P:(j + 1) * P], wo2[:, b, :],
                                         start=(b == 0), stop=(b == FB - 1))
                last.then_inc(ov_done, 1)

            front(0, 0, 0)

            def pair(i):
                last = isinstance(i, int) and i >= PAIRS - 1
                front(2 * i + 1, 1, i)
                if begun(i):
                    turn_yg(2 * i - 1, 1)
                if begun(i - 1):
                    turn_xf(i - 2)
                diag(2 * i, 0)
                if begun(i):
                    project(2 * i - 1, 1)
                if begun(i - 1):
                    router(i - 2)
                    hidden(i - 2, 0)
                    hidden(i - 2, 1)
                if not last:
                    front(2 * i + 2, 0, i + 1)
                turn_yg(2 * i, 0)
                diag(2 * i + 1, 1)
                if begun(i - 1):
                    hidden(i - 2, 2)
                    hidden(i - 2, 3)
                project(2 * i, 0)
                if begun(i - 1):
                    rank(i - 2)
                    overflow(i - 2)

            for i in range(3):
                pair(i)
            with pe.Fori(3, PAIRS - 1) as i:
                pair(i)
            pair(PAIRS - 1)
            turn_yg(NT - 1, 1)
            turn_xf(PAIRS - 2)
            router(PAIRS - 2)
            project(NT - 1, 1)
            for b in range(FB):
                hidden(PAIRS - 2, b)
            rank(PAIRS - 2)
            overflow(PAIRS - 2)
            pe.wait_ge(ygT_ready, NT)
            pe.wait_ge(xfT_ready, PAIRS - 1)
            turn_xf(PAIRS - 1)
            router(PAIRS - 1)
            for b in range(FB):
                hidden(PAIRS - 1, b)
            rank(PAIRS - 1)
            overflow(PAIRS - 1)

            for t in range(ST):
                pe.wait_ge(rows_in[t // (ST // 2)], 16)
                pe.transpose(bank[(0, 1, 2)[t // 4]][:, t % 4 * P:(t % 4 + 1) * P], rows[:, t, 0:D], ident[:, :]).then_inc(rows_turned, 1)

            def expert_hidden(e):
                pe.wait_ge(bufT_ready, 1 if (e + 1) * CAP <= 4 * P else 2 if (e + 1) * CAP <= 8 * P else 3)
                pe.wait_ge(w_in[e], 32)
                if e < 2:
                    pe.wait_ge(bufT_ready, 3)
                else:
                    pe.wait_ge(eh_act, (e - 1) * 2)
                    pe.wait_ge(eh_dve, (e - 1) * 2)
                for half in range(2):
                    for b in range(2):
                        last = pe.matmul(bank[(6, 0)[e % 2] + half][:, b * CAP:(b + 1) * CAP], w1s[:, e, (2 * half + b) * P:(2 * half + b + 1) * P],
                                         bufT[:, e * CAP:(e + 1) * CAP], start=True, stop=True)
                    last.then_inc(eh_done, 1)

            def expert_out(e):
                pe.wait_ge(eh_act, e * 2 + 2)
                pe.wait_ge(eh_dve, e * 2 + 2)
                if e < 2:
                    pe.wait_ge(ov_read, PAIRS)
                else:
                    pe.wait_ge(ey_ready, e - 1)
                for b in range(FB):
                    last = pe.matmul(bank[4 + e % 2][:, 0:CAP], w2s[:, e, b, :], hE[:, e % 2, b, :], start=(b == 0), stop=(b == FB - 1))
                last.then_inc(ey_done, 1)

            def turn_y(t):
                if t >= 2:
                    pe.wait_ge(yrow_ready, t - 1)
                pe.transpose(bank[2 + t % 2][:, 0:P], yT[:, t * P:(t + 1) * P], ident[:, :]).then_inc(ey_turned, 1)

            expert_hidden(0)
            done = 0
            for e in range(E):
                if e + 1 < E:
                    expert_hidden(e + 1)
                if e:
                    pe.wait_ge(ey_ready, e)
                while (done + 1) * P <= e * CAP:
                    turn_y(done)
                    done += 1
                expert_out(e)
            pe.wait_ge(ey_ready, E)
            for t in range(done, ST):
                turn_y(t)

        @block.vector
        def _(dve):
            def tile_of(ap, t):
                return ap[:, bass.ds(t, 1), :].rearrange("p a d -> p (a d)")

            def stats(g):
                dve.wait_ge(x_in[g], 16)
                for t in range(g * GT, (g + 1) * GT):
                    dve.bn_stats(st1[:, t, :], x_all[:, t, :]).then_inc(st1_ready, 1)
                for t in range(g * GT, (g + 1) * GT):
                    dve.wait_ge(st1_ready, t + 1)
                    dve.bn_aggr(mv1[:, t, :], st1[:, t, :]).then_inc(mv1_ready, 1)
                ts = slice(g * GT, (g + 1) * GT)
                dve.wait_ge(mv1_ready, (g + 1) * GT)
                dve.tensor_scalar(v1[:, 0, ts], mv1[:, ts, 1], EPS, None, ALU.add).then_inc(v1_ready, 1)
                dve.tensor_scalar(v1[:, 1, ts], mv1[:, ts, 1], 1.0 + EPS, EPS * EPS, ALU.mult, ALU.add).then_inc(v1_ready, 1)

            def normalise(g):
                dve.wait_ge(r1_ready, g + 1)
                if begun(g):
                    dve.wait_ge(xn_turned, g)
                for j in range(GT):
                    last = dve.tensor_scalar(xn[:, j, :], tile_of(x_all, g * GT + j), mv1[:, bass.ds(g * GT + j, 1), 0:1].rearrange("p a b -> p (a b)"),
                                             r1[:, 1, bass.ds(g * GT + j, 1)], ALU.subtract, ALU.mult)
                last.then_inc(xn_ready, 1)

            def take_dt(g):
                dve.wait_ge(dt_done, g + 1)
                dve.tensor_tensor(dt_all[:, bass.ts(g, GT * H)].rearrange("p (j h) -> p j h", h=H),
                                  bank[0][:, 0:GT * H].rearrange("p (j h) -> p j h", h=H),
                                  col(C_DTB, H).unsqueeze(1).to_broadcast([P, GT, H]), ALU.add).then_inc(dt_read, 1)

            def conv(g, m):
                for k in range(1, TAPS):
                    src = raw[:, m, bass.ds(g * GW + k, GW)]
                    if k == 1:
                        dve.wait_ge(tap0_ready, g * NB + m + 1)
                        if begun(g):
                            dve.wait_ge(cv_ready, (g - 1) * NB + m + 1)
                    else:
                        dve.wait_ge(tap_done, g * SC + m * (TAPS - 1) + k - 1)
                    before = tap0[:, m, :] if k == 1 else acc[:, m, :]
                    dve.scalar_tensor_tensor(out=acc[:, m, :], in0=src, scalar=col(C_CONVW + m * TAPS + k), in1=before,
                                             op0=ALU.mult, op1=ALU.add).then_inc(tap_done, 1)

            dve.wait_ge(par_in, 16)
            dve.wait_ge(zeroed, 1)
            stats(0)
            stats(1)
            normalise(0)
            take_dt(0)
            for g in range(2, G):
                stats(g)
            normalise(1)
            for m in range(NB):
                conv(0, m)
            take_dt(1)
            with dve.Fori(2, G) as g:
                normalise(g)
                for m in range(NB):
                    conv(g - 1, m)
                take_dt(g)

            step = 0

            def after_step(ins):
                nonlocal step
                step += 1
                ins.then_inc(sp_step, 1)

            def row(n):
                return sp[:, n, :]

            dve.wait_ge(dt_read, G)
            after_step(dve.tensor_scalar(row(0), dt_all[:, :], -1.0, None, ALU.mult))
            dve.wait_ge(sp_step, step)
            after_step(dve.tensor_tensor(row(1), row(0), dt_all[:, :], ALU.min))
            conv(G - 1, 0)
            dve.wait_ge(A_exp, 1)
            after_step(dve.tensor_scalar(nA[:, 1, :], nA[:, 0, :], -1.0, None, ALU.mult))
            dve.wait_ge(sp_exp, 1)
            after_step(dve.tensor_scalar(row(3), row(2), 2.0, None, ALU.add))
            dve.wait_ge(sp_step, step)
            after_step(dve.reciprocal(row(4), row(3)))
            dve.wait_ge(sp_step, step)
            after_step(dve.tensor_tensor(row(5), row(2), row(4), ALU.mult))
            dve.wait_ge(sp_step, step)
            after_step(dve.tensor_tensor(row(6), row(5), row(5), ALU.mult))
            dve.wait_ge(sp_step, step)
            after_step(dve.tensor_scalar(row(7), row(6), 1.0 / 15.0, None, ALU.mult))
            for n, odd in enumerate((13, 11, 9, 7, 5, 3)):
                dve.wait_ge(sp_step, step)
                after_step(dve.scalar_tensor_tensor(out=row(8 + n), in0=row(7 + n), scalar=1.0 / odd, in1=row(6), op0=ALU.add, op1=ALU.mult))
            dve.wait_ge(sp_step, step)
            after_step(dve.scalar_tensor_tensor(out=row(14), in0=row(13), scalar=1.0, in1=row(5), op0=ALU.add, op1=ALU.mult))
            after_step(dve.tensor_scalar(row(15), dt_all[:, :], 0.0, None, ALU.max))
            dve.wait_ge(sp_step, step)
            after_step(dve.scalar_tensor_tensor(out=dt_all[:, :], in0=row(14), scalar=2.0, in1=row(15), op0=ALU.mult, op1=ALU.add))
            dve.wait_ge(sp_step, step)
            dve.tensor_tensor(a_all[:, :].rearrange("p (t h) -> p t h", h=H), dt_all[:, :].rearrange("p (t h) -> p t h", h=H),
                              nA[:, 1, :].unsqueeze(1).to_broadcast([P, NT, H]), ALU.mult).then_inc(a_ready, 1)
            for m in range(1, NB):
                conv(G - 1, m)
            dve.wait_ge(sums_exp, 1)
            dve.tensor_tensor(w_all[:, :], ex_all[:, 1, :], dt_all[:, :], ALU.mult).then_inc(w_ready, 1)
            dve.wait_ge(consts, 13)
            dve.tensor_scalar(before[:, :], first_slot[:, :], 1.0 / P, None, ALU.mult).then_inc(consts_v, 1)
            dve.wait_ge(wout_in, 16)
            for m in range(2):
                dve.tensor_scalar(wout[:, m, :], wout[:, m, :], col(C_NORMW + m), float(DI) ** 0.5, ALU.mult, ALU.mult).then_inc(consts_v, 1)

            y_bank = (bank[0], bank[2])

            def scores(c, k):
                dve.wait_ge(cbst_done, c + 1)
                dve.tensor_tensor(cb[:, k, :], bank[1][:, 0:P], upto[:, :], ALU.mult).then_inc(cb_ready, 1)

            def carry_state(c, q=None):
                if q is not None:
                    dve.wait_ge(st2_ready, 2 * q + 2)
                    if begun(q):
                        dve.wait_ge(rs2_ready, q)
                dve.wait_ge(sdec_ready, c + 1)
                dve.wait_ge(off_done, c + 1)
                dve.tensor_tensor(state[:, :], bank[1][0:N, P:P + DI], sdec[:, :], ALU.add).then_inc(state_ready, 1)

            def mix(c, k):
                dve.wait_ge(decay_ready, c + 1)
                dve.wait_ge(cb_ready, c + 1)
                dve.scalar_tensor_tensor(out=by_head(m_t[:, k, :], P), in0=by_head(decay[:, k, :], P), scalar=1.0,
                                         in1=cb[:, k, :].unsqueeze(1).to_broadcast([P, H, P]), op0=ALU.min, op1=ALU.mult).then_inc(m_ready, 1)

            def gated(c, k):
                dve.wait_ge(diag_done, c + 1)
                dve.tensor_tensor(by_head(y_off[:, :], HD), by_head(y_bank[k][:, 0:DI], HD),
                                  heads(ex_all[:, 0, bass.ds(c * H, H)], HD), ALU.mult).then_inc(y_step, 1)
                dve.wait_ge(y_step, 3 * c + 1)
                dve.tensor_tensor(y_sum[:, :], y_bank[k][:, DI:2 * DI], y_off[:, :], ALU.add).then_inc(y_step, 1)
                dve.wait_ge(y_step, 3 * c + 2)
                dve.wait_ge(dxs_ready, c + 1)
                dve.tensor_tensor(y_skip[:, k, :], y_sum[:, :], dxs[:, k, :], ALU.add).then_inc(y_step, 1)
                dve.wait_ge(y_step, 3 * c + 3)
                dve.tensor_tensor(yg[:, k, :], y_skip[:, k, :], tile_of(sz_all, c), ALU.mult).then_inc(yg_ready, 1)

            def residual(c, k):
                dve.wait_ge(rms_ready, c + 1)
                dve.wait_ge(proj_done, c + 1)
                xt = tile_of(x_all, c)
                dve.scalar_tensor_tensor(out=xt, in0=bank[4][:, 0:D], scalar=rms[:, k:k + 1], in1=xt, op0=ALU.mult, op1=ALU.add).then_inc(x1_ready, 1)

            def ln2_stats(q):
                dve.wait_ge(x1_ready, 2 * q + 2)
                for j in range(2):
                    dve.bn_stats(st2[:, j, :], tile_of(x_all, 2 * q + j)).then_inc(st2_ready, 1)

            def ln2_aggregate(q):
                for j in range(2):
                    dve.bn_aggr(mv2[:, j, :], st2[:, j, :]).then_inc(mv2_ready, 1)

            def ln2(q):
                dve.wait_ge(rs2_ready, q + 1)
                if begun(q):
                    dve.wait_ge(xf_turned, q)
                    dve.wait_ge(rowS_ready, q)
                for j in range(2):
                    dve.tensor_scalar(rowC[:, j, :], tile_of(x_all, 2 * q + j), mv2[:, j, 0:1], rs2[:, j:j + 1], ALU.subtract, ALU.mult).then_inc(xf_ready, 1)

            def pairwise(ap):
                return ap.rearrange("p (j e) -> p j e", e=E)

            def choose(q):
                logits = pairwise(bank[5][:, DI:DI + 2 * E])
                dve.wait_ge(logits_done, q + 1)
                dve.tensor_reduce(lmax[:, :], logits, AX.X, ALU.max).then_inc(route_step, 1)
                dve.wait_ge(route_step, 3 * q + 1)
                for j in range(2):
                    dve.scalar_tensor_tensor(out=pref[:, j * E:(j + 1) * E], in0=bank[5][:, DI + j * E:DI + (j + 1) * E], scalar=lmax[:, j:j + 1],
                                             in1=prefer[:, j * E:(j + 1) * E], op0=ALU.is_equal, op1=ALU.mult).then_inc(route_step, 1)
                dve.wait_ge(route_step, 3 * q + 3)
                dve.tensor_reduce(pmax[:, :], pairwise(pref[:, :]), AX.X, ALU.max).then_inc(pm_ready, 1)
                dve.wait_ge(pm_ready, q + 1)
                dve.tensor_tensor(pairwise(oh[:, :]), pairwise(pref[:, :]), pmax[:, :].unsqueeze(2).to_broadcast([P, 2, E]), ALU.is_equal).then_inc(oh_ready, 1)
                dve.tensor_scalar(limit[:, :], pmax[:, :], -float(CAP), CAP * (E + 1) - 0.5, ALU.mult, ALU.add).then_inc(limit_ready, 1)

            def slots(q):
                dve.wait_ge(rank_done, q + 1)
                dve.scalar_tensor_tensor(out=chosen[:, :], in0=bank[6][:, 2 * P:2 * P + 2 * E], scalar=1.0, in1=oh[:, :],
                                         op0=ALU.subtract, op1=ALU.mult).then_inc(rank_step, 1)
                dve.tensor_tensor(both[:, :], oh[:, 0:E], oh[:, E:2 * E], ALU.add).then_inc(before_step, 1)
                dve.wait_ge(rank_step, 2 * q + 1)
                dve.tensor_reduce(slotf[:, :], pairwise(chosen[:, :]), AX.X, ALU.add).then_inc(rank_step, 1)
                dve.wait_ge(before_step, 2 * q + 1)
                dve.tensor_tensor(pairwise(before[:, :]), pairwise(before[:, :]), both[:, :].unsqueeze(1).to_broadcast([P, 2, E]), ALU.add).then_inc(before_step, 1)
                dve.wait_ge(limit_ready, q + 1)
                dve.wait_ge(rank_step, 2 * q + 2)
                dve.tensor_tensor(noslot[:, :], slotf[:, :], limit[:, :], ALU.is_gt).then_inc(noslot_ready, 1)
                if begun(q):
                    dve.wait_ge(scattered, 32 * q)
                dve.wait_ge(noslot_ready, q + 1)
                dve.scalar_tensor_tensor(out=sloti[:, :], in0=noslot[:, :], scalar=float(FAR), in1=slotf[:, :], op0=ALU.mult, op1=ALU.add).then_inc(slot_ready, 1)

            def finish(q):
                dve.wait_ge(ov_done, q + 1)
                dve.tensor_tensor(ovb[:, :, :], bank[5][:, 0:2 * D].rearrange("p (j d) -> p j d", j=2),
                                  col(C_OB2, D).unsqueeze(1).to_broadcast([P, 2, D]), ALU.add).then_inc(ov_read, 1)
                if begun(q):
                    dve.wait_ge(stored, 16 * q)
                dve.wait_ge(noslot_ready, q + 1)
                dve.wait_ge(ov_read, q + 1)
                for j in range(2):
                    last = dve.scalar_tensor_tensor(out=outrow[:, j, :], in0=ovb[:, j, :], scalar=noslot[:, j:j + 1], in1=tile_of(x_all, 2 * q + j),
                                                    op0=ALU.mult, op1=ALU.add)
                last.then_inc(outrow_ready, 1)

            dve.wait_ge(consts, 14)
            dve.wait_ge(xx_ready, G)
            scores(0, 0)
            carry_state(0)
            mix(0, 0)

            def pair(i):
                last = isinstance(i, int) and i >= PAIRS - 1
                scores(2 * i + 1, 1)
                carry_state(2 * i + 1)
                gated(2 * i, 0)
                mix(2 * i + 1, 1)
                if begun(i):
                    residual(2 * i - 1, 1)
                    ln2_stats(i - 1)
                if begun(i - 1):
                    choose(i - 2)
                if last:
                    dve.wait_ge(st2_ready, 2 * (i - 1) + 2)
                    dve.wait_ge(rs2_ready, i - 1)
                    ln2_aggregate(i - 1)
                else:
                    scores(2 * i + 2, 0)
                    carry_state(2 * i + 2, i - 1 if begun(i) else None)
                    if begun(i):
                        ln2_aggregate(i - 1)
                gated(2 * i + 1, 1)
                if not last:
                    mix(2 * i + 2, 0)
                residual(2 * i, 0)
                if begun(i - 1):
                    slots(i - 2)
                if begun(i):
                    ln2(i - 1)
                if begun(i - 1):
                    finish(i - 2)

            for i in range(3):
                pair(i)
            with dve.Fori(3, PAIRS - 1) as i:
                pair(i)
            pair(PAIRS - 1)
            residual(NT - 1, 1)
            q = PAIRS - 1
            ln2_stats(q)
            dve.wait_ge(st2_ready, 2 * q + 2)
            dve.wait_ge(rs2_ready, q)
            ln2_aggregate(q)
            choose(q - 1)
            slots(q - 1)
            ln2(q)
            finish(q - 1)
            choose(q)
            slots(q)
            finish(q)

            def expert_hidden(e):
                dve.wait_ge(eh_done, e * 2 + 2)
                if begun(e - 1):
                    dve.wait_ge(ey_done, e - 1)
                for b in range(2):
                    dve.tensor_scalar(hE[:, e % 2, 2 + b, :], bank[(7, 1)[e % 2]][:, b * CAP:(b + 1) * CAP],
                                      col(C_B1 + e * FB + 2 + b), 0.0, ALU.add, ALU.max).then_inc(eh_dve, 1)

            expert_hidden(0)
            for e in range(E):
                if e + 1 < E:
                    expert_hidden(e + 1)
                dve.wait_ge(ey_done, e + 1)
                dve.tensor_scalar(yT[:, e * CAP:(e + 1) * CAP], bank[4 + e % 2][:, 0:CAP], col(C_B2 + e), None, ALU.add).then_inc(ey_ready, 1)


def kernel(**inputs):
    import numpy as np
    import concourse.bacc as bacc
    from concourse.bass_utils import run_bass_kernel_spmd as run

    v = {k: np.asarray(a) for k, a in inputs.items()}

    def at(name):
        return v["L0_" + name]

    def rows(a):
        return np.broadcast_to(a.reshape(1, -1), (P, a.size))

    sheet = np.concatenate([
        at("attn_ln_w")[:, None], at("attn_ln_b")[:, None],
        at("attn_conv_w").reshape(NB, P, TAPS).transpose(1, 0, 2).reshape(P, NB * TAPS),
        at("attn_conv_b").reshape(NB, P).T, at("attn_norm_w").reshape(2, P).T,
        at("ffn_ob1").reshape(FB, P).T, at("ffn_b1").reshape(E * FB, P).T, at("ffn_b2").T,
        rows(at("attn_dt_bias")), rows(at("attn_A_log")), rows(at("attn_D_skip")), rows(at("ffn_router_b")),
        rows(at("ffn_ob2"))], axis=1)
    arrays = {
        "x": at("attn_x").reshape(T, D), "sheet": sheet, "in_w": at("attn_in_proj_w").T,
        "out_w": at("attn_out_proj_w").T.reshape(2, P, D).transpose(1, 0, 2), "router_w": at("ffn_router_w"),
        "ow1": at("ffn_ow1"), "ow2": at("ffn_ow2").reshape(FB, P, D).transpose(1, 0, 2),
        "w1": at("ffn_w1").transpose(1, 0, 2), "w2": at("ffn_w2").reshape(E, FB, P, D).transpose(2, 0, 1, 3),
    }
    arrays = {k: np.ascontiguousarray(a) for k, a in arrays.items()}
    nc = bacc.Bacc("TRN2", target_bir_lowering=False, num_devices=1)
    args = {k: nc.dram_tensor("in_" + k, a.shape, F32, kind="ExternalInput").ap() for k, a in arrays.items()}
    out = nc.dram_tensor("out_rows", [T, D], F32, kind="ExternalOutput").ap()
    build(nc, out=out, **args)
    r = run(nc, [{"in_" + k: a for k, a in arrays.items()}], core_ids=[0])
    return np.asarray(r.results[0]["out_rows"]).reshape(at("attn_x").shape)
```

```python
from contextlib import ExitStack

import concourse.bass as bass
from concourse import mybir

P = 128
T = 2048
D = 128
NT = T // P
DI = 256
H = 4
HD = DI // H
N = 64
NXBC = DI + 2 * N
NB = NXBC // P
TAPS = 4
GT = 4
G = NT // GT
GW = GT * P
E = 8
CAP = 160
F = 512
FB = F // P
PAIRS = NT // 2
SLOTS = E * CAP
ST = SLOTS // P
SLOT_PARTS = ((0, 2), (2, 6), (6, ST))
TAPS_V = (3, 3, 2)
TAP_COUNT = (0, 3, 6)
SC = sum(TAPS_V)
ROW = D + 1
EPS = 1e-5
FAR = 1 << 20

C_LNW, C_LNB, C_CONVW, C_CONVB = 0, 1, 2, 2 + NB * TAPS
C_NORMW = C_CONVB + NB
C_OB1 = C_NORMW + 2
C_B1 = C_OB1 + FB
C_B2 = C_B1 + E * FB
C_DTB = C_B2 + E
C_ALOG = C_DTB + H
C_DSKIP = C_ALOG + H
C_RB = C_DSKIP + H
C_OB2 = C_RB + E
SHEET = C_OB2 + D

F32 = mybir.dt.float32
BF16 = mybir.dt.bfloat16
I32 = mybir.dt.int32
ALU = mybir.AluOpType
ACT = mybir.ActivationFunctionType
AX = mybir.AxisListType


def build(nc, x, sheet, in_w, out_w, router_w, ow1, ow2, w1, w2, out):
    with ExitStack() as ctx:
        def sb(name, shape, dt=F32):
            return ctx.enter_context(nc.sbuf_tensor(name, shape, dt))

        def sem(name):
            return ctx.enter_context(nc.semaphore(name))

        bc_dram = nc.dram_tensor("bc_dram", [P, T], F32, kind="Internal").ap()
        cs_dram = nc.dram_tensor("cs_dram", [NT * H, P], F32, kind="Internal").ap()
        slots_dram = nc.dram_tensor("slots_dram", [SLOTS, ROW], F32, kind="Internal").ap()

        par = sb("par", [P, SHEET])
        win = sb("win", [P, 2 * DI + 2 * N + H])
        wout = sb("wout", [P, 2, D])
        wrt = sb("wrt", [P, E])
        wo1 = sb("wo1", [P, F])
        wo2 = sb("wo2", [P, FB, D])
        w1s = sb("w1s", [P, E, F])
        w2s = sb("w2s", [P, E, FB, D])

        ident = sb("ident", [P, P])
        upto = sb("upto", [P, P])
        after = sb("after", [P, P])
        ones = sb("ones", [P, P])
        upto_h = sb("upto_h", [P, P], BF16)
        ones_h = sb("ones_h", [P, P], BF16)
        mhalf = sb("mhalf", [P, 8])
        eps = sb("eps", [P, 8])
        eps_sum = sb("eps_sum", [P, 1])
        none = sb("none", [P, ST], I32)
        passed = sb("passed", [P, 1])
        minus = sb("minus", [P, 2])
        pair_step = sb("pair_step", [P, 2], I32)
        first_slot = sb("first_slot", [P, 2 * E])
        prefer = sb("prefer", [P, 2 * E])
        dskip = sb("dskip", [P, DI])

        x_all = sb("x_all", [P, NT, D])
        raw = sb("raw", [P, NB, TAPS - 1 + T])
        sz_all = sb("sz_all", [P, NT, DI])
        xs_all = sb("xs_all", [P, NT, DI + N])
        dt_all = sb("dt_all", [P, NT * H])
        a_all = sb("a_all", [P, NT * H])
        ex_all = sb("ex_all", [P, 3, NT * H])
        w_all = sb("w_all", [P, NT * H])

        st1 = sb("st1", [P, NT, 6])
        mv1 = sb("mv1", [P, NT, 2])
        v1 = sb("v1", [P, 2, NT])
        r1 = sb("r1", [P, 2, NT])
        s1 = sb("s1", [P, NT])
        nm1 = sb("nm1", [P, NT])
        xs1 = sb("xs1", [P, GT, D])
        tap0 = sb("tap0", [P, NB, GW])
        tap1 = sb("tap1", [P, GW])
        xn = sb("xn", [P, 2, GT, D])
        xnT = sb("xnT", [P, T])
        late = sb("late", [P, 2 * H * P + FB * 2 * P])
        acc = (sb("acc", [P, NB, GW]), late[:, 0:NB * GW].rearrange("p (m t) -> p m t", m=NB))
        cv = sb("cv", [P, NB, GW])
        sp = sb("sp", [P, 20, NT * H])
        nA = sb("nA", [P, 2, H])
        sums = sb("sums", [P, 3, NT * H])
        ncs_all = sb("ncs_all", [P, NT * H])
        csT = sb("csT", [NT * H, P])

        bcT = sb("bcT", [N, 2, 2, P])
        btok = sb("btok", [P, 2, N])
        csb = sb("csb", [P, 2, H * P])
        xdt = sb("xdt", [P, 2, DI])
        xw = sb("xw", [P, 2, DI])
        dxs = sb("dxs", [P, 2, DI])
        decay = late[:, 0:2 * H * P].rearrange("p (k n) -> p k n", k=2)
        cb = sb("cb", [P, 2, P])
        m_t = sb("m_t", [P, 2, H * P])
        state = sb("state", [N, DI])
        y_off = sb("y_off", [P, 2, DI])
        y_sum = sb("y_sum", [P, DI])
        y_skip = sb("y_skip", [P, 2, DI])
        yg = sb("yg", [P, 2, DI])
        junk = sb("junk", [P, DI])
        ssq = sb("ssq", [P, 2])
        msq = sb("msq", [P, 2])
        rms = sb("rms", [P, 2])
        ygT = sb("ygT", [P, 2, DI])

        st2 = sb("st2", [P, 2, 6])
        mv2 = sb("mv2", [P, 2, 2])
        ve2 = sb("ve2", [P, 2])
        rs2 = sb("rs2", [P, 2])
        nmean = sb("nmean", [P, 2])
        nm2 = sb("nm2", [P, 2])
        rowC = sb("rowC", [P, 2, D])
        rowS = sb("rowS", [P, 2, ROW])
        xfT = sb("xfT", [P, 2 * P])
        lmax = sb("lmax", [P, 2])
        pref = sb("pref", [P, 2 * E])
        pmax = sb("pmax", [P, 2])
        oh = sb("oh", [P, 2 * E], BF16)
        limit = sb("limit", [P, 2])
        before = sb("before", [P, 2 * E], BF16)
        both = sb("both", [P, E], BF16)
        chosen = sb("chosen", [P, 2 * E])
        slotf = sb("slotf", [P, 2])
        sloti = sb("sloti", [P, 2], I32)
        noslot = sb("noslot", [P, 2])
        hT_last = sb("hT_last", [P, FB, 2 * P])
        outrow_last = y_skip[:, :, 0:D]
        row_last = sb("row_last", [P, 2, ROW])
        slot_last = sb("slot_last", [P, 2], I32)
        noslot_last = sb("noslot_last", [P, 2])
        hT = late[:, 2 * H * P:].rearrange("p (b t) -> p b t", b=FB)
        ovb = sb("ovb", [P, 2, D])
        outrow = sb("outrow", [P, 2, D])

        fill = sb("fill", [P, ST, ROW])
        tok = sb("tok", [P, ST], I32)
        hE = cv[:, :, :].rearrange("p m t -> p (m t)")[:, 0:2 * FB * CAP].rearrange("p (k b c) -> p k b c", k=2, b=FB)
        bufT = raw[:, 0, 0:SLOTS]
        yT = raw[:, 1, 0:SLOTS]
        yrow = raw[:, 2, 0:SLOTS].rearrange("p (t d) -> p t d", d=D)
        rows = tap0[:, :, :].rearrange("p m t -> p (m t)")[:, 0:ST * ROW].rearrange("p (t r) -> p t r", r=ROW)

        bank = [ctx.enter_context(nc.psum_tensor(f"bank{i}", [P, 512], F32)) for i in range(8)]

        par_in, win_in, wout_in, ffn_in = sem("par_in"), sem("win_in"), sem("wout_in"), sem("ffn_in")
        x_in = [sem(f"x_in{g}") for g in range(G)]
        w_in = sem("w_in")
        const0, consts, filled = sem("const0"), sem("consts"), sem("filled")
        zeroed, consts_v = sem("zeroed"), sem("consts_v")
        rx_ready, tap0_step, tap01_ready, ncs_ready = sem("rx_ready"), sem("tap0_step"), sem("tap01_ready"), sem("ncs_ready")
        st1_ready, mv1_ready, v1_ready, r1_ready, s1_ready, xn_ready, xs1_ready, xx_ready, tap0_ready = (
            sem("st1_ready"), sem("mv1_ready"), sem("v1_ready"), sem("r1_ready"), sem("s1_ready"), sem("xn_ready"),
            sem("xs1_ready"), sem("xx_ready"), sem("tap0_ready"))
        xn_turned, xnT_ready, xbc_done, raw_ready = sem("xn_turned"), sem("xnT_ready"), sem("xbc_done"), sem("raw_ready")
        dt_done, dt_read, z_done, z_read = sem("dt_done"), sem("dt_read"), sem("z_done"), sem("z_read")
        tap_done, cv_ready, bc_stored, cv_turned, xs_ready = (
            sem("tap_done"), sem("cv_ready"), sem("bc_stored"), sem("cv_turned"), sem("xs_ready"))
        sp_step, sp_exp, A_exp, a_ready, sums_done, cs_ready, sums_exp, w_ready = (
            sem("sp_step"), sem("sp_exp"), sem("A_exp"), sem("a_ready"), sem("sums_done"), sem("cs_ready"),
            sem("sums_exp"), sem("w_ready"))
        cs_turned, csT_ready, cs_stored = sem("cs_turned"), sem("csT_ready"), sem("cs_stored")
        bc_in = [sem("bc_in0"), sem("bc_in1")]
        csb_in = [sem("csb_in0"), sem("csb_in1")]
        xdt_ready, xw_ready, dxs_ready, sdec_ready = (
            sem("xdt_ready"), sem("xw_ready"), sem("dxs_ready"), sem("sdec_ready"))
        cbst_done, off_done, decay_ready, cb_ready, state_ready, m_ready = (
            sem("cbst_done"), sem("off_done"), sem("decay_ready"), sem("cb_ready"),
            sem("state_ready"), sem("m_ready"))
        diag_done, y_step, yg_ready, ssq_ready, msq_ready, rms_ready = (
            sem("diag_done"), sem("y_step"), sem("yg_ready"), sem("ssq_ready"), sem("msq_ready"), sem("rms_ready"))
        yg_turned, ygT_ready, proj_done, x1_ready = sem("yg_turned"), sem("ygT_ready"), sem("proj_done"), sem("x1_ready")
        st2_ready, mv2_ready, ve2_ready, rs2_ready, xf_ready, xf_turned, xfT_ready = (
            sem("st2_ready"), sem("mv2_ready"), sem("ve2_ready"), sem("rs2_ready"), sem("xf_ready"),
            sem("xf_turned"), sem("xfT_ready"))
        logits_done, route_step, oh_ready, rank_done, rank_step, slot_ready = (
            sem("logits_done"), sem("route_step"), sem("oh_ready"), sem("rank_done"), sem("rank_step"), sem("slot_ready"))
        hid_done, hid_ready, ov_done, ov_read, outrow_ready = (
            sem("hid_done"), sem("hid_ready"), sem("ov_done"), sem("ov_read"), sem("outrow_ready"))
        nm2_ready, off_scaled = sem("nm2_ready"), sem("off_scaled")
        pm_ready, noslot_ready, passes = sem("pm_ready"), sem("noslot_ready"), sem("passes")
        rowS_ready, limit_ready, before_step = sem("rowS_ready"), sem("limit_ready"), sem("before_step")
        tok_ready, scattered, stored = sem("tok_ready"), sem("scattered"), sem("stored")
        rows_in = [sem("rows_in0"), sem("rows_in1"), sem("rows_in2")]
        bufT_in = [sem("bufT_in0"), sem("bufT_in1"), sem("bufT_in2")]
        rows_turned, toks_ready = sem("rows_turned"), sem("toks_ready")
        eh_done, eh_act, eh_dve, ey_done, ey_ready, ey_turned, yrow_ready, added = (
            sem("eh_done"), sem("eh_act"), sem("eh_dve"), sem("ey_done"), sem("ey_ready"), sem("ey_turned"),
            sem("yrow_ready"), sem("added"))

        def col(i, n=1):
            return par[:, i:i + n]

        def heads(ap, n):
            return ap.unsqueeze(2).to_broadcast([ap.shape[0], H, n])

        def by_head(ap, n):
            return ap.rearrange("p (h n) -> p h n", h=H)

        def begun(count):
            return not isinstance(count, int) or count > 0

        block = ctx.enter_context(nc.Block())

        @block.sync
        def _(sp_q):
            x_t = x.rearrange("(t p) d -> p t d", p=P)
            out_t = out.rearrange("(t p) d -> p t d", p=P)
            rows_t = slots_dram.rearrange("(t p) r -> p t r", p=P)
            sp_q.dma_start(x_all[:, 0:GT, :], x_t[:, 0:GT, :]).then_inc(x_in[0], 16)
            sp_q.dma_start(par[:, :], sheet).then_inc(par_in, 16)
            sp_q.dma_start(win[:, :], in_w).then_inc(win_in, 16)
            for g in range(1, G):
                sp_q.dma_start(x_all[:, g * GT:(g + 1) * GT, :], x_t[:, g * GT:(g + 1) * GT, :]).then_inc(x_in[g], 16)
            sp_q.dma_start(wout[:, :, :], out_w).then_inc(wout_in, 16)
            sp_q.dma_start(wrt[:, :], router_w).then_inc(ffn_in, 16)
            sp_q.dma_start(wo1[:, :], ow1).then_inc(ffn_in, 16)
            sp_q.dma_start(wo2[:, :, :], ow2).then_inc(ffn_in, 16)
            sp_q.wait_ge(zeroed, 2)
            sp_q.dma_start(rows_t, fill[:, :, :]).then_inc(filled, 16)

            def store_bc(g):
                sp_q.wait_ge(cv_ready, g * NB + NB)
                sp_q.dma_start(bc_dram[:, g * GW:(g + 1) * GW], cv[:, 2, :]).then_inc(bc_stored, 16)

            def load_sums(c, k):
                sp_q.dma_start(csb[:, k, :], cs_dram[bass.ds(c * H, H), :].rearrange("h l -> (h l)").partition_broadcast(P))\
                    .then_inc(csb_in[k], 16)

            store_bc(0)
            store_bc(1)
            sp_q.wait_ge(csT_ready, 1)
            sp_q.dma_start(cs_dram, csT[:, :]).then_inc(cs_stored, 16)
            sp_q.wait_ge(cs_stored, 16)
            for k in range(2):
                load_sums(k, k)
            def load_chunk(c, k):
                sp_q.dma_start(bcT[:, k, :, :], bc_dram[:, bass.ts(c, P)].rearrange("(b n) t -> n b t", b=2)).then_inc(bc_in[k], 16)
                sp_q.dma_start(btok[:, k, :], xs_all[:, bass.ds(c, 1), DI:DI + N].rearrange("p a n -> p (a n)")).then_inc(bc_in[k], 16)

            store_bc(2)
            sp_q.wait_ge(bc_stored, 32)
            sp_q.wait_ge(xs_ready, GT)
            for k in range(2):
                load_chunk(k, k)
            store_bc(3)

            def ahead(c, k, chunk=True, sums=True):
                if chunk:
                    sp_q.wait_ge(off_done, c + 1)
                    load_chunk(c + 2, k)
                if sums:
                    sp_q.wait_ge(decay_ready, c + 2)
                    load_sums(c + 3, 1 - k)

            def store_pair(q, rows_of=outrow):
                sp_q.wait_ge(outrow_ready, q + 1)
                sp_q.dma_start(out_t[:, bass.ds(2 * q, 2), :], rows_of[:, :, :]).then_inc(stored, 16)

            sp_q.wait_ge(decay_ready, 1)
            load_sums(2, 0)

            def pair(i):
                late = isinstance(i, int) and i >= PAIRS - 2
                last = isinstance(i, int) and i >= PAIRS - 1
                for k in range(2):
                    ahead(2 * i + k, k, chunk=not last, sums=not (last or late and k == 1))
                    if k == 0 and begun(i - 2):
                        store_pair(i - 3)
                sp_q.dma_start(w1s[:, bass.ds(i, 1), :], w1[:, bass.ds(i, 1), :]).then_inc(w_in, 16)
                sp_q.dma_start(w2s[:, bass.ds(i, 1), :, :], w2[:, bass.ds(i, 1), :, :]).then_inc(w_in, 16)

            pair(0)
            sp_q.wait_ge(bc_stored, 16 * G)
            sp_q.wait_ge(xs_ready, NT)
            for i in range(1, 3):
                pair(i)
            with sp_q.Fori(3, PAIRS - 2) as i:
                pair(i)
            for i in range(PAIRS - 2, PAIRS):
                pair(i)
            store_pair(PAIRS - 3)

            sp_q.wait_ge(scattered, 32 * PAIRS)
            sp_q.wait_ge(filled, 16)
            for n in range(3):
                part = slice(4 * n, min(4 * n + 4, ST))
                sp_q.dma_start(rows[:, part, :], rows_t[:, part, :]).then_inc(rows_in[n], 16)
            store_pair(PAIRS - 2)
            store_pair(PAIRS - 1, outrow_last)
            sp_q.wait_ge(stored, 16 * PAIRS)
            sp_q.wait_ge(added, 16 * ST)

        @block.gpsimd
        def _(pool):
            pool.memset(ones[:, :], 1.0).then_inc(const0, 1)
            pool.memset(ident[:, :], 0.0).then_inc(const0, 1)
            pool.memset(ones_h[:, :], 1.0).then_inc(consts, 1)
            pool.memset(mhalf[:, :], -0.5).then_inc(consts, 1)
            pool.wait_ge(const0, 2)
            pool.wait_ge(consts, 2)
            pool.affine_select(out=ident[:, :], in_=ident[:, :], compare_op=ALU.not_equal, fill=1.0, base=0,
                               pattern=[[-1, P]], channel_multiplier=1).then_inc(consts, 1)
            pool.memset(raw[:, :, 0:TAPS - 1], 0.0).then_inc(zeroed, 1)

            def ln1_factor(n, g):
                pool.wait_ge(v1_ready, 2 * g + 2)
                pool.tensor_tensor(r1[:, n, g * GT:(g + 1) * GT], v1[:, n, g * GT:(g + 1) * GT], mhalf[:, 0:GT], ALU.pow)\
                    .then_inc((rx_ready, r1_ready)[n], 1)

            ln1_factor(1, 0)
            ln1_factor(1, 1)
            ln1_factor(1, 2)
            pool.affine_select(out=upto[:, :], in_=ones[:, :], compare_op=ALU.is_ge, fill=0.0, base=0,
                               pattern=[[1, P]], channel_multiplier=-1).then_inc(consts, 1)
            pool.affine_select(out=after[:, :], in_=ones[:, :], compare_op=ALU.is_gt, fill=0.0, base=0,
                               pattern=[[-1, P]], channel_multiplier=1).then_inc(consts, 1)
            pool.affine_select(out=upto_h[:, :], in_=ones_h[:, :], compare_op=ALU.is_ge, fill=0.0, base=0,
                               pattern=[[1, P]], channel_multiplier=-1).then_inc(consts, 1)
            ln1_factor(1, 3)
            pool.memset(state[:, :], 0.0).then_inc(consts, 1)
            pool.memset(eps[:, :], EPS).then_inc(consts, 1)
            pool.memset(none[:, :], 0).then_inc(consts, 1)
            pool.memset(eps_sum[:, :], EPS * DI).then_inc(consts, 1)
            pool.memset(minus[:, :], -1.0).then_inc(consts, 1)
            pool.memset(pair_step[:, :], 2 * P).then_inc(consts, 1)
            pool.iota(first_slot[:, :], pattern=[[0, 2], [CAP, E]], base=0, channel_multiplier=0,
                      allow_small_or_imprecise_dtypes=True).then_inc(consts, 1)
            pool.iota(prefer[:, :], pattern=[[0, 2], [-1, E]], base=E, channel_multiplier=0,
                      allow_small_or_imprecise_dtypes=True).then_inc(consts, 1)
            pool.iota(rowS[:, :, D:ROW].bitcast(I32), pattern=[[P, 2], [1, 1]], base=-2 * P,
                      channel_multiplier=1).then_inc(tok_ready, 1)
            pool.iota(row_last[:, :, D:ROW].bitcast(I32), pattern=[[P, 2], [1, 1]], base=2 * P * (PAIRS - 1),
                      channel_multiplier=1).then_inc(consts, 1)

            def first_taps(g):
                m = NB - 1
                pool.wait_ge(raw_ready, g * NB + m + 1)
                if g:
                    pool.wait_ge(tap_done, (g - 1) * SC + TAP_COUNT[m] + 1)
                pool.tensor_tensor(tap0[:, m, :], raw[:, m, g * GW:(g + 1) * GW], col(C_CONVW + m * TAPS).to_broadcast([P, GW]),
                                   ALU.mult).then_inc(tap0_step, 1)
                pool.tensor_tensor(tap1[:, :], raw[:, m, g * GW + 1:(g + 1) * GW + 1], col(C_CONVW + m * TAPS + 1).to_broadcast([P, GW]),
                                   ALU.mult).then_inc(tap0_step, 1)
                pool.wait_ge(tap0_step, 2 * g + 2)
                pool.tensor_tensor(tap0[:, m, :], tap0[:, m, :], tap1[:, :], ALU.add).then_inc(tap01_ready, 1)

            def add_ln(g):
                t = slice(g * GT, (g + 1) * GT)
                pool.wait_ge(rx_ready, g + 1)
                pool.tensor_tensor(s1[:, t], r1[:, 0, t], ones[:, 0:GT], ALU.add).then_inc(s1_ready, 1)
                pool.tensor_tensor(nm1[:, t], r1[:, 0, t], mv1[:, t, 0], ALU.mult).then_inc(s1_ready, 1)
                pool.wait_ge(xn_ready, g + 1)
                pool.wait_ge(s1_ready, 2 * g + 2)
                if g:
                    pool.wait_ge(xx_ready, g)
                pool.tensor_tensor(xs1[:, :, :], x_all[:, t, :], s1[:, t].unsqueeze(2).to_broadcast([P, GT, D]), ALU.mult).then_inc(xs1_ready, 1)
                pool.wait_ge(xs1_ready, g + 1)
                pool.tensor_tensor(x_all[:, t, :], xs1[:, :, :], nm1[:, t].unsqueeze(2).to_broadcast([P, GT, D]), ALU.subtract).then_inc(xx_ready, 1)

            pool.wait_ge(par_in, 16)
            first_taps(0)
            pool.memset(fill[:, :, :], 0.0).then_inc(const0, 1)
            pool.wait_ge(const0, 3)
            pool.memset(fill[:, :, D:ROW].bitcast(I32), FAR).then_inc(zeroed, 1)
            for g in range(G):
                if g + 1 < G:
                    first_taps(g + 1)
                if g + 1 == G:
                    pool.tensor_copy(by_head(dskip[:, :], HD), heads(col(C_DSKIP, H), HD)).then_inc(consts, 1)
                ln1_factor(0, g)
                if g + 1 < G:
                    add_ln(g)

            pool.wait_ge(w_ready, 1)
            pool.wait_ge(xs_ready, GT)
            pool.wait_ge(consts, 16)

            def xs_of(c):
                return xs_all[:, bass.ds(c, 1), 0:DI].rearrange("p a n -> p (a n)")

            def weighted(c, k):
                if begun(c - 1):
                    pool.wait_ge(cbst_done, c - 1)
                pool.tensor_tensor(by_head(xw[:, k, :], HD), by_head(xs_of(c), HD), heads(w_all[:, bass.ds(c * H, H)], HD), ALU.mult).then_inc(xw_ready, 1)

            def inputs(c, k):
                if begun(c - 1):
                    pool.wait_ge(yg_ready, c - 1)
                pool.tensor_tensor(by_head(xdt[:, k, :], HD), by_head(xs_of(c), HD), heads(dt_all[:, bass.ds(c * H, H)], HD), ALU.mult).then_inc(xdt_ready, 1)
                pool.tensor_tensor(dxs[:, k, :], xs_of(c), dskip[:, :], ALU.mult).then_inc(dxs_ready, 1)

            def rms_factor(c, k):
                pool.wait_ge(ssq_ready, c + 1)
                pool.tensor_tensor(msq[:, k:k + 1], ssq[:, k:k + 1], eps_sum[:, :], ALU.add).then_inc(msq_ready, 1)
                pool.wait_ge(msq_ready, c + 1)
                if begun(c - 1):
                    pool.wait_ge(x1_ready, c - 1)
                pool.tensor_tensor(rms[:, k:k + 1], msq[:, k:k + 1], mhalf[:, 0:1], ALU.pow).then_inc(rms_ready, 1)

            def ln2_factor(q):
                pool.wait_ge(mv2_ready, 2 * q + 2)
                pool.tensor_tensor(ve2[:, :], mv2[:, :, 1], eps[:, 0:2], ALU.add).then_inc(ve2_ready, 1)
                pool.tensor_tensor(nmean[:, :], mv2[:, :, 0], minus[:, :], ALU.mult).then_inc(ve2_ready, 1)
                pool.wait_ge(ve2_ready, 2 * q + 2)
                if begun(q):
                    pool.wait_ge(xf_ready, 2 * q)
                pool.tensor_tensor(rs2[:, :], ve2[:, :], mhalf[:, 0:2], ALU.pow).then_inc(rs2_ready, 1)
                pool.wait_ge(rs2_ready, q + 1)
                pool.tensor_tensor(nm2[:, :], nmean[:, :], rs2[:, :], ALU.mult).then_inc(nm2_ready, 1)

            def pass_waits():
                pool.tensor_tensor(passed[:, :], eps_sum[:, :], eps_sum[:, :], ALU.add).then_inc(passes, 1)

            def scatter(q):
                pool.wait_ge(rowS_ready, q + 1)
                pool.wait_ge(tok_ready, q + 1)
                tok_c = rowS[:, :, D:ROW].bitcast(I32)
                pool.tensor_tensor(tok_c, tok_c, pair_step[:, :].unsqueeze(2), ALU.add).then_inc(tok_ready, 1)
                pool.wait_ge(tok_ready, q + 2)
                pool.wait_ge(slot_ready, q + 1)
                pool.wait_ge(filled, 16)
                pass_waits()
                for j in range(2):
                    pool.indirect_dma_start(slots_dram, bass.IndirectOffsetOnAxis(ap=sloti[:, j:j + 1], axis=0),
                                            rowS[:, j, :], None, bounds_check=SLOTS - 1, oob_is_err=False).then_inc(scattered, 16)

            weighted(0, 0)
            weighted(1, 1)
            inputs(0, 0)

            def pair(i):
                last = isinstance(i, int) and i >= PAIRS - 1
                if begun(i - 2):
                    scatter(i - 3)
                for k in range(2):
                    c = 2 * i + k
                    if k == 1:
                        rms_factor(c - 1, 0)
                    if not last:
                        weighted(c + 2, k)
                    if k == 0 and begun(i):
                        rms_factor(c - 1, 1)
                    if not (last and k == 1):
                        inputs(c + 1, 1 - k)
                    if k == 1 and begun(i):
                        ln2_factor(i - 1)

            add_ln(G - 1)
            pair(0)
            pool.wait_ge(xs_ready, NT)
            for i in range(1, 3):
                pair(i)
            with pool.Fori(3, PAIRS - 1) as i:
                pair(i)
            pair(PAIRS - 1)
            rms_factor(NT - 1, 1)
            scatter(PAIRS - 3)
            ln2_factor(PAIRS - 1)
            scatter(PAIRS - 2)
            pool.wait_ge(xf_ready, 2 * PAIRS)
            pool.wait_ge(slot_ready, PAIRS)
            for j in range(2):
                pool.indirect_dma_start(slots_dram, bass.IndirectOffsetOnAxis(ap=slot_last[:, j:j + 1], axis=0),
                                        row_last[:, j, :], None, bounds_check=SLOTS - 1, oob_is_err=False).then_inc(scattered, 16)

            for n in range(3):
                pool.wait_ge(rows_in[n], 16)
            pool.tensor_tensor(tok[:, :], rows[:, :, D].bitcast(I32), none[:, :], ALU.add).then_inc(toks_ready, 1)
            pool.wait_ge(toks_ready, 1)
            pool.wait_ge(stored, 16 * PAIRS)
            for t in range(ST):
                pool.wait_ge(yrow_ready, t + 1)
                pool.indirect_dma_start(out, bass.IndirectOffsetOnAxis(ap=tok[:, t:t + 1], axis=0),
                                        yrow[:, t, :], None, bounds_check=T - 1, oob_is_err=False,
                                        compute_op=ALU.add).then_inc(added, 16)

        @block.scalar
        def _(act):
            act.wait_ge(par_in, 16)
            act.activation(nA[:, 0, :], col(C_ALOG, H), ACT.Exp).then_inc(A_exp, 1)

            def take_xnT(g):
                act.wait_ge(xn_turned, g + 1)
                act.activation(xnT[:, g * GW:(g + 1) * GW], bank[0][:, :], ACT.Identity, bias=col(C_LNB), scale=col(C_LNW)).then_inc(xnT_ready, 1)

            def take_raw(g, m):
                act.wait_ge(xbc_done, g * NB + m + 1)
                act.activation(raw[:, m, g * GW + TAPS - 1:(g + 1) * GW + TAPS - 1], bank[1 + m][:, :], ACT.Copy).then_inc(raw_ready, 1)

            def first_tap(g, m):
                act.wait_ge(raw_ready, g * NB + m + 1)
                if g:
                    act.wait_ge(tap_done, (g - 1) * SC + TAP_COUNT[m] + 1)
                act.activation(tap0[:, m, :], raw[:, m, g * GW:(g + 1) * GW], ACT.Copy, scale=col(C_CONVW + m * TAPS)).then_inc(tap0_ready, 1)

            def gate(g):
                for p in range(2):
                    act.wait_ge(z_done, g * 2 + p + 1)
                    act.activation(sz_all[:, g * GT + 2 * p:g * GT + 2 * p + 2, :].rearrange("p a n -> p (a n)"), bank[4 + p][:, :],
                                   ACT.Silu).then_inc(z_read, 1)

            def silu_conv(g):
                for m in range(NB):
                    if m == 0 and g:
                        act.wait_ge(cv_turned, g * GT)
                    if m == NB - 1 and g:
                        act.wait_ge(bc_stored, 16 * g)
                    act.wait_ge(tap_done, g * SC + TAP_COUNT[m] + TAPS_V[m])
                    act.activation(cv[:, m, :], acc[g % 2][:, m, :], ACT.Silu, bias=col(C_CONVB + m)).then_inc(cv_ready, 1)

            def take_xs(g):
                for j in range(GT):
                    act.wait_ge(cv_turned, g * GT + j + 1)
                    act.activation(xs_all[:, g * GT + j, :], bank[6 + j % 2][:, 0:DI + N], ACT.Copy).then_inc(xs_ready, 1)

            def take_channels(g):
                for m in range(NB):
                    take_raw(g, m)
                    if m < NB - 1:
                        first_tap(g, m)

            act.wait_ge(zeroed, 1)
            take_xnT(0)
            take_xnT(1)
            take_raw(0, 0)
            take_xnT(2)
            first_tap(0, 0)
            take_raw(0, 1)
            take_xnT(3)
            first_tap(0, 1)
            take_raw(0, 2)
            take_channels(1)
            act.wait_ge(sp_step, 2)
            act.activation(sp[:, 2, :], sp[:, 1, :], ACT.Exp).then_inc(sp_exp, 1)
            silu_conv(0)
            gate(0)
            take_channels(2)
            take_xs(0)
            silu_conv(1)
            gate(1)
            take_raw(3, 0)
            first_tap(3, 0)
            take_raw(3, 1)
            gate(2)
            first_tap(3, 1)
            take_raw(3, 2)
            act.wait_ge(cs_turned, 1)
            act.activation(csT[:, :], bank[0][0:NT * H, 0:P], ACT.Copy).then_inc(csT_ready, 1)
            take_xs(1)
            silu_conv(2)
            gate(3)
            take_xs(2)
            silu_conv(3)
            act.activation(ex_all[:, :, :].rearrange("p a n -> p (a n)"), sums[:, :, :].rearrange("p a n -> p (a n)"), ACT.Exp).then_inc(sums_exp, 1)

            def chunk_decay(c, k, i):
                act.wait_ge(csb_in[k], 16 * i + 16)
                if begun(c - 1):
                    act.wait_ge(m_ready, c - 1)
                for h in range(H):
                    last = act.activation(decay[:, k, h * P:(h + 1) * P], csb[:, k, h * P:(h + 1) * P], ACT.Exp,
                                          bias=ncs_all[:, bass.ds(c * H + h, 1)])
                last.then_inc(decay_ready, 1)

            def scale_off(c, k):
                act.wait_ge(off_done, c + 1)
                for h in range(H):
                    last = act.activation(y_off[:, k, h * HD:(h + 1) * HD], bank[2 * k][:, h * HD:(h + 1) * HD], ACT.Copy,
                                          scale=ex_all[:, 0, bass.ds(c * H + h, 1)])
                last.then_inc(off_scaled, 1)

            def sum_squares(c, k):
                act.wait_ge(yg_ready, c + 1)
                if begun(c - 1):
                    act.wait_ge(msq_ready, c - 1)
                if begun(c):
                    act.wait_ge(ssq_ready, c)
                act.activation(junk[:, :], yg[:, k, :], ACT.Square, accum_out=ssq[:, k:k + 1]).then_inc(ssq_ready, 1)

            def take_ygT(c, k):
                act.wait_ge(yg_turned, c + 1)
                act.activation(ygT[:, k, :], bank[3][:, 0:DI], ACT.Copy).then_inc(ygT_ready, 1)

            def take_xfT(q, at=7):
                act.wait_ge(xf_turned, q + 1)
                if begun(q):
                    act.wait_ge(hid_done, q * FB)
                act.activation(xfT[:, :], bank[at][:, 2 * P:4 * P], ACT.Copy).then_inc(xfT_ready, 1)

            def ln2(q):
                act.wait_ge(nm2_ready, q + 1)
                if begun(q):
                    act.wait_ge(xf_turned, q)
                    act.wait_ge(rowS_ready, q)
                for j in range(2):
                    act.activation(rowC[:, j, :], x_all[:, bass.ds(2 * q + j, 1), :].rearrange("p a d -> p (a d)"), ACT.Identity,
                                   bias=nm2[:, j:j + 1], scale=rs2[:, j:j + 1]).then_inc(xf_ready, 1)

            def keep_rows(q):
                act.wait_ge(xf_ready, 2 * q + 2)
                if begun(q):
                    act.wait_ge(scattered, 32 * q)
                act.activation(rowS[:, :, 0:D], rowC[:, :, :], ACT.Copy).then_inc(rowS_ready, 1)

            def hidden(q, b):
                act.wait_ge(hid_done, q * FB + b + 1)
                if begun(q):
                    act.wait_ge(ov_done, q)
                act.activation(hT[:, b, :], bank[6 + b % 2][:, 0:2 * P], ACT.Relu, bias=col(C_OB1 + b)).then_inc(hid_ready, 1)

            def hidden_last(b):
                act.wait_ge(hid_done, (PAIRS - 1) * FB + b + 1)
                act.activation(hT_last[:, b, :], bank[7 - b % 2][:, 0:2 * P], ACT.Relu, bias=col(C_OB1 + b)).then_inc(hid_ready, 1)

            act.wait_ge(ncs_ready, 1)
            act.wait_ge(cv_ready, G * NB)
            chunk_decay(0, 0, 0)
            chunk_decay(1, 1, 0)
            scale_off(0, 0)

            def pair(i):
                last = isinstance(i, int) and i >= PAIRS - 1
                if begun(i):
                    take_ygT(2 * i - 1, 1)
                    sum_squares(2 * i - 1, 1)
                if begun(i - 1):
                    take_xfT(i - 2)
                scale_off(2 * i + 1, 1)
                if begun(i - 1):
                    hidden(i - 2, 0)
                    hidden(i - 2, 1)
                if not last:
                    chunk_decay(2 * i + 2, 0, i + 1)
                sum_squares(2 * i, 0)
                take_ygT(2 * i, 0)
                if begun(i - 1):
                    hidden(i - 2, 2)
                    hidden(i - 2, 3)
                if not last:
                    scale_off(2 * i + 2, 0)
                if begun(i - 1):
                    keep_rows(i - 2)
                if not last:
                    chunk_decay(2 * i + 3, 1, i + 1)
                if begun(i):
                    ln2(i - 1)

            for i in range(3):
                pair(i)
            with act.Fori(3, PAIRS - 1) as i:
                pair(i)
            pair(PAIRS - 1)
            sum_squares(NT - 1, 1)
            take_ygT(NT - 1, 1)
            take_xfT(PAIRS - 2)
            for b in range(FB - 1):
                hidden(PAIRS - 2, b)
            act.wait_ge(nm2_ready, PAIRS)
            for j in range(2):
                act.activation(row_last[:, j, 0:D], x_all[:, 2 * (PAIRS - 1) + j, :], ACT.Identity,
                               bias=nm2[:, j:j + 1], scale=rs2[:, j:j + 1]).then_inc(xf_ready, 1)
            keep_rows(PAIRS - 2)
            hidden(PAIRS - 2, FB - 1)
            take_xfT(PAIRS - 1, 3)
            for b in range(FB):
                hidden_last(b)

            def take_slots(n):
                first, end = SLOT_PARTS[n]
                act.wait_ge(rows_turned, end)
                act.activation(bufT[:, first * P:end * P], bank[n][:, 0:(end - first) * P], ACT.Copy).then_inc(bufT_in[n], 1)

            def expert_hidden(e):
                act.wait_ge(eh_done, e * 2 + 1)
                if begun(e - 1):
                    act.wait_ge(ey_done, e - 1)
                for b in range(2):
                    act.activation(hE[:, e % 2, b, :], bank[(6, 0)[e % 2]][:, b * CAP:(b + 1) * CAP], ACT.Relu,
                                   bias=col(C_B1 + e * FB + b)).then_inc(eh_act, 1)

            def take_rows(t):
                act.wait_ge(ey_turned, t + 1)
                act.activation(yrow[:, t, :], bank[2 + t % 2][:, 0:P], ACT.Copy).then_inc(yrow_ready, 1)

            take_slots(0)
            expert_hidden(0)
            done = 0
            for e in range(E):
                if e + 1 < E:
                    expert_hidden(e + 1)
                if e == 0:
                    take_slots(2)
                while (done + 1) * P <= (e + 1) * CAP:
                    take_rows(done)
                    done += 1

        @block.tensor
        def _(pe):
            pe.wait_ge(consts, 3)
            pe.wait_ge(win_in, 16)

            def turn_xn(g):
                pe.wait_ge(xn_ready, g + 1)
                if g:
                    pe.wait_ge(xnT_ready, g)
                for j in range(GT):
                    last = pe.transpose(bank[0][:, j * P:(j + 1) * P], xn[:, g % 2, j, :], ident[:, :])
                last.then_inc(xn_turned, 1)

            def dt_proj(g):
                pe.wait_ge(xnT_ready, g + 1)
                for t in range(g * GT, (g + 1) * GT):
                    last = pe.matmul(bank[7][:, 384 + t * H:384 + (t + 1) * H], xnT[:, t * P:(t + 1) * P], win[:, DI + NXBC:DI + NXBC + H],
                                     start=True, stop=True)
                last.then_inc(dt_done, 1)

            def xbc_proj(g, m):
                pe.wait_ge(xnT_ready, g + 1)
                if g:
                    pe.wait_ge(raw_ready, (g - 1) * NB + m + 1)
                pe.matmul(bank[1 + m][:, :], win[:, DI + m * P:DI + (m + 1) * P], xnT[:, g * GW:(g + 1) * GW], start=True, stop=True).then_inc(xbc_done, 1)

            def z_proj(g):
                for p in range(2):
                    if g:
                        pe.wait_ge(z_read, (g - 1) * 2 + p + 1)
                    for j in range(2):
                        t = g * GT + 2 * p + j
                        last = pe.matmul(bank[4 + p][:, j * DI:(j + 1) * DI], xnT[:, t * P:(t + 1) * P], win[:, 0:DI], start=True, stop=True)
                    last.then_inc(z_done, 1)

            def turn_cv(g):
                pe.wait_ge(cv_ready, g * NB + NB)
                for j in range(GT):
                    t = g * GT + j
                    if t >= 2:
                        pe.wait_ge(xs_ready, t - 1)
                    to = bank[6 + j % 2]
                    for m in range(2):
                        pe.transpose(to[:, m * P:(m + 1) * P], cv[:, m, j * P:(j + 1) * P], ident[:, :])
                    pe.transpose(to[:, DI:DI + N], cv[0:N, 2, j * P:(j + 1) * P], ident[0:N, 0:N]).then_inc(cv_turned, 1)

            turn_xn(0)
            turn_xn(1)
            xbc_proj(0, 0)
            turn_xn(2)
            xbc_proj(0, 1)
            turn_xn(3)
            xbc_proj(0, 2)
            for g in range(G):
                dt_proj(g)
            for m in range(NB):
                xbc_proj(1, m)
            z_proj(0)
            for m in range(NB):
                xbc_proj(2, m)
            pe.wait_ge(dt_read, 1)
            turn_cv(0)
            z_proj(1)
            w = NT * H
            pe.wait_ge(a_ready, 1)
            pe.wait_ge(consts, 6)
            pe.matmul(bank[0][:, 0:w], upto[:, :], a_all[:, :], start=True, stop=True)
            pe.matmul(bank[0][:, w:2 * w], after[:, :], a_all[:, :], start=True, stop=True)
            pe.matmul(bank[0][:, 2 * w:3 * w], ones[:, :], a_all[:, :], start=True, stop=True).then_inc(sums_done, 1)
            for m in range(NB):
                xbc_proj(3, m)
            z_proj(2)
            pe.wait_ge(cs_ready, 1)
            pe.transpose(bank[0][0:w, 0:P], sums[:, 0, :], ident[:, :]).then_inc(cs_turned, 1)
            turn_cv(1)
            z_proj(3)
            turn_cv(2)
            turn_cv(3)
            pe.wait_ge(consts, 15)
            pe.wait_ge(csT_ready, 1)
            pe.wait_ge(wout_in, 16)
            pe.wait_ge(consts_v, 3)
            pe.wait_ge(ffn_in, 48)

            y_bank = (bank[0], bank[2])

            def front(c, k, i):
                b_t, c_t = bcT[:, k, 0, :], bcT[:, k, 1, :]
                pe.wait_ge(bc_in[k], 32 * i + 32)
                pe.wait_ge(xw_ready, c + 1)
                if begun(c):
                    pe.wait_ge(state_ready, c)
                pe.matmul(bank[1][:, 0:P], b_t, c_t, start=True, stop=True)
                pe.matmul(bank[1][0:N, P:P + DI], btok[:, k, :], xw[:, k, :], start=True, stop=True).then_inc(cbst_done, 1)
                if begun(c - 1):
                    pe.wait_ge(y_step, 2 * c - 3)
                pe.matmul(y_bank[k][:, 0:DI], c_t, state[:, :], start=True, stop=True).then_inc(off_done, 1)

            def diag(c, k):
                pe.wait_ge(m_ready, c + 1)
                pe.wait_ge(xdt_ready, c + 1)
                pe.wait_ge(off_scaled, c + 1)
                for h in range(H):
                    last = pe.matmul(y_bank[k][:, DI + h * HD:DI + (h + 1) * HD], m_t[:, k, h * P:(h + 1) * P],
                                     xdt[:, k, h * HD:(h + 1) * HD], start=True, stop=True)
                last.then_inc(diag_done, 1)

            def turn_yg(c, k):
                pe.wait_ge(yg_ready, c + 1)
                if begun(c):
                    pe.wait_ge(ygT_ready, c)
                for m in range(2):
                    last = pe.transpose(bank[3][:, m * P:(m + 1) * P], yg[:, k, m * P:(m + 1) * P], ident[:, :])
                last.then_inc(yg_turned, 1)

            def project(c, k):
                pe.wait_ge(ygT_ready, c + 1)
                if begun(c):
                    pe.wait_ge(x1_ready, c)
                for m in range(2):
                    last = pe.matmul(bank[4][:, 0:D], ygT[:, k, m * P:(m + 1) * P], wout[:, m, :], start=(m == 0), stop=(m == 1))
                last.then_inc(proj_done, 1)

            def turn_xf(q, kept=rowC, at=7):
                pe.wait_ge(xf_ready, 2 * q + 2)
                for j in range(2):
                    last = pe.transpose(bank[at][:, (2 + j) * P:(3 + j) * P], kept[:, j, 0:D], ident[:, :])
                last.then_inc(xf_turned, 1)

            def router(q, at=5):
                if at == 5 and begun(q):
                    pe.wait_ge(ov_read, q)
                pe.matmul(bank[at][:, DI:DI + 2 * E], ones[0:1, :], par[0:1, C_RB:C_RB + E].unsqueeze(1).to_broadcast([1, 2, E]), start=True, stop=False)
                pe.wait_ge(xfT_ready, q + 1)
                for j in range(2):
                    last = pe.matmul(bank[at][:, DI + j * E:DI + (j + 1) * E], xfT[:, j * P:(j + 1) * P], wrt[:, :], start=False, stop=(j == 1))
                last.then_inc(logits_done, 1)

            def hidden(q, b):
                if b >= 2:
                    pe.wait_ge(hid_ready, q * FB + b - 1)
                if b == 0 and begun(q):
                    pe.wait_ge(rank_step, 2 * q - 1)
                pe.matmul(bank[6 + b % 2][:, 0:2 * P], wo1[:, b * P:(b + 1) * P], xfT[:, :], start=True, stop=True).then_inc(hid_done, 1)

            def hidden_last(b):
                if b != 1:
                    pe.wait_ge(hid_ready, (PAIRS - 1) * FB + (b - 1 if b else 0))
                else:
                    pe.wait_ge(rank_step, 2 * PAIRS - 1)
                pe.matmul(bank[7 - b % 2][:, 0:2 * P], wo1[:, b * P:(b + 1) * P], xfT[:, :], start=True, stop=True).then_inc(hid_done, 1)

            def rank(q, blocks=FB - 1):
                place = bank[6][:, 2 * P:2 * P + 2 * E]
                pe.wait_ge(oh_ready, q + 1)
                if begun(q):
                    pe.wait_ge(before_step, 2 * q)
                pe.wait_ge(hid_ready, q * FB + blocks)
                pe.matmul(place, upto_h[:, :], oh[:, :], start=True, stop=False)
                pe.matmul(place[:, E:2 * E], ones_h[:, :], oh[:, 0:E], start=False, stop=False)
                pe.matmul(place, ones_h[:, :], before[:, :], start=False, stop=True).then_inc(rank_done, 1)

            def overflow_tile(q, j, to, h):
                for b in range(FB):
                    if j == 0 and b >= FB - 2:
                        pe.wait_ge(hid_ready, q * FB + b + 1)
                    last = pe.matmul(to[:, j * D:(j + 1) * D], h[:, b, j * P:(j + 1) * P], wo2[:, b, :], start=(b == 0), stop=(b == FB - 1))
                return last

            def overflow(q, to=bank[5], h=hT):
                overflow_tile(q, 0, to, h)
                overflow_tile(q, 1, to, h).then_inc(ov_done, 1)

            front(0, 0, 0)

            def pair(i):
                last = isinstance(i, int) and i >= PAIRS - 1
                front(2 * i + 1, 1, i)
                if begun(i):
                    turn_yg(2 * i - 1, 1)
                diag(2 * i, 0)
                if begun(i - 1):
                    turn_xf(i - 2)
                if begun(i):
                    project(2 * i - 1, 1)
                if begun(i - 1):
                    router(i - 2)
                    hidden(i - 2, 0)
                    hidden(i - 2, 1)
                if not last:
                    front(2 * i + 2, 0, i + 1)
                turn_yg(2 * i, 0)
                diag(2 * i + 1, 1)
                if begun(i - 1):
                    hidden(i - 2, 2)
                    hidden(i - 2, 3)
                project(2 * i, 0)
                if begun(i - 1):
                    rank(i - 2)
                    overflow(i - 2)

            for i in range(3):
                pair(i)
            with pe.Fori(3, PAIRS - 1) as i:
                pair(i)
            pair(PAIRS - 1)
            turn_yg(NT - 1, 1)
            turn_xf(PAIRS - 2)
            project(NT - 1, 1)
            router(PAIRS - 2)
            for b in range(FB):
                hidden(PAIRS - 2, b)
            rank(PAIRS - 2)
            turn_xf(PAIRS - 1, row_last, 3)
            router(PAIRS - 1, 1)
            hidden_last(0)
            rank(PAIRS - 1, 0)
            pe.wait_ge(ov_read, PAIRS - 2)
            overflow_tile(PAIRS - 2, 0, bank[5], hT)
            for b in range(1, FB):
                hidden_last(b)
            overflow_tile(PAIRS - 2, 1, bank[5], hT).then_inc(ov_done, 1)
            pe.wait_ge(hid_ready, PAIRS * FB - 2)
            overflow(PAIRS - 1, bank[4], hT_last)

            def turn_rows(t):
                n = next(n for n, (first, end) in enumerate(SLOT_PARTS) if t < end)
                at = t - SLOT_PARTS[n][0]
                pe.wait_ge(rows_in[t // 4], 16)
                pe.transpose(bank[n][:, at * P:(at + 1) * P], rows[:, t, 0:D], ident[:, :]).then_inc(rows_turned, 1)

            def expert_hidden(e):
                for n, (first, end) in enumerate(SLOT_PARTS):
                    if first * P < (e + 1) * CAP:
                        pe.wait_ge(bufT_in[n], 1)
                pe.wait_ge(w_in, 32 * E)
                if e >= 2:
                    pe.wait_ge(eh_act, (e - 1) * 2)
                    pe.wait_ge(eh_dve, (e - 1) * 2)
                for half in range(2):
                    for b in range(2):
                        last = pe.matmul(bank[(6, 0)[e % 2] + half][:, b * CAP:(b + 1) * CAP], w1s[:, e, (2 * half + b) * P:(2 * half + b + 1) * P],
                                         bufT[:, e * CAP:(e + 1) * CAP], start=True, stop=True)
                    last.then_inc(eh_done, 1)

            def expert_out(e):
                pe.wait_ge(eh_act, e * 2 + 2)
                pe.wait_ge(eh_dve, e * 2 + 2)
                if e < 2:
                    pe.wait_ge(ov_read, PAIRS)
                else:
                    pe.wait_ge(ey_ready, e - 1)
                for b in range(FB):
                    last = pe.matmul(bank[4 + e % 2][:, 0:CAP], w2s[:, e, b, :], hE[:, e % 2, b, :], start=(b == 0), stop=(b == FB - 1))
                last.then_inc(ey_done, 1)

            def turn_y(t):
                if t >= 2:
                    pe.wait_ge(yrow_ready, t - 1)
                else:
                    pe.wait_ge(bufT_in[2], 1)
                pe.transpose(bank[2 + t % 2][:, 0:P], yT[:, t * P:(t + 1) * P], ident[:, :]).then_inc(ey_turned, 1)

            for t in range(SLOT_PARTS[2][0]):
                turn_rows(t)
            expert_hidden(0)
            done = 0
            for e in range(E):
                if e + 1 < E:
                    expert_hidden(e + 1)
                if e == 0:
                    for t in range(*SLOT_PARTS[2]):
                        turn_rows(t)
                if e:
                    pe.wait_ge(ey_ready, e)
                while (done + 1) * P <= e * CAP:
                    turn_y(done)
                    done += 1
                expert_out(e)
            pe.wait_ge(ey_ready, E)
            for t in range(done, ST):
                turn_y(t)

        @block.vector
        def _(dve):
            def tile_of(ap, t):
                return ap[:, bass.ds(t, 1), :].rearrange("p a d -> p (a d)")

            def stats(g):
                dve.wait_ge(x_in[g], 16)
                for t in range(g * GT, (g + 1) * GT):
                    dve.bn_stats(st1[:, t, :], x_all[:, t, :]).then_inc(st1_ready, 1)
                for t in range(g * GT, (g + 1) * GT):
                    dve.wait_ge(st1_ready, t + 1)
                    dve.bn_aggr(mv1[:, t, :], st1[:, t, :]).then_inc(mv1_ready, 1)
                ts = slice(g * GT, (g + 1) * GT)
                dve.wait_ge(mv1_ready, (g + 1) * GT)
                dve.tensor_scalar(v1[:, 0, ts], mv1[:, ts, 1], EPS, None, ALU.add).then_inc(v1_ready, 1)
                dve.tensor_scalar(v1[:, 1, ts], mv1[:, ts, 1], 1.0 + EPS, EPS * EPS, ALU.mult, ALU.add).then_inc(v1_ready, 1)

            def normalise(g):
                dve.wait_ge(r1_ready, g + 1)
                if g >= 2:
                    dve.wait_ge(xn_turned, g - 1)
                for j in range(GT):
                    t = g * GT + j
                    last = dve.tensor_scalar(xn[:, g % 2, j, :], x_all[:, t, :], mv1[:, t, 0:1], r1[:, 1, t:t + 1], ALU.subtract, ALU.mult)
                last.then_inc(xn_ready, 1)

            def tap(g, m, k):
                first = TAPS - TAPS_V[m]
                if k == first:
                    if m < NB - 1:
                        dve.wait_ge(tap0_ready, g * (NB - 1) + m + 1)
                    else:
                        dve.wait_ge(tap01_ready, g + 1)
                    if g >= 2:
                        dve.wait_ge(cv_ready, (g - 2) * NB + m + 1)
                else:
                    dve.wait_ge(tap_done, g * SC + TAP_COUNT[m] + k - first)
                to = acc[g % 2][:, m, :]
                before = tap0[:, m, :] if k == first else to
                dve.scalar_tensor_tensor(out=to, in0=raw[:, m, g * GW + k:(g + 1) * GW + k], scalar=col(C_CONVW + m * TAPS + k), in1=before,
                                         op0=ALU.mult, op1=ALU.add).then_inc(tap_done, 1)

            dve.wait_ge(par_in, 16)
            stats(0)
            stats(1)
            normalise(0)
            stats(2)
            normalise(1)
            stats(3)
            normalise(2)
            normalise(3)
            step = 0

            def after_step(ins):
                nonlocal step
                step += 1
                ins.then_inc(sp_step, 1)

            def row(n):
                return sp[:, n, :]

            for k in range(1, TAPS):
                tap(0, 0, k)
            tap(0, 1, 1)
            dve.wait_ge(dt_done, G)
            dve.tensor_tensor(dt_all[:, :].rearrange("p (t h) -> p t h", h=H), bank[7][:, 384:384 + NT * H].rearrange("p (t h) -> p t h", h=H),
                              col(C_DTB, H).unsqueeze(1).to_broadcast([P, NT, H]), ALU.add).then_inc(dt_read, 1)
            dve.wait_ge(dt_read, 1)
            after_step(dve.tensor_scalar(row(0), dt_all[:, :], -1.0, None, ALU.mult))
            dve.wait_ge(sp_step, step)
            after_step(dve.tensor_tensor(row(1), row(0), dt_all[:, :], ALU.min))
            tap(0, 1, 2)
            dve.wait_ge(A_exp, 1)
            after_step(dve.tensor_scalar(nA[:, 1, :], nA[:, 0, :], -1.0, None, ALU.mult))
            tap(0, 1, 3)
            tap(0, 2, 2)
            dve.wait_ge(sp_exp, 1)
            after_step(dve.tensor_scalar(row(3), row(2), 2.0, None, ALU.add))
            tap(0, 2, 3)
            dve.wait_ge(sp_step, step)
            after_step(dve.reciprocal(row(4), row(3)))
            tap(1, 0, 1)
            dve.wait_ge(sp_step, step)
            after_step(dve.tensor_tensor(row(5), row(2), row(4), ALU.mult))
            tap(1, 0, 2)
            dve.wait_ge(sp_step, step)
            after_step(dve.tensor_tensor(row(6), row(5), row(5), ALU.mult))
            tap(1, 0, 3)
            dve.wait_ge(sp_step, step)
            after_step(dve.tensor_scalar(row(7), row(6), 1.0 / 15.0, None, ALU.mult))
            for n, (odd, (m, k)) in enumerate(zip((13, 11, 9, 7, 5, 3), ((1, 1), (1, 2), (1, 3), (2, 2), (2, 3), (None, None)))):
                dve.wait_ge(sp_step, step)
                after_step(dve.scalar_tensor_tensor(out=row(8 + n), in0=row(7 + n), scalar=1.0 / odd, in1=row(6), op0=ALU.add, op1=ALU.mult))
                if m is not None:
                    tap(1, m, k)
            dve.wait_ge(sp_step, step)
            after_step(dve.scalar_tensor_tensor(out=row(14), in0=row(13), scalar=1.0, in1=row(5), op0=ALU.add, op1=ALU.mult))
            after_step(dve.tensor_scalar(row(15), dt_all[:, :], 0.0, None, ALU.max))
            dve.wait_ge(sp_step, step)
            after_step(dve.scalar_tensor_tensor(out=dt_all[:, :], in0=row(14), scalar=2.0, in1=row(15), op0=ALU.mult, op1=ALU.add))
            dve.wait_ge(sp_step, step)
            dve.tensor_tensor(a_all[:, :].rearrange("p (t h) -> p t h", h=H), dt_all[:, :].rearrange("p (t h) -> p t h", h=H),
                              nA[:, 1, :].unsqueeze(1).to_broadcast([P, NT, H]), ALU.mult).then_inc(a_ready, 1)
            for k in range(1, TAPS):
                tap(2, 0, k)
            dve.wait_ge(sums_done, 1)
            dve.tensor_copy(sums[:, :, :].rearrange("p a n -> p (a n)"), bank[0][:, 0:3 * NT * H]).then_inc(cs_ready, 1)
            for k in range(1, TAPS):
                tap(2, 1, k)
            dve.wait_ge(cs_ready, 1)
            dve.tensor_scalar(ncs_all[:, :], sums[:, 0, :], -1.0, None, ALU.mult).then_inc(ncs_ready, 1)
            dve.wait_ge(consts, 15)
            dve.tensor_scalar(before[:, :], first_slot[:, :], 1.0 / P, None, ALU.mult).then_inc(consts_v, 1)
            dve.wait_ge(wout_in, 16)
            for m in range(2):
                dve.tensor_scalar(wout[:, m, :], wout[:, m, :], col(C_NORMW + m), float(DI) ** 0.5, ALU.mult, ALU.mult).then_inc(consts_v, 1)
            for k in range(2, TAPS):
                tap(2, 2, k)
            for m in range(NB):
                for k in range(TAPS - TAPS_V[m], TAPS):
                    tap(G - 1, m, k)
            for t in range((G - 1) * GT, NT):
                if t == NT - 2:
                    dve.wait_ge(sums_exp, 1)
                    dve.tensor_tensor(w_all[:, :], ex_all[:, 1, :], dt_all[:, :], ALU.mult).then_inc(w_ready, 1)
                dve.wait_ge(cv_turned, t + 1)
                dve.tensor_copy(xs_all[:, t, :], bank[6 + t % 2][:, 0:DI + N]).then_inc(xs_ready, 1)

            y_bank = (bank[0], bank[2])

            def scores(c, k):
                dve.wait_ge(cbst_done, c + 1)
                dve.tensor_tensor(cb[:, k, :], bank[1][:, 0:P], upto[:, :], ALU.mult).then_inc(cb_ready, 1)

            def carry_state(c, q=None):
                if q is not None:
                    dve.wait_ge(st2_ready, 2 * q + 2)
                    if begun(q):
                        dve.wait_ge(nm2_ready, q)
                dve.wait_ge(off_done, c + 1)
                for h in range(H):
                    of_head = state[:, h * HD:(h + 1) * HD]
                    last = dve.scalar_tensor_tensor(out=of_head, in0=of_head, scalar=ex_all[0:N, 2, bass.ds(c * H + h, 1)],
                                                    in1=bank[1][0:N, P + h * HD:P + (h + 1) * HD], op0=ALU.mult, op1=ALU.add)
                last.then_inc(state_ready, 1)

            def mix(c, k):
                dve.wait_ge(decay_ready, c + 1)
                dve.wait_ge(cb_ready, c + 1)
                dve.scalar_tensor_tensor(out=by_head(m_t[:, k, :], P), in0=by_head(decay[:, k, :], P), scalar=1.0,
                                         in1=cb[:, k, :].unsqueeze(1).to_broadcast([P, H, P]), op0=ALU.min, op1=ALU.mult).then_inc(m_ready, 1)

            def summed(c, k):
                dve.wait_ge(diag_done, c + 1)
                dve.tensor_tensor(y_sum[:, :], y_bank[k][:, DI:2 * DI], y_off[:, k, :], ALU.add).then_inc(y_step, 1)
                dve.wait_ge(y_step, 2 * c + 1)
                dve.wait_ge(dxs_ready, c + 1)
                dve.tensor_tensor(y_skip[:, k, :], y_sum[:, :], dxs[:, k, :], ALU.add).then_inc(y_step, 1)

            def gate_y(c, k):
                dve.wait_ge(y_step, 2 * c + 2)
                dve.tensor_tensor(yg[:, k, :], y_skip[:, k, :], tile_of(sz_all, c), ALU.mult).then_inc(yg_ready, 1)

            def residual(c, k):
                dve.wait_ge(rms_ready, c + 1)
                dve.wait_ge(proj_done, c + 1)
                xt = tile_of(x_all, c)
                dve.scalar_tensor_tensor(out=xt, in0=bank[4][:, 0:D], scalar=rms[:, k:k + 1], in1=xt, op0=ALU.mult, op1=ALU.add).then_inc(x1_ready, 1)

            def ln2_stats(q):
                dve.wait_ge(x1_ready, 2 * q + 2)
                for j in range(2):
                    dve.bn_stats(st2[:, j, :], tile_of(x_all, 2 * q + j)).then_inc(st2_ready, 1)

            def ln2_aggregate(q):
                for j in range(2):
                    dve.bn_aggr(mv2[:, j, :], st2[:, j, :]).then_inc(mv2_ready, 1)

            def pairwise(ap):
                return ap.rearrange("p (j e) -> p j e", e=E)

            def choose(q, at=5):
                logits = pairwise(bank[at][:, DI:DI + 2 * E])
                dve.wait_ge(logits_done, q + 1)
                dve.tensor_reduce(lmax[:, :], logits, AX.X, ALU.max).then_inc(route_step, 1)
                dve.wait_ge(route_step, 3 * q + 1)
                for j in range(2):
                    dve.scalar_tensor_tensor(out=pref[:, j * E:(j + 1) * E], in0=bank[at][:, DI + j * E:DI + (j + 1) * E], scalar=lmax[:, j:j + 1],
                                             in1=prefer[:, j * E:(j + 1) * E], op0=ALU.is_equal, op1=ALU.mult).then_inc(route_step, 1)
                dve.wait_ge(route_step, 3 * q + 3)
                dve.tensor_reduce(pmax[:, :], pairwise(pref[:, :]), AX.X, ALU.max).then_inc(pm_ready, 1)
                dve.wait_ge(pm_ready, q + 1)
                dve.tensor_tensor(pairwise(oh[:, :]), pairwise(pref[:, :]), pmax[:, :].unsqueeze(2).to_broadcast([P, 2, E]), ALU.is_equal).then_inc(oh_ready, 1)
                dve.tensor_scalar(limit[:, :], pmax[:, :], -float(CAP), CAP * (E + 1) - 0.5, ALU.mult, ALU.add).then_inc(limit_ready, 1)

            def slots(q, to=sloti, no=noslot):
                dve.wait_ge(rank_done, q + 1)
                dve.scalar_tensor_tensor(out=chosen[:, :], in0=bank[6][:, 2 * P:2 * P + 2 * E], scalar=1.0, in1=oh[:, :],
                                         op0=ALU.subtract, op1=ALU.mult).then_inc(rank_step, 1)
                dve.tensor_tensor(both[:, :], oh[:, 0:E], oh[:, E:2 * E], ALU.add).then_inc(before_step, 1)
                dve.wait_ge(rank_step, 2 * q + 1)
                dve.tensor_reduce(slotf[:, :], pairwise(chosen[:, :]), AX.X, ALU.add).then_inc(rank_step, 1)
                dve.wait_ge(before_step, 2 * q + 1)
                dve.tensor_tensor(pairwise(before[:, :]), pairwise(before[:, :]), both[:, :].unsqueeze(1).to_broadcast([P, 2, E]), ALU.add).then_inc(before_step, 1)
                dve.wait_ge(limit_ready, q + 1)
                dve.wait_ge(rank_step, 2 * q + 2)
                dve.tensor_tensor(no[:, :], slotf[:, :], limit[:, :], ALU.is_gt).then_inc(noslot_ready, 1)
                if to is sloti and begun(q):
                    dve.wait_ge(scattered, 32 * q)
                dve.wait_ge(noslot_ready, q + 1)
                dve.scalar_tensor_tensor(out=to[:, :], in0=no[:, :], scalar=float(FAR), in1=slotf[:, :], op0=ALU.mult, op1=ALU.add).then_inc(slot_ready, 1)

            def finish(q, no=noslot, at=5, to=outrow):
                dve.wait_ge(ov_done, q + 1)
                dve.tensor_tensor(ovb[:, :, :], bank[at][:, 0:2 * D].rearrange("p (j d) -> p j d", j=2),
                                  col(C_OB2, D).unsqueeze(1).to_broadcast([P, 2, D]), ALU.add).then_inc(ov_read, 1)
                if to is outrow and begun(q):
                    dve.wait_ge(stored, 16 * q)
                dve.wait_ge(noslot_ready, q + 1)
                dve.wait_ge(ov_read, q + 1)
                for j in range(2):
                    last = dve.scalar_tensor_tensor(out=to[:, j, :], in0=ovb[:, j, :], scalar=no[:, j:j + 1], in1=tile_of(x_all, 2 * q + j),
                                                    op0=ALU.mult, op1=ALU.add)
                last.then_inc(outrow_ready, 1)

            dve.wait_ge(consts, 16)
            dve.wait_ge(xx_ready, G - 1)
            scores(0, 0)
            carry_state(0)
            mix(0, 0)

            def pair(i):
                last = isinstance(i, int) and i >= PAIRS - 1
                scores(2 * i + 1, 1)
                carry_state(2 * i + 1)
                summed(2 * i, 0)
                mix(2 * i + 1, 1)
                gate_y(2 * i, 0)
                if begun(i):
                    residual(2 * i - 1, 1)
                    ln2_stats(i - 1)
                if begun(i - 1):
                    choose(i - 2)
                if last:
                    dve.wait_ge(st2_ready, 2 * (i - 1) + 2)
                    dve.wait_ge(nm2_ready, i - 1)
                    ln2_aggregate(i - 1)
                else:
                    scores(2 * i + 2, 0)
                    carry_state(2 * i + 2, i - 1 if begun(i) else None)
                    if begun(i):
                        ln2_aggregate(i - 1)
                summed(2 * i + 1, 1)
                if not last:
                    mix(2 * i + 2, 0)
                gate_y(2 * i + 1, 1)
                residual(2 * i, 0)
                if begun(i - 1):
                    slots(i - 2)
                if begun(i - 1):
                    finish(i - 2)

            pair(0)
            dve.wait_ge(xx_ready, G)
            for i in range(1, 3):
                pair(i)
            with dve.Fori(3, PAIRS - 1) as i:
                pair(i)
            pair(PAIRS - 1)
            residual(NT - 1, 1)
            q = PAIRS - 1
            ln2_stats(q)
            dve.wait_ge(st2_ready, 2 * q + 2)
            dve.wait_ge(nm2_ready, q)
            ln2_aggregate(q)
            choose(q - 1)
            slots(q - 1)
            choose(q, 1)
            slots(q, slot_last, noslot_last)
            finish(q - 1)
            dve.wait_ge(outrow_ready, q)
            finish(q, noslot_last, 4, outrow_last)

            def expert_hidden(e):
                dve.wait_ge(eh_done, e * 2 + 2)
                if begun(e - 1):
                    dve.wait_ge(ey_done, e - 1)
                for b in range(2):
                    dve.tensor_scalar(hE[:, e % 2, 2 + b, :], bank[(7, 1)[e % 2]][:, b * CAP:(b + 1) * CAP],
                                      col(C_B1 + e * FB + 2 + b), 0.0, ALU.add, ALU.max).then_inc(eh_dve, 1)

            first, end = SLOT_PARTS[1]
            dve.wait_ge(rows_turned, end)
            dve.tensor_copy(bufT[:, first * P:end * P], bank[1][:, 0:(end - first) * P]).then_inc(bufT_in[1], 1)
            expert_hidden(0)
            for e in range(E):
                if e + 1 < E:
                    expert_hidden(e + 1)
                dve.wait_ge(ey_done, e + 1)
                dve.tensor_scalar(yT[:, e * CAP:(e + 1) * CAP], bank[4 + e % 2][:, 0:CAP], col(C_B2 + e), None, ALU.add).then_inc(ey_ready, 1)


def kernel(**inputs):
    import numpy as np
    import concourse.bacc as bacc
    from concourse.bass_utils import run_bass_kernel_spmd as run

    v = {k: np.asarray(a) for k, a in inputs.items()}

    def at(name):
        return v["L0_" + name]

    def rows(a):
        return np.broadcast_to(a.reshape(1, -1), (P, a.size))

    sheet = np.concatenate([
        at("attn_ln_w")[:, None], at("attn_ln_b")[:, None],
        at("attn_conv_w").reshape(NB, P, TAPS).transpose(1, 0, 2).reshape(P, NB * TAPS),
        at("attn_conv_b").reshape(NB, P).T, at("attn_norm_w").reshape(2, P).T,
        at("ffn_ob1").reshape(FB, P).T, at("ffn_b1").reshape(E * FB, P).T, at("ffn_b2").T,
        rows(at("attn_dt_bias")), rows(at("attn_A_log")), rows(at("attn_D_skip")), rows(at("ffn_router_b")),
        rows(at("ffn_ob2"))], axis=1)
    arrays = {
        "x": at("attn_x").reshape(T, D), "sheet": sheet, "in_w": at("attn_in_proj_w").T,
        "out_w": at("attn_out_proj_w").T.reshape(2, P, D).transpose(1, 0, 2), "router_w": at("ffn_router_w"),
        "ow1": at("ffn_ow1"), "ow2": at("ffn_ow2").reshape(FB, P, D).transpose(1, 0, 2),
        "w1": at("ffn_w1").transpose(1, 0, 2), "w2": at("ffn_w2").reshape(E, FB, P, D).transpose(2, 0, 1, 3),
    }
    arrays = {k: np.ascontiguousarray(a) for k, a in arrays.items()}
    nc = bacc.Bacc("TRN2", target_bir_lowering=False, num_devices=1)
    args = {k: nc.dram_tensor("in_" + k, a.shape, F32, kind="ExternalInput").ap() for k, a in arrays.items()}
    out = nc.dram_tensor("out_rows", [T, D], F32, kind="ExternalOutput").ap()
    build(nc, out=out, **args)
    r = run(nc, [{"in_" + k: a for k, a in arrays.items()}], core_ids=[0])
    return np.asarray(r.results[0]["out_rows"]).reshape(at("attn_x").shape)
```
